# Optimizing a Trainium2 kernel written in Bass

```python
import numpy as np
import jax
import jax.numpy as jnp

def _softmax(x, axis=-1):
    return jax.nn.softmax(x, axis=axis)

def _gelu(x):
    return jax.nn.gelu(x, approximate=True)

def _silu(x):
    return jax.nn.silu(x)

def _sigmoid(x):
    return jax.nn.sigmoid(x)

def _layernorm(x, axis=-1, eps=1e-05):
    m = jnp.mean(x, axis=axis, keepdims=True)
    v = jnp.var(x, axis=axis, keepdims=True)
    return (x - m) / jnp.sqrt(v + eps)

def _scatter_add(tgt, idx, src, axis=0):
    return tgt.at[idx].add(src)

def _segment_sum(src, seg, n):
    return jax.ops.segment_sum(src, seg, n)
kernel_name = 'mk_vit_tower_d1_tok_img2048_r4_153281'

def setup_inputs(seed: int=0):
    np.random.seed(seed)
    _w = jnp.asarray

    def _rec_inputs():
        import jax
        import jax.numpy as jnp
        _rk = jax.random.key(seed)
        x = -0.00178296 + 0.498989 * jax.random.normal(jax.random.fold_in(_rk, 1), (16, 256, 64, 2), jnp.float32)
        return x
    x = _rec_inputs()

    def _L0_tok_setup():
        import jax, jax.numpy as jnp
        import numpy as np
        H, N, CCH, LLEN = (256, 64, 1, 512)
        key = jax.random.key(seed)
        k1, k2 = jax.random.split(key, 2)
        log_dt = jax.random.uniform(k1, (H,), jnp.float32, float(np.log(0.001)), float(np.log(0.1)))
        C = 0.5 * jax.random.normal(k2, (CCH, H, N, 2), jnp.float32)
        log_w_real = jnp.full((H, N), float(np.log(0.5)), jnp.float32)
        w_imag = jnp.broadcast_to(np.pi * jnp.arange(N, dtype=jnp.float32), (H, N)) + jnp.zeros((H, N), jnp.float32)
        return {'C': C, 'log_dt': log_dt, 'log_w_real': log_w_real, 'w_imag': w_imag, 'L': LLEN}
    _L0_tok_all = _L0_tok_setup()
    _L0_tok_in = {k: v for k, v in _L0_tok_all.items() if k in ('log_dt', 'log_w_real', 'w_imag')}
    del _L0_tok_all

    def _L0_attn_setup():
        import jax, jax.numpy as jnp
        import numpy as np
        import math
        B_, L_, D_ = (1, 256, 512)
        ED, N, DCONV, DTR = (1024, 16, 4, 128)

        def _mamba_fwd(x, norm_w, W_in, conv_w, conv_b, W_x, W_dt, b_dt, A, D, W_out):
            u = x * jax.lax.rsqrt(jnp.mean(x * x, axis=-1, keepdims=True)) * norm_w
            xz = u @ W_in.T
            xc, z = jnp.split(xz, 2, axis=-1)
            xt = xc.transpose(0, 2, 1)
            conv = jax.lax.conv_general_dilated(xt, conv_w, (1,), [(DCONV - 1, 0)], feature_group_count=ED)
            conv = conv + conv_b[None, :, None]
            xs = jax.nn.silu(conv.transpose(0, 2, 1))
            dBC = xs @ W_x.T
            dt_lr = dBC[..., :DTR]
            Bm = dBC[..., DTR:DTR + N]
            Cm = dBC[..., DTR + N:]
            dt = jax.nn.softplus(dt_lr @ W_dt.T + b_dt)
            dA = jnp.exp(dt[..., None] * A)
            dBx = dt[..., None] * Bm[:, :, None, :] * xs[..., None]
            h0 = jnp.zeros((x.shape[0], ED, N), x.dtype)

            def step(h, inp):
                dA_t, dBx_t, C_t = inp
                h = dA_t * h + dBx_t
                y_t = jnp.einsum('bdn,bn->bd', h, C_t)
                return (h, y_t)
            _, ys = jax.lax.scan(step, h0, (dA.transpose(1, 0, 2, 3), dBx.transpose(1, 0, 2, 3), Cm.transpose(1, 0, 2)))
            y = ys.transpose(1, 0, 2) + xs * D
            out = y * jax.nn.silu(z) @ W_out.T
            return out + x
        key = jax.random.key(seed)
        ks = jax.random.split(key, 10)
        s = lambda fan_in: 1.0 / math.sqrt(fan_in)
        x = jax.random.normal(ks[0], (B_, L_, D_), jnp.float32)
        norm_w = jnp.ones((D_,), jnp.float32)
        W_in = jax.random.uniform(ks[1], (2 * ED, D_), jnp.float32, -s(D_), s(D_))
        conv_w = jax.random.uniform(ks[2], (ED, 1, DCONV), jnp.float32, -s(DCONV), s(DCONV))
        conv_b = jax.random.uniform(ks[3], (ED,), jnp.float32, -s(DCONV), s(DCONV))
        W_x = jax.random.uniform(ks[4], (DTR + 2 * N, ED), jnp.float32, -s(ED), s(ED))
        W_dt = jax.random.uniform(ks[5], (ED, DTR), jnp.float32, -s(DTR), s(DTR))
        dt = jnp.exp(jax.random.uniform(ks[6], (ED,), jnp.float32) * (math.log(0.1) - math.log(0.001)) + math.log(0.1))
        dt = jnp.clip(dt, 0.0001, None)
        b_dt = dt + jnp.log(-jnp.expm1(-dt))
        A = -jnp.tile(jnp.arange(1, N + 1, dtype=jnp.float32)[None, :], (ED, 1))
        D = jnp.ones((ED,), jnp.float32)
        W_out = jax.random.uniform(ks[7], (D_, ED), jnp.float32, -s(ED), s(ED))
        return {'x': x, 'norm_w': norm_w, 'W_in': W_in, 'conv_w': conv_w, 'conv_b': conv_b, 'W_x': W_x, 'W_dt': W_dt, 'b_dt': b_dt, 'A': A, 'D': D, 'W_out': W_out}
    _L0_attn_all = _L0_attn_setup()
    _L0_attn_in = {k: v for k, v in _L0_attn_all.items() if k in ('norm_w', 'W_in', 'conv_w', 'conv_b', 'W_x', 'W_dt', 'b_dt', 'A', 'D', 'W_out')}
    del _L0_attn_all

    def _L0_ffn_setup():
        import jax, jax.numpy as jnp
        import numpy as np
        MIN_EXPERTS = 2
        NEG_INF = -1000000000.0

        def _l2norm(x, axis):
            return x / jnp.maximum(jnp.linalg.norm(x, axis=axis, keepdims=True), 1e-12)

        def _ste(x):
            return x + jax.lax.stop_gradient((x > 0).astype(x.dtype) - x)

        def _forward(hidden_states, sim_matrix, gates, q_proj, k_proj, v_proj, o_proj):
            B, T, C = hidden_states.shape
            E = gates.shape[0]
            H = q_proj.shape[-1]
            x = hidden_states.reshape(B * T, C)
            logits = _l2norm(x, -1) @ _l2norm(sim_matrix, 0) - jax.nn.sigmoid(gates)
            gated = jax.nn.relu(logits)
            mask = _ste(gated)
            inactive = jnp.sum(mask, axis=1) == 0
            fb_idx = jax.lax.top_k(logits, MIN_EXPERTS)[1]
            fb_mask = jnp.max(jax.nn.one_hot(fb_idx, E, dtype=mask.dtype), axis=1)
            mask = jnp.where(inactive[:, None] & (fb_mask > 0), jnp.ones_like(mask), mask)
            masked_logits = jnp.where(mask > 0, gated, jnp.full_like(gated, NEG_INF))
            probs = jax.nn.softmax(masked_logits, axis=-1)
            w = probs * (mask > 0)

            def mix(proj):
                pe = jnp.einsum('nc,ech->neh', x, proj)
                return jnp.einsum('ne,neh->nh', w, pe).reshape(B, T, H)
            q, k, v = (mix(q_proj), mix(k_proj), mix(v_proj))
            scale = 1.0 / jnp.sqrt(jnp.asarray(H, dtype=q.dtype))
            scores = jnp.einsum('bqh,bkh->bqk', q, k) * scale
            causal = jnp.tril(jnp.ones((T, T), dtype=bool))
            scores = jnp.where(causal[None], scores, jnp.full_like(scores, NEG_INF))
            attn = jax.nn.softmax(scores, axis=-1)
            ao = jnp.einsum('bqk,bkh->bqh', attn, v).reshape(B * T, H)
            wa = jnp.einsum('ne,nh->enh', w, ao)
            out = jnp.einsum('enh,ehc->nc', wa, o_proj)
            return out.reshape(B, T, C)
        key = jax.random.key(seed)
        ks = jax.random.split(key, 6)
        B, T, C, H, E = (4, 512, 512, 128, 16)
        xavier_qkv = float(np.sqrt(2.0 / (C + H)))
        return {'hidden_states': jax.random.normal(ks[0], (B, T, C), dtype=jnp.float32), 'sim_matrix': jax.random.normal(ks[1], (C, E), dtype=jnp.float32), 'gates': jnp.full((E,), -6.0, dtype=jnp.float32), 'q_proj': jax.random.normal(ks[2], (E, C, H), dtype=jnp.float32) * xavier_qkv, 'k_proj': jax.random.normal(ks[3], (E, C, H), dtype=jnp.float32) * xavier_qkv, 'v_proj': jax.random.normal(ks[4], (E, C, H), dtype=jnp.float32) * xavier_qkv, 'o_proj': jax.random.normal(ks[5], (E, H, C), dtype=jnp.float32) * xavier_qkv}
    _L0_ffn_all = _L0_ffn_setup()
    _L0_ffn_in = {k: v for k, v in _L0_ffn_all.items() if k in ('sim_matrix', 'gates', 'q_proj', 'k_proj', 'v_proj', 'o_proj')}
    del _L0_ffn_all
    return {'x': x, 'L0_tok_log_dt': _L0_tok_in['log_dt'], 'L0_tok_log_w_real': _L0_tok_in['log_w_real'], 'L0_tok_w_imag': _L0_tok_in['w_imag'], 'L0_attn_norm_w': _L0_attn_in['norm_w'], 'L0_attn_W_in': _L0_attn_in['W_in'], 'L0_attn_conv_w': _L0_attn_in['conv_w'], 'L0_attn_conv_b': _L0_attn_in['conv_b'], 'L0_attn_W_x': _L0_attn_in['W_x'], 'L0_attn_W_dt': _L0_attn_in['W_dt'], 'L0_attn_b_dt': _L0_attn_in['b_dt'], 'L0_attn_A': _L0_attn_in['A'], 'L0_attn_D': _L0_attn_in['D'], 'L0_attn_W_out': _L0_attn_in['W_out'], 'L0_ffn_sim_matrix': _L0_ffn_in['sim_matrix'], 'L0_ffn_gates': _L0_ffn_in['gates'], 'L0_ffn_q_proj': _L0_ffn_in['q_proj'], 'L0_ffn_k_proj': _L0_ffn_in['k_proj'], 'L0_ffn_v_proj': _L0_ffn_in['v_proj'], 'L0_ffn_o_proj': _L0_ffn_in['o_proj']}

def reference(x, L0_tok_log_dt, L0_tok_log_w_real, L0_tok_w_imag, L0_attn_norm_w, L0_attn_W_in, L0_attn_conv_w, L0_attn_conv_b, L0_attn_W_x, L0_attn_W_dt, L0_attn_b_dt, L0_attn_A, L0_attn_D, L0_attn_W_out, L0_ffn_sim_matrix, L0_ffn_gates, L0_ffn_q_proj, L0_ffn_k_proj, L0_ffn_v_proj, L0_ffn_o_proj):
    import jax
    import jax.numpy as jnp

    def _L0_tok_ref(C, log_dt, log_w_real, w_imag, L):
        import jax, jax.numpy as jnp
        import numpy as np
        H, N, CCH, LLEN = (256, 64, 1, 512)
        dt = jnp.exp(log_dt)
        Cc = C[..., 0] + 1j * C[..., 1]
        w = -jnp.exp(log_w_real) + 1j * w_imag
        dtA = w * dt[:, None]
        K = dtA[:, :, None] * jnp.arange(L)
        Cm = Cc * (jnp.exp(dtA) - 1.0) / w
        K = jnp.einsum('chn,hnl->chl', Cm, jnp.exp(K))
        return 2 * K.real

    def _L0_attn_ref(x, norm_w, W_in, conv_w, conv_b, W_x, W_dt, b_dt, A, D, W_out):
        import jax, jax.numpy as jnp
        import numpy as np
        import math
        B_, L_, D_ = (1, 256, 512)
        ED, N, DCONV, DTR = (1024, 16, 4, 128)

        def _mamba_fwd(x, norm_w, W_in, conv_w, conv_b, W_x, W_dt, b_dt, A, D, W_out):
            u = x * jax.lax.rsqrt(jnp.mean(x * x, axis=-1, keepdims=True)) * norm_w
            xz = u @ W_in.T
            xc, z = jnp.split(xz, 2, axis=-1)
            xt = xc.transpose(0, 2, 1)
            conv = jax.lax.conv_general_dilated(xt, conv_w, (1,), [(DCONV - 1, 0)], feature_group_count=ED)
            conv = conv + conv_b[None, :, None]
            xs = jax.nn.silu(conv.transpose(0, 2, 1))
            dBC = xs @ W_x.T
            dt_lr = dBC[..., :DTR]
            Bm = dBC[..., DTR:DTR + N]
            Cm = dBC[..., DTR + N:]
            dt = jax.nn.softplus(dt_lr @ W_dt.T + b_dt)
            dA = jnp.exp(dt[..., None] * A)
            dBx = dt[..., None] * Bm[:, :, None, :] * xs[..., None]
            h0 = jnp.zeros((x.shape[0], ED, N), x.dtype)

            def step(h, inp):
                dA_t, dBx_t, C_t = inp
                h = dA_t * h + dBx_t
                y_t = jnp.einsum('bdn,bn->bd', h, C_t)
                return (h, y_t)
            _, ys = jax.lax.scan(step, h0, (dA.transpose(1, 0, 2, 3), dBx.transpose(1, 0, 2, 3), Cm.transpose(1, 0, 2)))
            y = ys.transpose(1, 0, 2) + xs * D
            out = y * jax.nn.silu(z) @ W_out.T
            return out + x
        return _mamba_fwd(x, norm_w, W_in, conv_w, conv_b, W_x, W_dt, b_dt, A, D, W_out)

    def _L0_ffn_ref(hidden_states, sim_matrix, gates, q_proj, k_proj, v_proj, o_proj):
        import jax, jax.numpy as jnp
        import numpy as np
        MIN_EXPERTS = 2
        NEG_INF = -1000000000.0

        def _l2norm(x, axis):
            return x / jnp.maximum(jnp.linalg.norm(x, axis=axis, keepdims=True), 1e-12)

        def _ste(x):
            return x + jax.lax.stop_gradient((x > 0).astype(x.dtype) - x)

        def _forward(hidden_states, sim_matrix, gates, q_proj, k_proj, v_proj, o_proj):
            B, T, C = hidden_states.shape
            E = gates.shape[0]
            H = q_proj.shape[-1]
            x = hidden_states.reshape(B * T, C)
            logits = _l2norm(x, -1) @ _l2norm(sim_matrix, 0) - jax.nn.sigmoid(gates)
            gated = jax.nn.relu(logits)
            mask = _ste(gated)
            inactive = jnp.sum(mask, axis=1) == 0
            fb_idx = jax.lax.top_k(logits, MIN_EXPERTS)[1]
            fb_mask = jnp.max(jax.nn.one_hot(fb_idx, E, dtype=mask.dtype), axis=1)
            mask = jnp.where(inactive[:, None] & (fb_mask > 0), jnp.ones_like(mask), mask)
            masked_logits = jnp.where(mask > 0, gated, jnp.full_like(gated, NEG_INF))
            probs = jax.nn.softmax(masked_logits, axis=-1)
            w = probs * (mask > 0)

            def mix(proj):
                pe = jnp.einsum('nc,ech->neh', x, proj)
                return jnp.einsum('ne,neh->nh', w, pe).reshape(B, T, H)
            q, k, v = (mix(q_proj), mix(k_proj), mix(v_proj))
            scale = 1.0 / jnp.sqrt(jnp.asarray(H, dtype=q.dtype))
            scores = jnp.einsum('bqh,bkh->bqk', q, k) * scale
            causal = jnp.tril(jnp.ones((T, T), dtype=bool))
            scores = jnp.where(causal[None], scores, jnp.full_like(scores, NEG_INF))
            attn = jax.nn.softmax(scores, axis=-1)
            ao = jnp.einsum('bqk,bkh->bqh', attn, v).reshape(B * T, H)
            wa = jnp.einsum('ne,nh->enh', w, ao)
            out = jnp.einsum('enh,ehc->nc', wa, o_proj)
            return out.reshape(B, T, C)
        return _forward(hidden_states, sim_matrix, gates, q_proj, k_proj, v_proj, o_proj)
    h = _L0_tok_ref(x, L0_tok_log_dt, L0_tok_log_w_real, L0_tok_w_imag, 512)
    h = h + _L0_attn_ref(_layernorm(h, axis=-1), L0_attn_norm_w, L0_attn_W_in, L0_attn_conv_w, L0_attn_conv_b, L0_attn_W_x, L0_attn_W_dt, L0_attn_b_dt, L0_attn_A, L0_attn_D, L0_attn_W_out)
    h = h + _L0_ffn_ref(_layernorm(h, axis=-1), L0_ffn_sim_matrix, L0_ffn_gates, L0_ffn_q_proj, L0_ffn_k_proj, L0_ffn_v_proj, L0_ffn_o_proj)
    return h

_drawn_inputs = setup_inputs


def setup_inputs(seed=0):
    import zlib

    import numpy as np

    out = dict(_drawn_inputs(seed))
    spreads = {'L0_tok_log_w_real': (-0.6931471824645996, 0.2),
     'L0_attn_norm_w': (1.0, 0.6),
     'L0_attn_D': (1.0, 0.6),
     'L0_ffn_gates': (-6.0, 0.6)}
    factors = {'L0_attn_W_x': 4.979,
     'L0_attn_W_dt': 8.0,
     'L0_attn_b_dt': 6.61,
     'L0_attn_A': 8.0,
     'L0_ffn_sim_matrix': 3.109,
     'L0_ffn_q_proj': 8.0,
     'L0_ffn_k_proj': 8.0,
     'L0_ffn_v_proj': 2.865,
     'L0_ffn_o_proj': 2.81}
    for name, (base, spread) in spreads.items():
        noise = np.random.default_rng([zlib.crc32(name.encode()), seed]).standard_normal(out[name].shape)
        drawn = base * np.exp(spread * noise) if base else spread * noise
        out[name] = jnp.asarray(drawn.astype(out[name].dtype))
    for name, factor in factors.items():
        out[name] = (out[name] * factor).astype(out[name].dtype)
    return out
```

```python
import math
from contextlib import ExitStack

import concourse.bass as bass
from concourse import mybir

P = 128
F32 = mybir.dt.float32
F32R = mybir.dt.float32r
I32 = mybir.dt.int32
ALU = mybir.AluOpType
ACT = mybir.ActivationFunctionType
AX = mybir.AxisListType

MAGIC = 1.5 * 2 ** 23
LOG2E = 1.0 / math.log(2.0)
LN2_HI = 0.693359375
LN2_LO = math.log(2.0) - LN2_HI
TWO_PI = 2 * math.pi
TWO_PI_HI = 6.28125
TWO_PI_LO = TWO_PI - TWO_PI_HI
PI_IN = 3.1415925
EPS = 1e-5
START = 1


def token_stage(nc, io, h0_scratch):
    H, N = io["w_imag"].shape[1] * 2, 64
    Q = H // 2
    CH = io["xT"].shape[1] // (2 * Q)
    LEN = h0_scratch.shape[2]
    L0 = P
    L1 = LEN // L0
    LT = L0 + L1
    QC = 16
    CHUNKS = Q // QC
    QB = 512 // L0
    BANKS = QC // QB

    with ExitStack() as ctx:
        def sb(name, shape, dt=F32):
            return ctx.enter_context(nc.sbuf_tensor(name, shape, dt))

        def sem(name):
            return ctx.enter_context(nc.semaphore(name))

        coef = sb("tk_coef", [P, 2, CH, Q])
        prod = sb("tk_prod", [P, 4, CH, Q])
        logs = sb("tk_logs", [P, 2, Q])
        w_im = sb("tk_w_im", [P, Q])
        exps = sb("tk_exps", [P, 2, Q])
        w_re = sb("tk_w_re", [P, Q])
        a = sb("tk_a", [P, Q])
        b = sb("tk_b", [P, Q])
        em1 = sb("tk_em1", [P, Q])
        t = [sb(f"tk_t{i}", [P, 2, Q]) for i in range(5)]
        ti = sb("tk_ti", [P, 2, Q], I32)
        g = sb("tk_g", [P, 2, Q])
        pos_i = sb("tk_pos_i", [P, LT], I32)
        pos = sb("tk_pos", [P, LT])
        phase = sb("tk_phase", [P, 2, QC, LT])
        turns = sb("tk_turns", [P, QC, LT])
        decay = sb("tk_decay", [P, 2, QC, LT])
        nsin = sb("tk_nsin", [P, 2, QC, LT])
        cosine = sb("tk_cosine", [P, 2, QC, LT])
        e_re = sb("tk_e_re", [P, 2, QC, LT])
        e_nim = sb("tk_e_nim", [P, 2, QC, LT])
        p_t = prod[:].rearrange("p i c q -> p i (c q)")[:, :, 0:QC * CH * L1]\
            .rearrange("p i (q c l) -> p i q c l", q=QC, c=CH)
        p_re = sb("tk_p_re", [P, 2, QC, CH, L1])
        p_im = sb("tk_p_im", [P, 2, QC, CH, L1])
        stage = sb("tk_stage", [P, 2, QC, L0])
        half_angle = sb("tk_half_angle", [P, Q])
        sine = sb("tk_sine", [P, Q])
        absolute = sb("tk_absolute", [P, Q])
        half_pi = sb("tk_half_pi", [P, 1])
        ps = ctx.enter_context(nc.psum_tensor("tk_ps", [P, 8, 512], F32))

        loaded = sem("tk_loaded")
        positions = sem("tk_positions")
        angle_ready = sem("tk_angle_ready")
        trig_ready = sem("tk_trig_ready")
        ab_ready = sem("tk_ab_ready")
        g_ready = sem("tk_g_ready")
        products_ready = sem("tk_products_ready")
        im_ready = sem("tk_im_ready")
        coef_ready = sem("tk_coef_ready")
        phase_ready = sem("tk_phase_ready")
        decay_arg = sem("tk_decay_arg")
        trig_step = sem("tk_trig_step")
        e_ready = sem("tk_e_ready")
        p_im_step = sem("tk_p_im_step")
        p_re_ready = sem("tk_p_re_ready")
        sums_ready = sem("tk_sums_ready")
        staged = sem("tk_staged")
        stored = [sem(f"tk_stored{i}") for i in range(2)]
        dve_step = sem("tk_dve_step")
        pe_idle = sem("tk_pe_idle")

        def bq(x):
            return x.unsqueeze(1).broadcast_to([P, CH, Q])

        block = ctx.enter_context(nc.Block())

        @block.sync
        def _(sp):
            sp.dma_start(logs[0:64, 0, :], io["log_dt"][0:1, :].partition_broadcast(64)).then_inc(loaded, 16)
            sp.dma_start(logs[64:P, 0, :], io["log_dt"][1:2, :].partition_broadcast(64)).then_inc(loaded, 16)
            sp.dma_start(logs[:, 1, :], io["log_w_real"]).then_inc(loaded, 16)
            sp.dma_start(w_im[:], io["w_imag"]).then_inc(loaded, 16)
            sp.dma_start(coef[:].rearrange("p r c q -> p (r c q)"), io["xT"]).then_inc(loaded, 16)
            h0_v = h0_scratch.rearrange("c (q two) (l1 l0) -> two c l1 q l0", two=2, l0=L0)

            def store(k, slot):
                sp.wait_ge(staged, BANKS * (k + 1))
                for h2 in range(2):
                    for c in range(CH):
                        pt = 64 * h2 + L1 * c
                        sp.dma_start(h0_v[h2, c, :, bass.ds(k * QC, QC), :],
                                     stage[pt:pt + L1, slot, :, :]).then_inc(stored[slot], 16)

            with sp.Fori(0, CHUNKS // 2) as pair:
                for slot in range(2):
                    store(pair * 2 + slot, slot)
            for slot in range(2):
                sp.wait_ge(stored[slot], 16 * CH * CHUNKS)

        @block.gpsimd
        def _(pool):
            nc.gpsimd.iota(pos_i[:, 0:L0], pattern=[[1, L0]], base=0, channel_multiplier=0).then_inc(positions, 1)
            nc.gpsimd.iota(pos_i[:, L0:LT], pattern=[[L0, L1]], base=0, channel_multiplier=0).then_inc(positions, 1)
            nc.gpsimd.memset(half_pi[:], math.pi / 2).then_inc(positions, 1)
            pool.wait_ge(positions, 3)
            nc.gpsimd.tensor_copy(pos[:], pos_i[:]).then_inc(positions, 1)

            def decay_argument(k, slot):
                if not isinstance(k, int) or k >= 2:
                    pool.wait_ge(e_ready, 2 * k - 2)
                nc.gpsimd.tensor_tensor(decay[:, slot], a[:, bass.ds(k * QC, QC)].unsqueeze(2).broadcast_to([P, QC, LT]),
                                        pos[:].unsqueeze(1).broadcast_to([P, QC, LT]),
                                        ALU.mult).then_inc(decay_arg, 1)

            def imaginary_p(k, slot):
                qs = bass.ds(k * QC, QC)
                pool.wait_ge(e_ready, 2 * k + 2)
                if not isinstance(k, int) or k >= 2:
                    pool.wait_ge(sums_ready, k - 1)
                c_re = coef[:, 0, :, qs].rearrange("p c q -> p q c").unsqueeze(3).broadcast_to([P, QC, CH, L1])
                c_im = coef[:, 1, :, qs].rearrange("p c q -> p q c").unsqueeze(3).broadcast_to([P, QC, CH, L1])
                er = e_re[:, slot, :, L0:LT].unsqueeze(2).broadcast_to([P, QC, CH, L1])
                ei = e_nim[:, slot, :, L0:LT].unsqueeze(2).broadcast_to([P, QC, CH, L1])
                nc.gpsimd.tensor_tensor(p_t[:, 2], c_im, er, ALU.mult).then_inc(p_im_step, 1)
                nc.gpsimd.tensor_tensor(p_t[:, 3], c_re, ei, ALU.mult).then_inc(p_im_step, 1)
                pool.wait_ge(p_im_step, 3 * k + 2)
                nc.gpsimd.tensor_tensor(p_im[:, slot], p_t[:, 2], p_t[:, 3], ALU.subtract).then_inc(p_im_step, 1)
                pool.wait_ge(p_im_step, 3 * k + 3)

            pool.wait_ge(positions, 4)
            pool.wait_ge(ab_ready, 1)
            decay_argument(0, 0)
            pool.wait_ge(g_ready, 1)
            nc.gpsimd.tensor_tensor(prod[:, 2], coef[:, 0], bq(g[:, 1]), ALU.mult).then_inc(im_ready, 1)
            nc.gpsimd.tensor_tensor(prod[:, 3], coef[:, 1], bq(g[:, 0]), ALU.mult).then_inc(im_ready, 1)
            pool.wait_ge(im_ready, 2)
            pool.wait_ge(products_ready, 1)
            nc.gpsimd.tensor_tensor(coef[:, 1], prod[:, 2], prod[:, 3], ALU.add).then_inc(im_ready, 1)
            pool.wait_ge(im_ready, 3)
            decay_argument(1, 1)
            pool.wait_ge(coef_ready, 1)
            imaginary_p(0, 0)
            with pool.Fori(1, CHUNKS // 2) as pair:
                decay_argument(pair * 2, 0)
                imaginary_p(pair * 2 - 1, 1)
                decay_argument(pair * 2 + 1, 1)
                imaginary_p(pair * 2, 0)
            imaginary_p(CHUNKS - 1, 1)

        @block.scalar
        def _(act):
            act.wait_ge(positions, 3)
            act.wait_ge(angle_ready, 1)
            nc.scalar.activation(sine[:], half_angle[:], ACT.Sin).then_inc(trig_ready, 1)
            nc.scalar.activation(absolute[:], half_angle[:], ACT.Abs).then_inc(trig_ready, 1)
            act.wait_ge(trig_ready, 2)
            nc.scalar.activation(t[3][:, 0], absolute[:], ACT.Sin, bias=half_pi[:], scale=-1.0).then_inc(trig_ready, 1)

            def trigs(k, slot):
                act.wait_ge(phase_ready, k + 1)
                if not isinstance(k, int) or k >= 2:
                    act.wait_ge(e_ready, 2 * k - 2)
                nc.scalar.activation(nsin[:, slot], phase[:, slot], ACT.Sin, scale=-1.0).then_inc(trig_step, 1)
                nc.scalar.activation(cosine[:, slot], phase[:, slot], ACT.Abs).then_inc(trig_step, 1)
                act.wait_ge(trig_step, 4 * k + 2)
                nc.scalar.activation(cosine[:, slot], cosine[:, slot], ACT.Sin, bias=half_pi[:], scale=-1.0)\
                    .then_inc(trig_step, 1)
                act.wait_ge(decay_arg, k + 1)
                nc.scalar.activation(decay[:, slot], decay[:, slot], ACT.Exp).then_inc(trig_step, 1)

            def copy_out(k, slot):
                act.wait_ge(sums_ready, k + 1)
                if not isinstance(k, int) or k >= 2:
                    act.wait_ge(stored[slot], 16 * CH * (k - slot))
                for qb in range(BANKS):
                    nc.scalar.activation(stage[:, slot, QB * qb:QB * qb + QB, :],
                                         ps[:, BANKS * slot + qb, :].rearrange("p (q l) -> p q l", q=QB),
                                         ACT.Copy).then_inc(staged, 1)

            trigs(0, 0)
            trigs(1, 1)
            copy_out(0, 0)
            with act.Fori(1, CHUNKS // 2) as pair:
                trigs(pair * 2, 0)
                copy_out(pair * 2 - 1, 1)
                trigs(pair * 2 + 1, 1)
                copy_out(pair * 2, 0)
            copy_out(CHUNKS - 1, 1)

        @block.vector
        def _(dve):
            count = [0]

            def link(ins):
                count[0] += 1
                ins.then_inc(dve_step, 1)
                dve.wait_ge(dve_step, count[0])

            V = nc.vector

            def exp_parts(x, k, r, q, two_k):
                link(V.tensor_scalar(k, x, LOG2E, MAGIC, ALU.mult, ALU.add))
                link(V.tensor_scalar(k, k, MAGIC, None, ALU.subtract))
                link(V.tensor_scalar(k, k, -126.0, 127.0, ALU.max, ALU.min))
                link(V.scalar_tensor_tensor(r, k, -LN2_HI, x, ALU.mult, ALU.add))
                link(V.scalar_tensor_tensor(r, k, -LN2_LO, r, ALU.mult, ALU.add))
                link(V.tensor_scalar(q, r, 1.0 / math.factorial(8), None, ALU.mult))
                for n in range(7, 0, -1):
                    link(V.scalar_tensor_tensor(q, q, 1.0 / math.factorial(n), r, ALU.add, ALU.mult))
                link(V.tensor_scalar(two_k, k, 127.0, float(1 << 23), ALU.add, ALU.mult))

            def phases(k, slot, link):
                ph = phase[:, slot]
                link(V.tensor_tensor(ph, b[:, bass.ds(k * QC, QC)].unsqueeze(2).broadcast_to([P, QC, LT]),
                                     pos[:].unsqueeze(1).broadcast_to([P, QC, LT]), ALU.mult))
                link(V.tensor_scalar(turns[:], ph, 1 / TWO_PI, MAGIC, ALU.mult, ALU.add))
                link(V.tensor_scalar(turns[:], turns[:], MAGIC, None, ALU.subtract))
                link(V.scalar_tensor_tensor(ph, turns[:], -TWO_PI_HI, ph, ALU.mult, ALU.add))
                link(V.scalar_tensor_tensor(ph, turns[:], -TWO_PI_LO, ph, ALU.mult, ALU.add))
                link(V.tensor_scalar(ph, ph, -PI_IN, PI_IN, ALU.max, ALU.min))
                dve.sem_inc(phase_ready, 1)

            dve.wait_ge(loaded, 16 * 5)
            exp_parts(logs[:], t[0][:], t[1][:], t[2][:], ti[:])
            two_k = ti[:].bitcast(F32)
            link(V.tensor_tensor(t[2][:], t[2][:], two_k, ALU.mult))
            link(V.tensor_tensor(exps[:], t[2][:], two_k, ALU.add))
            link(V.scalar_tensor_tensor(a[:], exps[:, 1], -1.0, exps[:, 0], ALU.mult, ALU.mult))
            link(V.tensor_scalar(w_re[:], exps[:, 1], -1.0, None, ALU.mult))
            link(V.tensor_tensor(b[:], w_im[:], exps[:, 0], ALU.mult))
            dve.sem_inc(ab_ready, 1)
            link(V.tensor_scalar(half_angle[:], b[:], 0.5, None, ALU.mult))
            link(V.tensor_scalar(t[4][:, 0], half_angle[:], 1 / TWO_PI, MAGIC, ALU.mult, ALU.add))
            link(V.tensor_scalar(t[4][:, 0], t[4][:, 0], MAGIC, None, ALU.subtract))
            link(V.scalar_tensor_tensor(half_angle[:], t[4][:, 0], -TWO_PI_HI, half_angle[:], ALU.mult, ALU.add))
            link(V.scalar_tensor_tensor(half_angle[:], t[4][:, 0], -TWO_PI_LO, half_angle[:], ALU.mult, ALU.add))
            link(V.tensor_scalar(half_angle[:], half_angle[:], -PI_IN, PI_IN, ALU.max, ALU.min))
            dve.sem_inc(angle_ready, 1)
            dve.wait_ge(positions, 4)
            phases(0, 0, link)
            exp_parts(a[:], t[0][:, 0], t[1][:, 0], t[2][:, 0], ti[:, 0])
            two_k = ti[:, 0].bitcast(F32)
            link(V.tensor_tensor(t[2][:, 0], t[2][:, 0], two_k, ALU.mult))
            link(V.scalar_tensor_tensor(em1[:], two_k, -1.0, t[2][:, 0], ALU.add, ALU.add))
            link(V.tensor_tensor(t[4][:, 0], w_re[:], w_re[:], ALU.mult))
            link(V.tensor_tensor(t[4][:, 1], w_im[:], w_im[:], ALU.mult))
            link(V.tensor_tensor(t[4][:, 0], t[4][:, 0], t[4][:, 1], ALU.add))
            link(V.reciprocal(t[4][:, 1], t[4][:, 0]))
            link(V.tensor_scalar(t[4][:, 1], t[4][:, 1], 2.0, None, ALU.mult))
            inv = t[4][:, 1]
            dve.wait_ge(trig_ready, 3)
            s, c = sine[:], t[3][:, 0]
            u, er, ei = t[4][:, 0], t[0][:, 1], t[1][:, 1]
            link(V.scalar_tensor_tensor(u, s, -2.0, s, ALU.mult, ALU.mult))
            link(V.scalar_tensor_tensor(er, em1[:], 1.0, u, ALU.add, ALU.mult))
            link(V.tensor_tensor(er, er, em1[:], ALU.add))
            link(V.scalar_tensor_tensor(u, s, 2.0, c, ALU.mult, ALU.mult))
            link(V.scalar_tensor_tensor(ei, em1[:], 1.0, u, ALU.add, ALU.mult))
            x1, x2 = t[2][:, 0], t[2][:, 1]
            link(V.tensor_tensor(x1, er, w_re[:], ALU.mult))
            link(V.tensor_tensor(x2, ei, w_im[:], ALU.mult))
            link(V.tensor_tensor(x1, x1, x2, ALU.add))
            link(V.tensor_tensor(g[:, 0], x1, inv, ALU.mult))
            link(V.tensor_tensor(x1, ei, w_re[:], ALU.mult))
            link(V.tensor_tensor(x2, er, w_im[:], ALU.mult))
            link(V.tensor_tensor(x1, x1, x2, ALU.subtract))
            link(V.tensor_tensor(g[:, 1], x1, inv, ALU.mult))
            dve.sem_inc(g_ready, 1)
            link(V.tensor_tensor(prod[:, 0], coef[:, 0], bq(g[:, 0]), ALU.mult))
            link(V.tensor_tensor(prod[:, 1], coef[:, 1], bq(g[:, 1]), ALU.mult))
            dve.wait_ge(im_ready, 2)
            V.tensor_tensor(coef[:, 0], prod[:, 0], prod[:, 1], ALU.subtract).then_inc(coef_ready, 1)
            dve.sem_inc(products_ready, 1)
            dve.wait_ge(coef_ready, 1)
            dve.wait_ge(im_ready, 3)
            PHASE_STEPS, STEPS = 6, 9
            setup = count[0] - PHASE_STEPS

            def chunk_link(k, local):
                def link(ins):
                    local[0] += 1
                    ins.then_inc(dve_step, 1)
                    dve.wait_ge(dve_step, k * STEPS + (setup + PHASE_STEPS + local[0]))
                return link

            def middle(k, slot, link):
                dve.wait_ge(trig_step, 4 * k + 4)
                if not isinstance(k, int) or k >= 2:
                    dve.wait_ge(sums_ready, k - 1)
                V.tensor_tensor(e_re[:, slot], cosine[:, slot], decay[:, slot], ALU.mult).then_inc(e_ready, 1)
                V.tensor_tensor(e_nim[:, slot], nsin[:, slot], decay[:, slot], ALU.mult).then_inc(e_ready, 1)
                dve.wait_ge(e_ready, 2 * k + 2)
                qs = bass.ds(k * QC, QC)
                c_re = coef[:, 0, :, qs].rearrange("p c q -> p q c").unsqueeze(3).broadcast_to([P, QC, CH, L1])
                c_im = coef[:, 1, :, qs].rearrange("p c q -> p q c").unsqueeze(3).broadcast_to([P, QC, CH, L1])
                er = e_re[:, slot, :, L0:LT].unsqueeze(2).broadcast_to([P, QC, CH, L1])
                ei = e_nim[:, slot, :, L0:LT].unsqueeze(2).broadcast_to([P, QC, CH, L1])
                link(V.tensor_tensor(p_t[:, 0], c_re, er, ALU.mult))
                link(V.tensor_tensor(p_t[:, 1], c_im, ei, ALU.mult))
                link(V.tensor_tensor(p_re[:, slot], p_t[:, 0], p_t[:, 1], ALU.add))
                dve.sem_inc(p_re_ready, 1)

            def step(k, slot):
                link = chunk_link(k, [0])
                dve.wait_ge(trig_step, 4 * k)
                phases(k + 1, 1 - slot, link)
                middle(k, slot, link)

            link0 = chunk_link(0, [0])
            phases(1, 1, link0)
            middle(0, 0, link0)
            with dve.Fori(1, CHUNKS // 2) as pair:
                step(pair * 2 - 1, 1)
                step(pair * 2, 0)
            middle(CHUNKS - 1, 1, chunk_link(CHUNKS - 1, [0]))

        @block.tensor
        def _(pe):
            def sums(k, slot):
                pe.wait_ge(p_re_ready, k + 1)
                pe.wait_ge(p_im_step, 3 * k + 3)
                if not isinstance(k, int) or k >= 2:
                    pe.wait_ge(staged, BANKS * (k - 1))
                    pe.sem_inc(pe_idle, 1)
                for q in range(QC):
                    for part, (lhs, rhs) in enumerate(((p_re, e_re), (p_im, e_nim))):
                        for h2 in range(2):
                            rows = slice(64 * h2, 64 * h2 + 64)
                            last = nc.tensor.matmul(
                                ps[rows, BANKS * slot + q // QB, q % QB * L0:(q % QB + 1) * L0],
                                lhs[rows, slot, q].rearrange("p c l -> p (c l)"), rhs[rows, slot, q, 0:L0],
                                start=(part == 0), stop=(part == 1))
                last.then_inc(sums_ready, 1)

            for slot in range(2):
                sums(slot, slot)
            with pe.Fori(1, CHUNKS // 2) as pair:
                for slot in range(2):
                    sums(pair * 2 + slot, slot)


def mamba_stage(nc, io, h0_scratch, b_scratch, h1_scratch):
    BATCH, T, D = h0_scratch.shape
    KC = D // P
    TJ = T // P
    ED = io["w_in"].shape[1] // KC // 2
    DI = ED // P
    NS = io["a"].shape[1] // DI
    R = P
    WX = R + 2 * NS
    TAPS = io["conv_w"].shape[1] // DI
    HALF = DI // 2
    STEPS = 2 * NS
    SW = HALF * T
    BG = 4
    FILLS = 16
    B0 = P - 2 * NS

    with ExitStack() as ctx:
        def sb(name, shape, dt=F32):
            return ctx.enter_context(nc.sbuf_tensor(name, shape, dt))

        def sem(name):
            return ctx.enter_context(nc.semaphore(name))

        w_in = sb("ma_w_in", [P, KC, 2 * ED])
        w_x = sb("ma_w_x", [P, DI, WX])
        w_dt = sb("ma_w_dt", [P, ED])
        w_out = sb("ma_w_out", [P, DI, D])
        norm_w = sb("ma_norm_w", [P, KC])
        conv_w = sb("ma_conv_w", [P, DI, TAPS])
        conv_b = sb("ma_conv_b", [P, DI])
        b_dt = sb("ma_b_dt", [P, DI])
        a_w = sb("ma_a", [P, DI, NS])
        d_w = sb("ma_d", [P, DI])
        ident = sb("ma_ident", [P, P])
        minus_half = sb("ma_minus_half", [P, TJ])
        minus_one = sb("ma_minus_one", [P, TJ])
        one = sb("ma_one", [P, TJ])
        eps = sb("ma_eps", [P, TJ])

        hin = sb("ma_hin", [P, TJ, D])
        stats = sb("ma_stats", [P, TJ, 6])
        mv = sb("ma_mv", [P, TJ, 2])
        ln = sb("ma_ln", [P, 8, TJ])
        u = sb("ma_u", [P, TJ, D])
        res = sb("ma_res", [P, 2, TJ, D])
        u_t = sb("ma_u_t", [P, KC, T])
        xc = sb("ma_xc", [P, DI, TAPS - 1 + T])
        gate = sb("ma_gate", [P, 2, DI, T])
        t1 = sb("ma_t1", [P, DI, T])
        t2 = sb("ma_t2", [P, DI, T])
        xs = sb("ma_xs", [P, 2, DI, T])
        dt_lr = sb("ma_dt_lr", [P, T])
        bc_t = sb("ma_bc_t", [P, T])
        c_tok = sb("ma_c_tok", [P, 2, TJ, NS])
        dt = sb("ma_dt", [P, DI, T])
        dtx = sb("ma_dtx", [P, DI, T])
        b_all = sb("ma_b_all", [P, 2, BG, T])
        da = sb("ma_da", [P, 2, HALF, T])
        dbx = sb("ma_dbx", [P, 2, HALF, T])
        hs = sb("ma_hs", [P, 2, HALF, T])
        y = sb("ma_y", [P, TJ, ED])
        yg = sb("ma_yg", [P, DI, T])
        ps_h = ctx.enter_context(nc.psum_tensor("ma_ps_h", [P, 2, TJ, 512], F32))
        ps_p = ctx.enter_context(nc.psum_tensor("ma_ps_p", [P, 4, 512], F32))

        small = sem("ma_small")
        w_in_loaded = sem("ma_w_in_loaded")
        weights = sem("ma_weights")
        consts = sem("ma_consts")
        hin_loaded = sem("ma_hin_loaded")
        stats_step = sem("ma_stats_step")
        ln_step = sem("ma_ln_step")
        u_ready = sem("ma_u_ready")
        res_ready = sem("ma_res_ready")
        filled = sem("ma_filled")
        emptied = sem("ma_emptied")
        conv_step = sem("ma_conv_step")
        first_step = sem("ma_first_step")
        c_turned = sem("ma_c_turned")
        act_idle = sem("ma_act_idle")
        dve_idle = sem("ma_dve_idle")
        sp_idle = sem("ma_sp_idle")
        xs_ready = sem("ma_xs_ready")
        dtlr_ready = sem("ma_dtlr_ready")
        c_ready = sem("ma_c_ready")
        b_stored = sem("ma_b_stored")
        b_loaded = [sem(f"ma_b_loaded{i}") for i in range(2)]
        soft_arg = sem("ma_soft_arg")
        soft_log = sem("ma_soft_log")
        soft_corr = sem("ma_soft_corr")
        soft_step = sem("ma_soft_step")
        dt_ready = sem("ma_dt_ready")
        da_ready = sem("ma_da_ready")
        dbx_ready = sem("ma_dbx_ready")
        scanned = sem("ma_scanned")
        turned = sem("ma_turned")
        summed = sem("ma_summed")
        y_turned = sem("ma_y_turned")
        gated = sem("ma_gated")
        out_ready = sem("ma_out_ready")
        h1_ready = sem("ma_h1_ready")
        h1_stored = sem("ma_h1_stored")

        LOADS = 3
        SMALL = 6
        LN_OPS = 9
        CONV_OPS = 2 * TAPS - 1
        PRIME = 2

        block = ctx.enter_context(nc.Block())

        @block.sync
        def _(sp):
            def load(dst, name, signal):
                flat = dst[:] if len(dst.shape) == 2 else dst[:].rearrange("p a b -> p (a b)")
                sp.dma_start(flat, io[name]).then_inc(signal, 16)

            def load_hin(m):
                row = bass.ds(sp.snap(m % BATCH), 1) if not isinstance(m, int) else bass.ds(0, 1)
                sp.wait_ge(res_ready, TJ * m)
                sp.sem_inc(sp_idle, 1)
                sp.dma_start(hin[:], h0_scratch[row].rearrange("o (j p) d -> (o p) j d", p=P))\
                    .then_inc(hin_loaded, 16)

            def store_b(m):
                sp.wait_ge(emptied, FILLS * m + 12)
                sp.dma_start(b_scratch, bc_t[B0:B0 + NS, :]).then_inc(b_stored, 16)
                sp.wait_ge(b_stored, 16 * (m + 1))
                sp.sem_inc(sp_idle, 1)

            def load_b(m, g):
                if g:
                    sp.wait_ge(scanned, STEPS * m + 2 * BG * (g - 1) + PRIME)
                sp.dma_start(b_all[:, g % 2].rearrange("p n t -> p (n t)"),
                             b_scratch[g * BG:(g + 1) * BG, :].rearrange("n t -> (n t)").unsqueeze(0)
                             .partition_broadcast(P)).then_inc(b_loaded[g % 2], 16)

            load_hin(0)
            for dst, name in ((norm_w, "norm_w"), (conv_w, "conv_w"), (conv_b, "conv_b"), (b_dt, "b_dt"), (a_w, "a"),
                              (d_w, "d")):
                load(dst, name, small)
            load(w_in, "w_in", w_in_loaded)
            load(w_x, "w_x", weights)
            load(w_dt, "w_dt", weights)
            load(w_out, "w_out", weights)
            store_b(0)
            load_b(0, 0)
            load_b(0, 1)
            with sp.Fori(0, BATCH) as b:
                load_hin(b + 1)
                sp.wait_ge(h1_ready, TJ * (b + 1))
                sp.dma_start(h1_scratch[bass.ds(b, 1)].rearrange("o (j p) d -> (o p) j d", p=P),
                             res[:, bass.ds((b + 1) % 2, 1)].rearrange("p o j d -> p (o j) d")).then_inc(h1_stored, 16)
                load_b(b, 2)
                load_b(b, 3)
                sp.wait_ge(b_loaded[0], 16 * (2 * b + 2))
                sp.wait_ge(b_loaded[1], 16 * (2 * b + 2))
                store_b(b + 1)
                sp.wait_ge(scanned, STEPS * b + 2 * BG * 3 + PRIME)
                load_b(b + 1, 0)
                load_b(b + 1, 1)
            sp.wait_ge(h1_ready, TJ * (BATCH + 1))
            sp.dma_start(h1_scratch[BATCH].rearrange("(j p) d -> p j d", p=P),
                         res[:, (BATCH + 1) % 2]).then_inc(h1_stored, 16)
            sp.wait_ge(h1_stored, 16 * (BATCH + 1))
            sp.wait_ge(b_stored, 16 * (BATCH + 1))
            sp.wait_ge(b_loaded[0], 16 * (2 * BATCH + 1))
            sp.wait_ge(b_loaded[1], 16 * (2 * BATCH + 1))

        @block.gpsimd
        def _(pool):
            G = nc.gpsimd
            G.memset(ident[:], 0.0).then_inc(consts, 1)
            G.memset(minus_half[:], -0.5).then_inc(consts, 1)
            G.memset(xc[:, :, 0:TAPS - 1], 0.0).then_inc(consts, 1)
            G.memset(da[:, :, :, 0:1], 0.0).then_inc(consts, 1)
            G.memset(yg[:], 0.0).then_inc(consts, 1)
            G.memset(res[:, 1], 0.0).then_inc(consts, 1)
            G.memset(minus_one[:], -1.0).then_inc(consts, 1)
            G.memset(one[:], 1.0).then_inc(consts, 1)
            G.memset(eps[:], EPS).then_inc(consts, 1)
            pool.wait_ge(consts, 9)
            G.affine_select(out=ident[:], in_=ident[:], compare_op=ALU.not_equal, fill=1.0, base=0,
                            pattern=[[-1, P]], channel_multiplier=1).then_inc(consts, 1)
            pool.wait_ge(consts, 10)
            pool.wait_ge(small, 16 * SMALL)

            def norm_scalars(m):
                n = [0]

                def link(ins):
                    n[0] += 1
                    ins.then_inc(ln_step, 1)
                    pool.wait_ge(ln_step, m * (LN_OPS + 1) + n[0])

                pool.wait_ge(stats_step, 2 * TJ * (m + 1))
                pool.wait_ge(res_ready, TJ * m)
                mean, var = mv[:, :, 0], mv[:, :, 1]
                link(G.tensor_tensor(ln[:, 0], var, eps[:], ALU.add))
                link(G.tensor_tensor(ln[:, 1], ln[:, 0], minus_half[:], ALU.pow))
                link(G.tensor_tensor(ln[:, 2], var, ln[:, 1], ALU.mult))
                link(G.tensor_tensor(ln[:, 3], ln[:, 2], ln[:, 1], ALU.mult))
                link(G.tensor_tensor(ln[:, 4], ln[:, 3], minus_half[:], ALU.pow))
                link(G.tensor_tensor(ln[:, 5], ln[:, 1], ln[:, 4], ALU.mult))
                link(G.tensor_tensor(ln[:, 6], mean, ln[:, 1], ALU.mult))
                link(G.tensor_tensor(ln[:, 6], ln[:, 6], minus_one[:], ALU.mult))
                link(G.tensor_tensor(ln[:, 0], ln[:, 1], one[:], ALU.add))
                G.tensor_tensor(ln[:, 7], ln[:, 6], ln[:, 4], ALU.mult).then_inc(ln_step, 1)
                assert n[0] == LN_OPS

            def convolve(m):
                pool.wait_ge(emptied, FILLS * m + 6)
                pool.wait_ge(soft_step, 4 * m)
                for k in range(TAPS):
                    w = conv_w[:, :, k:k + 1].broadcast_to([P, DI, T])
                    G.tensor_tensor((t2 if k else t1)[:], xc[:, :, k:k + T], w, ALU.mult).then_inc(conv_step, 1)
                    if k:
                        pool.wait_ge(conv_step, CONV_OPS * m + 2 * k)
                        G.tensor_tensor(t1[:], t1[:], t2[:], ALU.add).then_inc(conv_step, 1)
                        pool.wait_ge(conv_step, CONV_OPS * m + 2 * k + 1)

            def soft_correction(m):
                pool.wait_ge(soft_step, 4 * m + 1)
                G.tensor_tensor(t1[:], t1[:], dtx[:], ALU.subtract).then_inc(soft_corr, 1)

            def prepare(m):
                norm_scalars(m)
                convolve(m)
                soft_correction(m)

            norm_scalars(0)
            soft_correction(0)
            with pool.Fori(0, BATCH) as b:
                prepare(b + 1)

        @block.scalar
        def _(act):
            A = nc.scalar
            act.wait_ge(small, 16 * SMALL)
            act.wait_ge(consts, 10)

            def settle():
                act.sem_inc(act_idle, 1)

            def prep_norm(m):
                act.wait_ge(ln_step, (LN_OPS + 1) * (m + 1))
                act.wait_ge(filled, FILLS * m)
                for j in range(TJ):
                    A.activation(u[:, j], hin[:, j], ACT.Identity, scale=ln[:, 5, j:j + 1],
                                 bias=ln[:, 7, j:j + 1]).then_inc(u_ready, 1)

            def prep_u_t(m):
                for f in range(2):
                    act.wait_ge(filled, FILLS * m + f + 1)
                    for i in range(2):
                        kc = 2 * f + i
                        last = A.activation(u_t[:, kc], ps_p[:, f, i * T:(i + 1) * T], ACT.Copy, scale=norm_w[:, kc:kc + 1])
                    last.then_inc(emptied, 1)

            def prep_x(m, i):
                act.wait_ge(filled, FILLS * m + 3 + i)
                if i == 0:
                    act.wait_ge(soft_step, 4 * m)
                A.activation(xc[:, 2 * i:2 * i + 2, TAPS - 1:], ps_p[:, i % 2].rearrange("p (i t) -> p i t", i=2),
                             ACT.Copy).then_inc(emptied, 1)

            def prep_z(m, i):
                act.wait_ge(filled, FILLS * m + 7 + i)
                settle()
                A.activation(gate[:, bass.ds(m % 2, 1), 2 * i:2 * i + 2, :].rearrange("p o i t -> p (o i t)"),
                             ps_p[:, i % 2], ACT.Copy).then_inc(emptied, 1)

            def prep_res(m):
                act.wait_ge(h1_stored, 16 * m)
                act.wait_ge(u_ready, TJ * (m + 1))
                settle()
                for j in range(TJ):
                    A.activation(res[:, bass.ds(m % 2, 1), j, :].rearrange("p o d -> p (o d)"), hin[:, j], ACT.Identity,
                                 scale=ln[:, 0, j:j + 1], bias=ln[:, 6, j:j + 1]).then_inc(res_ready, 1)

            def prep_silu(m):
                act.wait_ge(emptied, FILLS * m + 10)
                act.wait_ge(conv_step, CONV_OPS * (m + 1))
                settle()
                g = gate[:, bass.ds(m % 2, 1)].rearrange("p o i t -> p (o i t)")
                A.activation(g, g, ACT.Silu).then_inc(xs_ready, 1)
                for i in range(DI):
                    A.activation(xs[:, bass.ds(m % 2, 1), i, :].rearrange("p o t -> p (o t)"), t1[:, i], ACT.Silu,
                                 bias=conv_b[:, i:i + 1]).then_inc(xs_ready, 1)

            def prep_bc(m):
                act.wait_ge(filled, FILLS * m + 11)
                A.activation(dt_lr[:], ps_p[:, 0, 0:T], ACT.Copy).then_inc(emptied, 1)
                act.wait_ge(filled, FILLS * m + 12)
                act.wait_ge(b_stored, 16 * m)
                A.activation(bc_t[:], ps_p[:, 1, 0:T], ACT.Copy).then_inc(emptied, 1)

            def prep_c(m):
                act.wait_ge(c_turned, m + 1)
                settle()
                A.activation(c_tok[:, bass.ds(m % 2, 1)].rearrange("p o j n -> p (o j) n"),
                             ps_p[:, 0, 0:TJ * P].rearrange("p (j r) -> p j r", j=TJ)[:, :, B0 + NS:],
                             ACT.Copy).then_inc(c_ready, 1)

            def prep_soft_arg(m, i):
                act.wait_ge(filled, FILLS * m + 13 + i)
                for k in range(2):
                    src = ps_p[:, i % 2, k * T:(k + 1) * T]
                    c = 2 * i + k
                    A.activation(t1[:, c], src, ACT.Abs, bias=b_dt[:, c:c + 1]).then_inc(soft_arg, 1)
                    ins = A.activation(t2[:, c], src, ACT.Relu, bias=b_dt[:, c:c + 1])
                    ins.then_inc(emptied if k else soft_arg, 1)

            def prep_soft_log(m):
                act.wait_ge(soft_arg, 12 * (m + 1))
                A.activation(t1[:], t1[:], ACT.Exp, scale=-1.0).then_inc(soft_log, 1)
                act.wait_ge(soft_log, 2 * m + 1)
                A.activation(xc[:, :, TAPS - 1:], t1[:], ACT.Ln, bias=1.0).then_inc(soft_log, 1)

            def exps(b, s):
                n, half = s // 2, s % 2
                act.wait_ge(scanned, STEPS * b + s + PRIME - 1)
                if s == 0:
                    act.wait_ge(dt_ready, 2 * b + 1)
                for i in range(HALF):
                    c = half * HALF + i
                    A.activation(da[:, s % 2, i, 1:T], dt[:, c, 1:T], ACT.Exp, scale=a_w[:, c, n:n + 1]).then_inc(da_ready, 1)

            pieces = {0: [prep_norm], 1: [prep_u_t], 4: [prep_res], 10: [prep_silu], 12: [prep_bc], 13: [prep_c],
                      15: [prep_soft_log]}
            for i in range(4):
                pieces.setdefault(2 + i, []).append(lambda m, i=i: prep_x(m, i))
                pieces.setdefault(6 + i, []).append(lambda m, i=i: prep_z(m, i))
                pieces.setdefault(13 + i // 2, []).append(lambda m, i=i: prep_soft_arg(m, i))
            for n in range(NS):
                for piece in pieces.get(n, []):
                    piece(0)
            with act.Fori(0, BATCH) as b:
                for n in range(NS):
                    exps(b, 2 * n)
                    exps(b, 2 * n + 1)
                    for piece in pieces.get(n, []):
                        piece(b + 1)

        @block.vector
        def _(dve):
            V = nc.vector
            for signal in (gated,):
                dve.sem_inc(signal, START)
            dve.sem_inc(scanned, PRIME)
            dve.wait_ge(small, 16 * SMALL)
            dve.wait_ge(consts, 10)

            def prep_stats(m):
                dve.wait_ge(hin_loaded, 16 * (m + 1))
                dve.wait_ge(ln_step, (LN_OPS + 1) * m)
                for j in range(TJ):
                    V.bn_stats(stats[:, j], hin[:, j]).then_inc(stats_step, 1)
                dve.wait_ge(stats_step, 2 * TJ * m + TJ)
                dve.sem_inc(dve_idle, 1)
                for j in range(TJ):
                    V.bn_aggr(mv[:, j], stats[:, j]).then_inc(stats_step, 1)

            def softplus(m):
                dve.wait_ge(soft_log, 2 * (m + 1))
                dve.wait_ge(scanned, STEPS * m + PRIME)
                V.tensor_scalar(dtx[:], t1[:], 1.0, 1.0, ALU.add, ALU.subtract).then_inc(soft_step, 1)
                V.tensor_tensor(t2[:], t2[:], xc[:, :, TAPS - 1:], ALU.add).then_inc(soft_step, 1)
                dve.wait_ge(soft_corr, m + 1)
                dve.wait_ge(soft_step, 4 * m + 2)
                V.tensor_tensor(dt[:], t2[:], t1[:], ALU.add).then_inc(dt_ready, 1)
                dve.wait_ge(xs_ready, (DI + 1) * (m + 1))
                dve.wait_ge(dt_ready, 2 * m + 1)
                dve.sem_inc(soft_step, 2)
                V.tensor_tensor(dtx[:], dt[:], xs[:, bass.ds(m % 2, 1)].rearrange("p o i t -> p (o i) t"),
                                ALU.mult).then_inc(dt_ready, 1)

            def drive(b, s):
                n, half = s // 2, s % 2
                if s == 0:
                    dve.wait_ge(dt_ready, 2 * b + 2)
                if s % (2 * BG) == 0:
                    g = s // (2 * BG)
                    dve.wait_ge(b_loaded[g % 2], 16 * (2 * b + g // 2 + 1))
                dve.wait_ge(scanned, STEPS * b + s + PRIME - 1)
                V.tensor_tensor(dbx[:, s % 2], dtx[:, half * HALF:(half + 1) * HALF],
                                b_all[:, n // BG % 2, n % BG].unsqueeze(1).broadcast_to([P, HALF, T]),
                                ALU.mult).then_inc(dbx_ready, 1)

            def scan(b, s):
                dve.wait_ge(dbx_ready, STEPS * b + s + 1)
                dve.wait_ge(da_ready, HALF * (STEPS * b + s + 1))
                if s >= 2:
                    dve.wait_ge(turned, TJ * (STEPS * b + s - 1))
                V.tensor_tensor_scan(hs[:, s % 2].rearrange("p i t -> p (i t)"), da[:, s % 2].rearrange("p i t -> p (i t)"),
                                     dbx[:, s % 2].rearrange("p i t -> p (i t)"), 0.0, ALU.mult, ALU.add)\
                    .then_inc(scanned, 1)

            def weigh(b, s, j):
                n, half = s // 2, s % 2
                dve.wait_ge(turned, TJ * (STEPS * b + s) + j + 1)
                out = y[:, j, half * SW // TJ:(half + 1) * SW // TJ]
                c = c_tok[:, bass.ds(b % 2, 1), j, n:n + 1].rearrange("p o n -> p (o n)")
                if n == 0:
                    if s == 0 and j == 0:
                        dve.wait_ge(y_turned, 4 * b + START)
                        dve.wait_ge(c_ready, b + 1)
                    V.tensor_scalar(out, ps_h[:, s % 2, j], c, None, ALU.mult).then_inc(summed, 1)
                else:
                    dve.wait_ge(summed, TJ * (STEPS * b + s - 2) + j + 1)
                    V.scalar_tensor_tensor(out, ps_h[:, s % 2, j], c, out, ALU.mult, ALU.add).then_inc(summed, 1)

            def gate_y(b):
                for i in range(DI):
                    if i % 2 == 0:
                        dve.wait_ge(y_turned, 4 * b + i // 2 + 1 + START)
                    if i == 0:
                        dve.wait_ge(out_ready, TJ * (b + 1))
                    V.scalar_tensor_tensor(yg[:, i], xs[:, bass.ds(b % 2, 1), i, :].rearrange("p o t -> p (o t)"),
                                           d_w[:, i:i + 1], ps_p[:, i // 2, i % 2 * T:(i % 2 + 1) * T],
                                           ALU.mult, ALU.add).then_inc(gated, 1)
                dve.wait_ge(gated, (DI + 1) * b + DI + START)
                V.tensor_tensor(yg[:], yg[:], gate[:, bass.ds(b % 2, 1)].rearrange("p o i t -> p (o i) t"),
                                ALU.mult).then_inc(gated, 1)

            def add_res(b, j):
                dve.wait_ge(out_ready, TJ * b + j + 1)
                r = res[:, bass.ds((b + 1) % 2, 1), j, :].rearrange("p o d -> p (o d)")
                V.tensor_tensor(r, ps_p[:, 2 + j], r, ALU.add).then_inc(h1_ready, 1)

            def first_convolve():
                n = 0
                for i in range(DI):
                    if i % 2 == 0:
                        dve.wait_ge(emptied, 3 + i // 2)
                    V.tensor_scalar(t1[:, i], xc[:, i, 0:T], conv_w[:, i, 0:1], None, ALU.mult).then_inc(first_step, 1)
                    for k in range(1, TAPS):
                        n += 1
                        dve.wait_ge(first_step, n)
                        V.scalar_tensor_tensor(t1[:, i], xc[:, i, k:k + T], conv_w[:, i, k:k + 1], t1[:, i],
                                               ALU.mult, ALU.add).then_inc(first_step, 1)
                    n += 1
                dve.wait_ge(first_step, TAPS * DI)
                dve.sem_inc(conv_step, CONV_OPS)

            prep_stats(0)
            first_convolve()
            softplus(0)
            with dve.Fori(0, BATCH) as b:
                for s in range(STEPS):
                    drive(b, s)
                    if s >= 2:
                        weigh(b, s - 2, 0)
                    scan(b, s)
                    if s >= 2:
                        weigh(b, s - 2, 1)
                    if s == 0:
                        prep_stats(b + 1)
                    if s in (3, 5):
                        add_res(b, s // 2 - 1)
                for s in (STEPS - 2, STEPS - 1):
                    weigh(b, s, 0)
                    weigh(b, s, 1)
                softplus(b + 1)
                gate_y(b)
            for j in range(TJ):
                add_res(BATCH, j)

        @block.tensor
        def _(pe):
            M = nc.tensor.matmul
            for signal in (y_turned,):
                pe.sem_inc(signal, START)
            pe.wait_ge(consts, 10)

            def fill_wait(m, f):
                if f < 2:
                    return
                if f == 12:
                    pe.wait_ge(c_ready, m + 1)
                else:
                    pe.wait_ge(emptied, FILLS * m + f - 1)

            def fill_u(m):
                pe.wait_ge(u_ready, TJ * (m + 1))
                for f in range(2):
                    fill_wait(m, f)
                    for i in range(2):
                        kc = 2 * f + i
                        for j in range(TJ):
                            last = nc.tensor.transpose(ps_p[:, f, i * T + j * P:i * T + (j + 1) * P],
                                                       u[:, j, kc * P:(kc + 1) * P], ident[:])
                    last.then_inc(filled, 1)

            def fill_in(m, i):
                if i == 0:
                    pe.wait_ge(emptied, FILLS * m + 2)
                fill_wait(m, 2 + i)
                for k in range(2):
                    r = (2 * i + k) * P
                    for kc in range(KC):
                        last = M(ps_p[:, i % 2, k * T:(k + 1) * T], w_in[:, kc, r:r + P], u_t[:, kc],
                                 start=(kc == 0), stop=(kc == KC - 1))
                last.then_inc(filled, 1)

            def fill_x(m):
                pe.wait_ge(xs_ready, (DI + 1) * (m + 1))
                for f, r in ((0, 0), (1, WX - P)):
                    fill_wait(m, 10 + f)
                    for i in range(DI):
                        last = M(ps_p[:, f, 0:T], w_x[:, i, r:r + P],
                                 xs[:, bass.ds(m % 2, 1), i, :].rearrange("p o t -> p (o t)"),
                                 start=(i == 0), stop=(i == DI - 1))
                    last.then_inc(filled, 1)

            def turn_c(m):
                pe.wait_ge(emptied, FILLS * m + 12)
                for j in range(TJ):
                    last = nc.tensor.transpose(ps_p[:, 0, j * P:(j + 1) * P], bc_t[:, j * P:(j + 1) * P], ident[:])
                last.then_inc(c_turned, 1)

            def fill_dt(m, i):
                fill_wait(m, 12 + i)
                for k in range(2):
                    c = 2 * i + k
                    last = M(ps_p[:, i % 2, k * T:(k + 1) * T], w_dt[:, c * P:(c + 1) * P], dt_lr[:], start=True, stop=True)
                last.then_inc(filled, 1)

            def turn(b, s):
                pe.wait_ge(scanned, STEPS * b + s + 1 + PRIME)
                for j in range(TJ):
                    if s >= 2:
                        pe.wait_ge(summed, TJ * (STEPS * b + s - 2) + j + 1)
                    for i in range(HALF):
                        last = nc.tensor.transpose(ps_h[:, s % 2, j, i * P:(i + 1) * P], hs[:, s % 2, i, j * P:(j + 1) * P],
                                                   ident[:])
                    last.then_inc(turned, 1)

            def turn_y(b):
                pe.wait_ge(summed, TJ * STEPS * (b + 1))
                pe.wait_ge(emptied, FILLS * (b + 2))
                pe.wait_ge(h1_ready, TJ * (b + 1))
                for i in range(DI):
                    for j in range(TJ):
                        last = nc.tensor.transpose(ps_p[:, i // 2, i % 2 * T + j * P:i % 2 * T + (j + 1) * P],
                                                   y[:, j, i * P:(i + 1) * P], ident[:])
                    if i % 2:
                        last.then_inc(y_turned, 1)

            def project_out(b, j, part):
                if j == 0 and part == 0:
                    pe.wait_ge(gated, (DI + 1) * b + START)
                for i in range(part * DI // 2, (part + 1) * DI // 2):
                    last = M(ps_p[:, 2 + j], yg[:, i, j * P:(j + 1) * P], w_out[:, i], start=(i == 0), stop=(i == DI - 1))
                if part:
                    last.then_inc(out_ready, 1)

            pieces = {1: [fill_u], 12: [fill_x], 13: [turn_c]}
            for i in range(8):
                pieces.setdefault(2 + i, []).append(lambda m, i=i: fill_in(m, i))
            for i in range(4):
                pieces.setdefault(13 + i // 2, []).append(lambda m, i=i: fill_dt(m, i))
            for n in range(NS):
                if n == 2:
                    pe.wait_ge(w_in_loaded, 16)
                if n == 12:
                    pe.wait_ge(weights, 16 * LOADS)
                for piece in pieces.get(n, []):
                    piece(0)
            with pe.Fori(0, BATCH) as b:
                for s in range(STEPS):
                    if s < 4:
                        project_out(b, s // 2, s % 2)
                    if s % 2 == 0:
                        for piece in pieces.get(s // 2, []):
                            piece(b + 1)
                    turn(b, s)
                turn_y(b)
            for j in range(TJ):
                for part in range(2):
                    project_out(BATCH, j, part)


def expert_stage(nc, io, h1_scratch, out):
    BATCH, T, D = out.shape
    KC = D // P
    TJ = T // P
    NT = BATCH * TJ
    E = io["sim"].shape[1] // KC
    HD = P
    W3 = 3 * HD
    SCALE = 1.0 / math.sqrt(HD)
    NEG = -1e9

    with ExitStack() as outer:
        def sb_in(stack, name, shape, dt=F32):
            return stack.enter_context(nc.sbuf_tensor(name, shape, dt))

        def sem(name):
            return outer.enter_context(nc.semaphore(name))

        w = sb_in(outer, "ff_w", [P, NT, E])
        ident = sb_in(outer, "ff_ident", [P, P])
        consts = sem("ff_consts")
        done_experts = sem("ff_done_experts")
        act_idle, pool_idle, dve_idle, sp_idle = (sem(f"ff_idle_{n}") for n in ("act", "pool", "dve", "sp"))
        idle = [dve_idle, pool_idle]
        qkv = sb_in(outer, "ff_qkv", [P, NT, W3])

        with ExitStack() as mid:
            x_hi = sb_in(mid, "ff_x_hi", [P, KC, NT, P], F32R)
            x_lo = sb_in(mid, "ff_x_lo", [P, KC, NT, P], F32R)

            with ExitStack() as ctx:
                ps = ctx.enter_context(nc.psum_tensor("ff_ps1", [P, 8, 512], F32))

                def sb(name, shape, dt=F32):
                    return sb_in(ctx, name, shape, dt)

                minus_half = sb("ff_minus_half", [P, E])
                minus_one = sb("ff_minus_one", [P, TJ])
                width = sb("ff_width", [P, TJ])
                eps = sb("ff_eps", [P, TJ])
                ones = sb("ff_ones", [P, P])
                rank_i = sb("ff_rank_i", [P, E], I32)
                rank = sb("ff_rank", [P, E])
                sim = sb("ff_sim", [P, KC, E])
                sim_sq = sb("ff_sim_sq", [P, KC, E])
                sim_rn = sb("ff_sim_rn", [P, E])
                sim_hi = sb("ff_sim_hi", [P, KC, E], F32R)
                sim_lo = sb("ff_sim_lo", [P, KC, E], F32R)
                gates = sb("ff_gates", [P, E])
                hin = sb("ff_hin", [P, 2, TJ, D])
                stats = sb("ff_stats", [P, 2, TJ, 6])
                mv = sb("ff_mv", [P, 2, TJ, 2])
                ln = sb("ff_ln", [P, 2, 4, TJ])
                xn = sb("ff_xn", [P, 2, TJ, D])
                rn = sb("ff_rn", [P, NT])
                r = [qkv[:, :, i * E:(i + 1) * E] for i in range(5)]
                col = sb("ff_col", [P, 4, NT])

                loaded = sem("ff_loaded")
                hin_loaded = [sem(f"ff_hin_loaded{i}") for i in range(2)]
                stats_step = sem("ff_stats_step")
                ln_step = sem("ff_ln_step")
                xn_ready = sem("ff_xn_ready")
                filled = sem("ff_filled")
                hi_ready = sem("ff_hi_ready")
                lo_ready = sem("ff_lo_ready")
                sim_step = sem("ff_sim_step")
                sim_summed = sem("ff_sim_summed")
                sim_norm = sem("ff_sim_norm")
                gate_step = sem("ff_gate_step")
                logits_ready = sem("ff_logits_ready")
                route_step = sem("ff_route_step")
                route_exp = sem("ff_route_exp")
                LN_OPS = 8
                ROUTE_EXP = 26
                block = ctx.enter_context(nc.Block())

                @block.sync
                def _(sp):
                    for signal in (xn_ready, filled, ln_step, lo_ready):
                        sp.sem_inc(signal, START)
                    sp.dma_start(sim[:].rearrange("p k e -> p (k e)"), io["sim"]).then_inc(loaded, 16)
                    sp.dma_start(gates[:], io["gates"].partition_broadcast(P)).then_inc(loaded, 16)
                    with sp.Fori(0, BATCH // 2) as b2:
                        for o in range(2):
                            row = bass.ds(sp.snap(2 * b2 + (o + 1)), 1)
                            sp.wait_ge(xn_ready, TJ * 2 * b2 + START)
                            sp.dma_start(hin[:, o], h1_scratch[row]
                                         .rearrange("o (j p) d -> (o p) j d", p=P)).then_inc(hin_loaded[o], 16)

                @block.gpsimd
                def _(pool):
                    G = nc.gpsimd
                    G.memset(ident[:], 0.0).then_inc(consts, 1)
                    G.memset(ones[:], 1.0).then_inc(consts, 1)
                    G.memset(minus_half[:], -0.5).then_inc(consts, 1)
                    G.memset(minus_one[:], -1.0).then_inc(consts, 1)
                    G.memset(width[:], float(D)).then_inc(consts, 1)
                    G.memset(eps[:], EPS).then_inc(consts, 1)
                    G.iota(rank_i[:], pattern=[[-1, E]], base=E, channel_multiplier=0).then_inc(consts, 1)
                    pool.wait_ge(consts, 7)
                    G.affine_select(out=ident[:], in_=ident[:], compare_op=ALU.not_equal, fill=1.0, base=0,
                                    pattern=[[-1, P]], channel_multiplier=1).then_inc(consts, 1)
                    G.tensor_copy(rank[:], rank_i[:]).then_inc(consts, 1)
                    pool.wait_ge(consts, 9)
                    pool.wait_ge(sim_step, 2)
                    G.tensor_tensor(sim_rn[:], sim_rn[:], minus_half[:, 0:E], ALU.pow).then_inc(sim_norm, 1)
                    with pool.Fori(0, BATCH // 2) as b2:
                        for o in range(2):
                            n = [0]

                            def link(ins):
                                n[0] += 1
                                ins.then_inc(ln_step, 1)
                                pool.wait_ge(ln_step, (2 * b2 + o) * LN_OPS + n[0] + START)

                            pool.wait_ge(stats_step, 2 * TJ * (2 * b2 + o + 1))
                            pool.wait_ge(xn_ready, TJ * 2 * b2 + START)
                            pool.sem_inc(pool_idle, 1)
                            mean, var = mv[:, o, :, 0], mv[:, o, :, 1]
                            half = minus_half[:, 0:TJ]
                            link(G.tensor_tensor(ln[:, o, 0], var, eps[:], ALU.add))
                            link(G.tensor_tensor(ln[:, o, 0], ln[:, o, 0], half, ALU.pow))
                            link(G.tensor_tensor(ln[:, o, 1], mean, ln[:, o, 0], ALU.mult))
                            link(G.tensor_tensor(ln[:, o, 2], var, ln[:, o, 0], ALU.mult))
                            link(G.tensor_tensor(ln[:, o, 2], ln[:, o, 2], ln[:, o, 0], ALU.mult))
                            link(G.tensor_tensor(ln[:, o, 1], ln[:, o, 1], minus_one[:, 0:TJ], ALU.mult))
                            link(G.tensor_tensor(ln[:, o, 2], ln[:, o, 2], width[:, 0:TJ], ALU.mult))
                            pool.sem_inc(pool_idle, 1)
                            link(G.tensor_tensor(rn[:, bass.ds((2 * b2 + o) * TJ, TJ)], ln[:, o, 2], half, ALU.pow))
                            assert n[0] == LN_OPS

                @block.scalar
                def _(act):
                    A = nc.scalar
                    act.wait_ge(loaded, 32)
                    act.wait_ge(consts, 9)
                    A.activation(gates[:], gates[:], ACT.Exp, scale=-1.0).then_inc(gate_step, 1)
                    act.wait_ge(sim_step, 3)
                    A.activation(sim_hi[:], sim_sq[:], ACT.Copy).then_inc(sim_norm, 1)
                    with act.Fori(0, BATCH // 2) as b2:
                        for o in range(2):
                            act.wait_ge(ln_step, LN_OPS * (2 * b2 + o + 1) + START)
                            act.wait_ge(filled, TJ * 2 * b2 + START)
                            for j in range(TJ):
                                A.activation(xn[:, o, j], hin[:, o, j], ACT.Identity, scale=ln[:, o, 0, j:j + 1],
                                             bias=ln[:, o, 1, j:j + 1]).then_inc(xn_ready, 1)
                        for o in range(2):
                            for j in range(TJ):
                                act.wait_ge(filled, TJ * (2 * b2 + o) + j + 1 + START)
                                act.sem_inc(act_idle, 1)
                                A.activation(x_hi[:, :, bass.ds((2 * b2 + o) * TJ + j, 1), :].rearrange("p k o t -> p (k o) t"),
                                             ps[:, o * TJ + j].rearrange("p (k t) -> p k t", k=KC),
                                             ACT.Copy).then_inc(hi_ready, 1)
                    act.wait_ge(route_step, ROUTE_EXP)
                    A.activation(r[0], r[0], ACT.Exp).then_inc(route_exp, 1)

                @block.vector
                def _(dve):
                    V = nc.vector
                    dve.wait_ge(loaded, 32)
                    dve.wait_ge(consts, 9)
                    V.tensor_tensor(sim_sq[:], sim[:], sim[:], ALU.mult).then_inc(sim_step, 1)
                    dve.wait_ge(sim_summed, 1)
                    V.tensor_scalar(sim_rn[:], ps[:, 0, 0:E], 1e-24, None, ALU.max).then_inc(sim_step, 1)
                    dve.wait_ge(sim_norm, 1)
                    V.tensor_tensor(sim_sq[:], sim[:], sim_rn[:].unsqueeze(1).broadcast_to([P, KC, E]),
                                    ALU.mult).then_inc(sim_step, 1)
                    dve.wait_ge(sim_norm, 2)
                    V.tensor_tensor(sim_lo[:], sim_sq[:], sim_hi[:].bitcast(F32), ALU.subtract).then_inc(sim_step, 1)
                    dve.wait_ge(gate_step, 1)
                    V.tensor_scalar(gates[:], gates[:], 1.0, None, ALU.add).then_inc(gate_step, 1)
                    dve.wait_ge(gate_step, 2)
                    V.reciprocal(gates[:], gates[:]).then_inc(gate_step, 1)
                    with dve.Fori(0, BATCH // 2) as b2:
                        for o in range(2):
                            dve.wait_ge(hin_loaded[o], 16 * (b2 + 1))
                            dve.wait_ge(ln_step, LN_OPS * 2 * b2 + START)
                            for j in range(TJ):
                                V.bn_stats(stats[:, o, j], hin[:, o, j]).then_inc(stats_step, 1)
                            dve.wait_ge(stats_step, 2 * TJ * (2 * b2 + o) + TJ)
                            dve.sem_inc(dve_idle, 1)
                            for j in range(TJ):
                                V.bn_aggr(mv[:, o, j], stats[:, o, j]).then_inc(stats_step, 1)
                        for o in range(2):
                            for j in range(TJ):
                                tile = (2 * b2 + o) * TJ + j
                                dve.wait_ge(hi_ready, tile + 1)
                                V.tensor_tensor(x_lo[:, :, bass.ds(tile, 1), :].rearrange("p k o t -> p (k o) t"),
                                                ps[:, o * TJ + j].rearrange("p (k t) -> p k t", k=KC),
                                                x_hi[:, :, bass.ds(tile, 1), :].rearrange("p k o t -> p (k o) t").bitcast(F32),
                                                ALU.subtract).then_inc(lo_ready, 1)
                    n = [0]

                    def link(ins):
                        n[0] += 1
                        ins.then_inc(route_step, 1)
                        dve.wait_ge(route_step, n[0])

                    def by_token(x):
                        return x.unsqueeze(2).broadcast_to([P, NT, E])

                    def by_expert(x):
                        return x.unsqueeze(1).broadcast_to([P, NT, E])

                    logits, gated, mask, pick, key = r
                    first, top, none = col[:, 0], col[:, 1], col[:, 2]
                    dve.wait_ge(ln_step, LN_OPS * BATCH + START)
                    dve.wait_ge(logits_ready, 1)
                    link(V.tensor_tensor(logits, ps[:, 7].rearrange("p (t e) -> p t e", e=E), by_token(rn[:]), ALU.mult))
                    link(V.tensor_tensor(logits, logits, by_expert(gates[:]), ALU.subtract))
                    link(V.tensor_scalar(mask, logits, 0.0, None, ALU.is_gt))
                    link(V.tensor_scalar(gated, logits, 0.0, None, ALU.max))
                    link(V.tensor_reduce(none, mask, AX.X, ALU.max))
                    link(V.tensor_scalar(none, none, -1.0, 1.0, ALU.mult, ALU.add))
                    for k in range(2):
                        link(V.tensor_reduce(top, logits, AX.X, ALU.max))
                        link(V.tensor_tensor(key, logits, by_token(top), ALU.is_equal))
                        link(V.tensor_tensor(key, key, by_expert(rank[:]), ALU.mult))
                        link(V.tensor_reduce(first, key, AX.X, ALU.max))
                        link(V.tensor_tensor(key, by_expert(rank[:]), by_token(first), ALU.is_equal))
                        if k == 0:
                            link(V.tensor_copy(pick, key))
                            link(V.scalar_tensor_tensor(logits, key, -1e30, logits, ALU.mult, ALU.add))
                    link(V.tensor_tensor(pick, pick, key, ALU.add))
                    link(V.tensor_tensor(pick, pick, by_token(none), ALU.mult))
                    link(V.tensor_tensor(mask, mask, pick, ALU.add))
                    link(V.tensor_tensor(gated, gated, mask, ALU.mult))
                    link(V.tensor_scalar(key, mask, 1.0, -NEG, ALU.subtract, ALU.mult))
                    link(V.tensor_tensor(gated, gated, key, ALU.add))
                    link(V.tensor_reduce(top, gated, AX.X, ALU.max))
                    link(V.tensor_tensor(logits, gated, by_token(top), ALU.subtract))
                    assert n[0] == ROUTE_EXP, n[0]
                    dve.wait_ge(route_exp, 1)
                    link(V.tensor_reduce(top, logits, AX.X, ALU.add))
                    link(V.reciprocal(first, top))
                    link(V.tensor_tensor(logits, logits, mask, ALU.mult))
                    link(V.tensor_tensor(w[:], logits, by_token(first), ALU.mult))

                @block.tensor
                def _(pe):
                    pe.wait_ge(consts, 9)
                    pe.wait_ge(sim_step, 1)
                    for k in range(KC):
                        last = nc.tensor.matmul(ps[:, 0, 0:E], ones[:], sim_sq[:, k], start=(k == 0), stop=(k == KC - 1))
                    last.then_inc(sim_summed, 1)
                    pe.wait_ge(sim_step, 4)
                    with pe.Fori(0, BATCH // 2) as b2:
                        for o in range(2):
                            for j in range(TJ):
                                pe.wait_ge(xn_ready, TJ * (2 * b2 + o) + j + 1 + START)
                                pe.wait_ge(lo_ready, TJ * 2 * b2 + START)
                                for k in range(KC):
                                    last = nc.tensor.transpose(ps[:, o * TJ + j, k * P:(k + 1) * P],
                                                               xn[:, o, j, k * P:(k + 1) * P], ident[:])
                                last.then_inc(filled, 1)
                    pe.wait_ge(lo_ready, NT + START)
                    for i in range(NT):
                        first = True
                        for a, s in ((x_hi, sim_hi), (x_hi, sim_lo), (x_lo, sim_hi)):
                            for k in range(KC):
                                last = nc.tensor.matmul(ps[:, 7, i * E:(i + 1) * E], a[:, k, i], s[:, k],
                                                        start=first, stop=(a is x_lo and k == KC - 1))
                                first = False
                    last.then_inc(logits_ready, 1)

            with ExitStack() as ctx:
                ps = ctx.enter_context(nc.psum_tensor("ff_ps2", [P, 8, 512], F32))
                KH = KC // 2
                raw = sb_in(ctx, "ff_raw", [P, KH, W3])
                e_hi = sb_in(ctx, "ff_e_hi", [P, 2, KC, W3], F32R)
                e_lo = sb_in(ctx, "ff_e_lo", [P, 2, KC, W3], F32R)
                raw_loaded = sem("ff_raw_loaded")
                raw_hi = sem("ff_raw_hi")
                raw_lo = sem("ff_raw_lo")
                cleared = sem("ff_cleared")
                mixed = sem("ff_mixed")
                added = sem("ff_added")
                BANKS = 8
                block = ctx.enter_context(nc.Block())

                @block.sync
                def _(sp):
                    for signal in (raw_lo,):
                        sp.sem_inc(signal, START)
                    with sp.Fori(0, E) as e:
                        for h in range(2):
                            cols = bass.ds(sp.snap((2 * e + h) * KH * W3), KH * W3)
                            sp.wait_ge(raw_lo, 2 * e + h + START)
                            sp.dma_start(raw[:].rearrange("p k n -> p (k n)"),
                                         io["w_qkv"][:, cols]).then_inc(raw_loaded, 16)

                @block.gpsimd
                def _(pool):
                    nc.gpsimd.memset(qkv[:], 0.0).then_inc(cleared, 1)
                    pool.wait_ge(cleared, 1)

                @block.scalar
                def _(act):
                    with act.Fori(0, E) as e:
                        for h in range(2):
                            act.wait_ge(raw_loaded, 16 * (2 * e + h + 1))
                            act.wait_ge(done_experts, e + 1)
                            act.sem_inc(act_idle, 1)
                            nc.scalar.activation(e_hi[:, bass.ds(e % 2, 1), h * KH:(h + 1) * KH].rearrange("p o k n -> p (o k) n"),
                                                 raw[:], ACT.Copy).then_inc(raw_hi, 1)

                @block.vector
                def _(dve):
                    V = nc.vector
                    dve.sem_inc(added, BANKS)
                    dve.wait_ge(cleared, 1)

                    def split(e, h):
                        dve.wait_ge(raw_hi, 2 * e + h + 1)
                        hi = e_hi[:, bass.ds(e % 2, 1), h * KH:(h + 1) * KH].rearrange("p o k n -> p (o k) n")
                        lo = e_lo[:, bass.ds(e % 2, 1), h * KH:(h + 1) * KH].rearrange("p o k n -> p (o k) n")
                        V.tensor_tensor(lo, raw[:], hi.bitcast(F32), ALU.subtract).then_inc(raw_lo, 1)

                    def add(e, i):
                        dve.wait_ge(mixed, NT * e + i + 1)
                        V.scalar_tensor_tensor(qkv[:, i], ps[:, i % BANKS, 0:W3], w[:, i, bass.ds(e, 1)], qkv[:, i],
                                               ALU.mult, ALU.add).then_inc(added, 1)

                    split(0, 0)
                    split(0, 1)
                    with dve.Fori(0, E - 1) as e:
                        for i in range(NT):
                            if i in (4, 8):
                                split(e + 1, i // 4 - 1)
                            add(e, i)
                    for i in range(NT):
                        add(E - 1, i)

                @block.tensor
                def _(pe):
                    pe.sem_inc(done_experts, 2)
                    with pe.Fori(0, E) as e:
                        pe.wait_ge(raw_lo, 2 * e + 2 + START)
                        for i in range(NT):
                            pe.wait_ge(added, NT * e + i + 1)
                            first = True
                            for a, s in ((x_hi, e_hi), (x_hi, e_lo), (x_lo, e_hi)):
                                for k in range(KC):
                                    last = nc.tensor.matmul(ps[:, i % BANKS, 0:W3], a[:, k, i],
                                                            s[:, bass.ds(e % 2, 1), k, :].rearrange("p o n -> p (o n)"),
                                                            start=first, stop=(a is x_lo and k == KC - 1))
                                    first = False
                            last.then_inc(mixed, 1)
                        pe.wait_ge(mixed, NT * (e + 1))
                        pe.sem_inc(done_experts, 1)

        with ExitStack() as ctx:
            def sb(name, shape, dt=F32):
                return sb_in(ctx, name, shape, dt)

            EG = 4
            NG = TJ * E // EG
            RS = 4
            ps_o = ctx.enter_context(nc.psum_tensor("ff_ps_o", [P, TJ, 512], F32))
            ps_w = ctx.enter_context(nc.psum_tensor("ff_ps_w", [P, 2, 512], F32))
            ps_a = ctx.enter_context(nc.psum_tensor("ff_ps_a", [P, 3, 512], F32))
            o_raw = sb("ff_o_raw", [P, 2, D])
            o_hi = sb("ff_o_hi", [P, E, D], F32R)
            o_lo = sb("ff_o_lo", [P, E, D], F32R)
            keep = sb("ff_keep", [P, 3 * P])
            hide = sb("ff_hide", [P, 3 * P])
            qk = sb("ff_qk", [P, TJ, 2 * HD])
            qk_t = sb("ff_qk_t", [P, 2, T])
            score = sb("ff_score", [P, 3 * P])
            prob = sb("ff_prob", [P, 3 * P])
            prob_t = sb("ff_prob_t", [P, 3 * P])
            top = sb("ff_top", [P, TJ])
            total = sb("ff_total", [P, TJ])
            head = sb("ff_head", [P, TJ, HD])
            weighted = sb("ff_weighted", [P, TJ, E, HD])
            wt_hi = sb("ff_wt_hi", [P, RS, EG, P], F32R)
            wt_lo = sb("ff_wt_lo", [P, RS, EG, P], F32R)
            h1 = sb("ff_h1", [P, 2, TJ, D])
            o_loaded = [sem(f"ff_o_loaded{i}") for i in range(2)]
            o_hi_ready = sem("ff_o_hi_ready")
            o_lo_ready = sem("ff_o_lo_ready")
            masks = sem("ff_masks")
            qk_copied = sem("ff_qk_copied")
            qk_turned = sem("ff_qk_turned")
            qk_t_ready = sem("ff_qk_t_ready")
            scored = sem("ff_scored")
            score_step = sem("ff_score_step")
            prob_ready = sem("ff_prob_ready")
            prob_turned = sem("ff_prob_turned")
            prob_t_ready = sem("ff_prob_t_ready")
            head_summed = sem("ff_head_summed")
            inv_ready = sem("ff_inv_ready")
            head_ready = sem("ff_head_ready")
            weighted_ready = [sem(f"ff_weighted_ready{i}") for i in range(TJ)]
            wt_turned = sem("ff_wt_turned")
            wt_hi_ready = sem("ff_wt_hi_ready")
            wt_lo_ready = sem("ff_wt_lo_ready")
            wt_used = sem("ff_wt_used")
            out_summed = sem("ff_out_summed")
            h1_loaded = sem("ff_h1_loaded")
            out_ready = sem("ff_out_ready")
            out_stored = sem("ff_out_stored")
            SCORE_OPS = 5
            block = ctx.enter_context(nc.Block())

            @block.sync
            def _(sp):
                for signal in (out_stored, wt_turned, out_ready):
                    sp.sem_inc(signal, START)
                for e in range(E):
                    if e >= 2:
                        sp.wait_ge(o_lo_ready, e - 1)
                    sp.dma_start(o_raw[:, e % 2], io["w_o"][:, e * D:(e + 1) * D]).then_inc(o_loaded[e % 2], 16)

                def load_h1(row, slot):
                    sp.dma_start(h1[:, slot].rearrange("p o j d -> p (o j) d"),
                                 h1_scratch[row].rearrange("o (j p) d -> (o p) j d", p=P)).then_inc(h1_loaded, 16)

                load_h1(bass.ds(1, 1), bass.ds(0, 1))
                with sp.Fori(0, BATCH) as b:
                    row, slot = bass.ds(sp.snap((b + 1) % BATCH + 1), 1), bass.ds(sp.snap((b + 1) % 2), 1)
                    sp.wait_ge(h1_loaded, 16 * (b + 1))
                    sp.sem_inc(sp_idle, 1)
                    sp.wait_ge(out_stored, 16 * b + START)
                    sp.sem_inc(sp_idle, 1)
                    load_h1(row, slot)
                    sp.wait_ge(out_ready, TJ * (b + 1) + START)
                    sp.sem_inc(sp_idle, 1)
                    sp.dma_start(out[bass.ds(b, 1)].rearrange("o (j p) d -> (o p) j d", p=P),
                                 h1[:, bass.ds(b % 2, 1)].rearrange("p o j d -> p (o j) d")).then_inc(out_stored, 16)
                sp.wait_ge(h1_loaded, 16 * (BATCH + 1))
                sp.wait_ge(out_stored, 16 * BATCH + START)

            def weigh_heads(eng, E_, m, j):
                eng.wait_ge(head_ready, TJ * m + j + 1)
                eng.wait_ge(wt_turned, NG * m + START)
                eng.sem_inc(idle[j], 1)
                E_.tensor_tensor(weighted[:, j], head[:, j].unsqueeze(1).broadcast_to([P, E, HD]),
                                 w[:, bass.ds((TJ * m) % NT + j, 1), :].rearrange("p o e -> p (o e)").unsqueeze(2)
                                 .broadcast_to([P, E, HD]), ALU.mult).then_inc(weighted_ready[j], 1)

            @block.gpsimd
            def _(pool):
                G = nc.gpsimd
                G.memset(keep[:], 1.0).then_inc(masks, 1)
                G.memset(hide[:], 0.0).then_inc(masks, 1)
                pool.wait_ge(masks, 2)
                for c in (0, 2 * P):
                    for m, fill in ((keep, 0.0), (hide, NEG)):
                        G.affine_select(out=m[:, c:c + P], in_=m[:, c:c + P], compare_op=ALU.is_ge, fill=fill, base=0,
                                        pattern=[[-1, P]], channel_multiplier=1).then_inc(masks, 1)
                with pool.Fori(0, BATCH + 1) as m:
                    weigh_heads(pool, G, m, 1)

            @block.scalar
            def _(act):
                A = nc.scalar
                for e in range(E):
                    act.wait_ge(o_loaded[e % 2], 16 * (e // 2 + 1))
                    A.activation(o_hi[:, e], o_raw[:, e % 2], ACT.Copy).then_inc(o_hi_ready, 1)

                def copy_qk(m):
                    act.wait_ge(qk_turned, m)
                    act.sem_inc(act_idle, 1)
                    A.activation(qk[:], qkv[:, bass.ds((TJ * m) % NT, TJ), 0:2 * HD], ACT.Copy).then_inc(qk_copied, 1)

                def place_qk_t(m):
                    act.wait_ge(scored, m)
                    act.wait_ge(qk_turned, m + 1)
                    A.activation(qk_t[:].rearrange("p a t -> p (a t)"), ps_a[:, 0], ACT.Copy).then_inc(qk_t_ready, 1)

                def exponentials(m):
                    act.wait_ge(score_step, SCORE_OPS * (m + 1))
                    act.wait_ge(prob_turned, m)
                    act.wait_ge(head_ready, TJ * m)
                    A.activation(prob[:, 0:P], score[:, 0:P], ACT.Exp, bias=top[:, 0:1],
                                 accum_out=total[:, 0:1]).then_inc(prob_ready, 1)
                    A.activation(prob[:, P:], score[:, P:], ACT.Exp, bias=top[:, 1:2],
                                 accum_out=total[:, 1:2]).then_inc(prob_ready, 1)

                def place_prob_t(m):
                    act.wait_ge(head_summed, m)
                    act.wait_ge(prob_turned, m + 1)
                    A.activation(prob_t[:], ps_a[:, 2, 0:3 * P], ACT.Copy).then_inc(prob_t_ready, 1)

                def place_heads(m):
                    act.wait_ge(inv_ready, m + 1)
                    act.wait_ge(weighted_ready[0], m)
                    act.wait_ge(weighted_ready[1], m)
                    act.wait_ge(head_summed, m + 1)
                    for j in range(TJ):
                        A.activation(head[:, j], ps_a[:, 0, j * HD:(j + 1) * HD], ACT.Copy,
                                     scale=total[:, j:j + 1]).then_inc(head_ready, 1)

                steps = {0: copy_qk, 1: place_qk_t, 4: exponentials, 6: place_prob_t, 7: place_heads}
                for k in sorted(steps):
                    steps[k](0)
                with act.Fori(0, BATCH) as b:
                    for g in range(NG):
                        act.wait_ge(wt_turned, NG * b + g + 1 + START)
                        act.wait_ge(wt_used, NG * b + g + 1)
                        A.activation(wt_hi[:, g % RS], ps_w[:, g % 2].rearrange("p (e t) -> p e t", e=EG),
                                     ACT.Copy).then_inc(wt_hi_ready, 1)
                        if g in steps:
                            steps[g](b + 1)

            @block.vector
            def _(dve):
                V = nc.vector
                dve.sem_inc(wt_lo_ready, 2)
                for e in range(E):
                    dve.wait_ge(o_hi_ready, e + 1)
                    V.tensor_tensor(o_lo[:, e], o_raw[:, e % 2], o_hi[:, e].bitcast(F32), ALU.subtract)\
                        .then_inc(o_lo_ready, 1)
                dve.wait_ge(masks, 6)

                def mask_scores(m):
                    n = [0]

                    def link(ins):
                        n[0] += 1
                        ins.then_inc(score_step, 1)
                        dve.wait_ge(score_step, SCORE_OPS * m + n[0])

                    dve.wait_ge(scored, m + 1)
                    dve.wait_ge(prob_ready, TJ * m)
                    link(V.scalar_tensor_tensor(score[:], ps_a[:, 1, 0:3 * P], SCALE, keep[:], ALU.mult, ALU.mult))
                    link(V.tensor_tensor(score[:], score[:], hide[:], ALU.add))
                    link(V.tensor_reduce(top[:, 0:1], score[:, 0:P], AX.X, ALU.max))
                    link(V.tensor_reduce(top[:, 1:2], score[:, P:], AX.X, ALU.max))
                    link(V.tensor_scalar(top[:], top[:], -1.0, None, ALU.mult))
                    assert n[0] == SCORE_OPS

                def invert(m):
                    dve.wait_ge(prob_ready, TJ * (m + 1))
                    V.reciprocal(total[:], total[:]).then_inc(inv_ready, 1)

                def weigh(m):
                    weigh_heads(dve, V, m, 0)

                def finish(b, j):
                    dve.wait_ge(out_summed, TJ * b + j + 1)
                    dve.wait_ge(h1_loaded, 16 * (b + 1))
                    h = h1[:, bass.ds(b % 2, 1), j, :].rearrange("p o d -> p (o d)")
                    V.tensor_tensor(h, ps_o[:, j], h, ALU.add).then_inc(out_ready, 1)

                steps = {3: mask_scores, 5: invert, 7: weigh}
                for k in sorted(steps):
                    steps[k](0)
                with dve.Fori(0, BATCH) as b:
                    for g in range(NG):
                        dve.wait_ge(wt_hi_ready, NG * b + g + 1)
                        V.tensor_tensor(wt_lo[:, g % RS], ps_w[:, g % 2].rearrange("p (e t) -> p e t", e=EG),
                                        wt_hi[:, g % RS].bitcast(F32), ALU.subtract).then_inc(wt_lo_ready, 1)
                        if g in steps:
                            steps[g](b + 1)
                        if g == NG // 2 + 2:
                            finish(b, 0)
                    finish(b, 1)

            @block.tensor
            def _(pe):
                M = nc.tensor.matmul
                pe.sem_inc(wt_used, RS)

                def turn_qk(m):
                    pe.wait_ge(qk_copied, m + 1)
                    pe.wait_ge(head_ready, TJ * m)
                    for a in range(2):
                        for j in range(TJ):
                            last = nc.tensor.transpose(ps_a[:, 0, a * T + j * P:a * T + (j + 1) * P],
                                                       qk[:, j, a * HD:(a + 1) * HD], ident[:])
                    last.then_inc(qk_turned, 1)

                def score_tokens(m):
                    pe.wait_ge(qk_t_ready, m + 1)
                    pe.wait_ge(score_step, SCORE_OPS * m)
                    M(ps_a[:, 1, 0:P], qk_t[:, 0, 0:P], qk_t[:, 1, 0:P], start=True, stop=True)
                    M(ps_a[:, 1, P:3 * P], qk_t[:, 0, P:], qk_t[:, 1], start=True, stop=True).then_inc(scored, 1)

                def turn_prob(m):
                    pe.wait_ge(prob_ready, TJ * (m + 1))
                    pe.wait_ge(prob_t_ready, m)
                    for k in range(3):
                        last = nc.tensor.transpose(ps_a[:, 2, k * P:(k + 1) * P], prob[:, k * P:(k + 1) * P], ident[:])
                    last.then_inc(prob_turned, 1)

                def sum_heads(m):
                    pe.wait_ge(prob_t_ready, m + 1)
                    for j, k, c in ((0, 0, 0), (1, 0, 1), (1, 1, 2)):
                        last = M(ps_a[:, 0, j * HD:(j + 1) * HD], prob_t[:, c * P:(c + 1) * P],
                                 qkv[:, bass.ds((TJ * m) % NT + k, 1), 2 * HD:].rearrange("p o h -> p (o h)"),
                                 start=(k == 0), stop=(k == j))
                    last.then_inc(head_summed, 1)

                def turn_weighted(b, g):
                    j, e0 = g // (NG // TJ), g % (NG // TJ) * EG
                    if g % (NG // TJ) == 0:
                        pe.wait_ge(weighted_ready[j], b + 1)
                    pe.wait_ge(wt_lo_ready, NG * b + g + 1)
                    for e in range(EG):
                        last = nc.tensor.transpose(ps_w[:, g % 2, e * P:(e + 1) * P], weighted[:, j, e0 + e], ident[:])
                    last.then_inc(wt_turned, 1)

                def project(b, g):
                    j, e0 = g // (NG // TJ), g % (NG // TJ) * EG
                    pe.wait_ge(wt_lo_ready, NG * b + g + 1 + 2)
                    if e0 == 0:
                        pe.wait_ge(out_ready, TJ * b + START)
                    for e in range(EG):
                        for a, s in ((wt_hi, o_hi), (wt_hi, o_lo), (wt_lo, o_hi)):
                            last = M(ps_o[:, j], a[:, g % RS, e], s[:, e0 + e],
                                     start=(e0 + e == 0 and a is wt_hi and s is o_hi),
                                     stop=(e0 + e == E - 1 and a is wt_lo))
                    last.then_inc(wt_used, 1)
                    if e0 + EG == E:
                        pe.wait_ge(wt_used, NG * b + g + 1 + RS)
                        pe.sem_inc(out_summed, 1)

                pieces = {0: turn_qk, 1: score_tokens, 4: turn_prob, 6: sum_heads}
                for k in sorted(pieces):
                    pieces[k](0)
                pe.wait_ge(o_lo_ready, E)
                with pe.Fori(0, BATCH) as b:
                    turn_weighted(b, 0)
                    for g in range(NG):
                        if g + 1 < NG:
                            turn_weighted(b, g + 1)
                        project(b, g)
                        if g in pieces:
                            pieces[g](b + 1)


def program(nc, io, out):
    batch, tokens, width = out.shape
    states = 16
    h0_scratch = nc.dram_tensor("h0_scratch", (batch, tokens, width), F32).ap()
    b_scratch = nc.dram_tensor("b_scratch", (states, tokens), F32).ap()
    h1_scratch = nc.dram_tensor("h1_scratch", (batch + 1, tokens, width), F32).ap()
    token_stage(nc, io, h0_scratch)
    mamba_stage(nc, io, h0_scratch, b_scratch, h1_scratch)
    expert_stage(nc, io, h1_scratch, out)


def _rows(w):
    return w.reshape(w.shape[0] // P, P, -1).transpose(1, 0, 2).reshape(P, -1)


def _layout(x, log_dt, log_w_real, w_imag, norm_w, w_in, conv_w, conv_b, w_x, w_dt, b_dt, a, d, w_out,
            sim, gates, q_proj, k_proj, v_proj, o_proj):
    import numpy as np

    ch, h, n, _ = x.shape
    experts, width, head = q_proj.shape
    pairs = h // 2

    def by_pair(w):
        return w.reshape(pairs, 2, n).transpose(1, 2, 0).reshape(2 * n, pairs)

    qkv = np.stack([q_proj, k_proj, v_proj], axis=2).reshape(experts, width // P, P, 3 * head)
    return {
        "xT": x.reshape(ch, pairs, 2, n, 2).transpose(2, 3, 4, 0, 1).reshape(2 * n, 2 * ch * pairs),
        "log_dt": log_dt.reshape(pairs, 2).T,
        "log_w_real": by_pair(log_w_real),
        "w_imag": by_pair(w_imag),
        "norm_w": _rows(norm_w),
        "w_in": _rows(w_in.T),
        "conv_w": _rows(conv_w),
        "conv_b": _rows(conv_b),
        "w_x": _rows(w_x.T),
        "w_dt": w_dt.T,
        "b_dt": _rows(b_dt),
        "a": _rows(a),
        "d": _rows(d),
        "w_out": _rows(w_out.T),
        "sim": _rows(sim),
        "gates": gates.reshape(1, experts),
        "w_qkv": qkv.transpose(2, 0, 1, 3).reshape(P, -1),
        "w_o": o_proj.transpose(1, 0, 2).reshape(head, -1),
    }


def kernel(x, L0_tok_log_dt, L0_tok_log_w_real, L0_tok_w_imag, L0_attn_norm_w, L0_attn_W_in, L0_attn_conv_w,
           L0_attn_conv_b, L0_attn_W_x, L0_attn_W_dt, L0_attn_b_dt, L0_attn_A, L0_attn_D, L0_attn_W_out,
           L0_ffn_sim_matrix, L0_ffn_gates, L0_ffn_q_proj, L0_ffn_k_proj, L0_ffn_v_proj, L0_ffn_o_proj):
    import numpy as np
    import concourse.bacc as bacc
    from concourse.bass_utils import run_bass_kernel_spmd

    given = (x, L0_tok_log_dt, L0_tok_log_w_real, L0_tok_w_imag, L0_attn_norm_w, L0_attn_W_in, L0_attn_conv_w,
             L0_attn_conv_b, L0_attn_W_x, L0_attn_W_dt, L0_attn_b_dt, L0_attn_A, L0_attn_D, L0_attn_W_out,
             L0_ffn_sim_matrix, L0_ffn_gates, L0_ffn_q_proj, L0_ffn_k_proj, L0_ffn_v_proj, L0_ffn_o_proj)
    laid = _layout(*(np.asarray(v) for v in given))
    nc = bacc.Bacc("TRN2", target_bir_lowering=False, num_devices=1)
    arrays, io = {}, {}
    for name, v in laid.items():
        v = np.ascontiguousarray(v)
        arrays[f"in_{name}"] = v
        io[name] = nc.dram_tensor(f"in_{name}", v.shape, mybir.dt.from_np(v.dtype), kind="ExternalInput").ap()
    ch, h = x.shape[0], x.shape[1]
    width = L0_ffn_q_proj.shape[1]
    out = nc.dram_tensor("out_0", (ch, h, width), F32, kind="ExternalOutput").ap()
    program(nc, io, out)
    result = run_bass_kernel_spmd(nc, [arrays], core_ids=[0])
    return result.results[0]["out_0"]
```

```python
import math
from contextlib import ExitStack

import concourse.bass as bass
from concourse import mybir

P = 128
F32 = mybir.dt.float32
F32R = mybir.dt.float32r
I32 = mybir.dt.int32
ALU = mybir.AluOpType
ACT = mybir.ActivationFunctionType
AX = mybir.AxisListType

MAGIC = 1.5 * 2 ** 23
LOG2E = 1.0 / math.log(2.0)
LN2_HI = 0.693359375
LN2_LO = math.log(2.0) - LN2_HI
TWO_PI = 2 * math.pi
TWO_PI_HI = 6.28125
TWO_PI_LO = TWO_PI - TWO_PI_HI
PI_IN = 3.1415925
EPS = 1e-5
START = 1


def token_stage(nc, io, h0_scratch):
    H, N = io["w_imag"].shape[1] * 2, 64
    Q = H // 2
    CH = io["xT"].shape[1] // (2 * Q)
    LEN = h0_scratch.shape[2]
    L0 = P
    L1 = LEN // L0
    LT = L0 + L1
    QC = 16
    CHUNKS = Q // QC
    QB = 512 // L0
    BANKS = QC // QB

    with ExitStack() as ctx:
        def sb(name, shape, dt=F32):
            return ctx.enter_context(nc.sbuf_tensor(name, shape, dt))

        def sem(name):
            return ctx.enter_context(nc.semaphore(name))

        coef = sb("tk_coef", [P, 2, CH, Q])
        prod = sb("tk_prod", [P, 4, CH, Q])
        logs = sb("tk_logs", [P, 2, Q])
        w_im = sb("tk_w_im", [P, Q])
        exps = sb("tk_exps", [P, 2, Q])
        w_re = sb("tk_w_re", [P, Q])
        a = sb("tk_a", [P, Q])
        b = sb("tk_b", [P, Q])
        em1 = sb("tk_em1", [P, Q])
        t = [sb(f"tk_t{i}", [P, 2, Q]) for i in range(5)]
        ti = sb("tk_ti", [P, 2, Q], I32)
        g = sb("tk_g", [P, 2, Q])
        pos_i = sb("tk_pos_i", [P, LT], I32)
        pos = sb("tk_pos", [P, LT])
        phase = sb("tk_phase", [P, 2, QC, LT])
        turns = sb("tk_turns", [P, QC, LT])
        decay = sb("tk_decay", [P, 2, QC, LT])
        nsin = sb("tk_nsin", [P, 2, QC, LT])
        cosine = sb("tk_cosine", [P, 2, QC, LT])
        e_re = sb("tk_e_re", [P, 2, QC, LT])
        e_nim = sb("tk_e_nim", [P, 2, QC, LT])
        p_t = prod[:].rearrange("p i c q -> p i (c q)")[:, :, 0:QC * CH * L1]\
            .rearrange("p i (q c l) -> p i q c l", q=QC, c=CH)
        p_re = sb("tk_p_re", [P, 2, QC, CH, L1])
        p_im = sb("tk_p_im", [P, 2, QC, CH, L1])
        stage = sb("tk_stage", [P, 2, QC, L0])
        half_angle = sb("tk_half_angle", [P, Q])
        sine = sb("tk_sine", [P, Q])
        absolute = sb("tk_absolute", [P, Q])
        half_pi = sb("tk_half_pi", [P, 1])
        ps = ctx.enter_context(nc.psum_tensor("tk_ps", [P, 8, 512], F32))

        loaded = sem("tk_loaded")
        positions = sem("tk_positions")
        angle_ready = sem("tk_angle_ready")
        trig_ready = sem("tk_trig_ready")
        ab_ready = sem("tk_ab_ready")
        g_ready = sem("tk_g_ready")
        products_ready = sem("tk_products_ready")
        im_ready = sem("tk_im_ready")
        coef_ready = sem("tk_coef_ready")
        phase_ready = sem("tk_phase_ready")
        decay_arg = sem("tk_decay_arg")
        trig_step = sem("tk_trig_step")
        e_ready = sem("tk_e_ready")
        p_im_step = sem("tk_p_im_step")
        p_re_ready = sem("tk_p_re_ready")
        sums_ready = sem("tk_sums_ready")
        staged = sem("tk_staged")
        stored = [sem(f"tk_stored{i}") for i in range(2)]
        dve_step = sem("tk_dve_step")
        pe_idle = sem("tk_pe_idle")

        def bq(x):
            return x.unsqueeze(1).broadcast_to([P, CH, Q])

        block = ctx.enter_context(nc.Block())

        @block.sync
        def _(sp):
            sp.dma_start(logs[0:64, 0, :], io["log_dt"][0:1, :].partition_broadcast(64)).then_inc(loaded, 16)
            sp.dma_start(logs[64:P, 0, :], io["log_dt"][1:2, :].partition_broadcast(64)).then_inc(loaded, 16)
            sp.dma_start(logs[:, 1, :], io["log_w_real"]).then_inc(loaded, 16)
            sp.dma_start(w_im[:], io["w_imag"]).then_inc(loaded, 16)
            sp.dma_start(coef[:].rearrange("p r c q -> p (r c q)"), io["xT"]).then_inc(loaded, 16)
            h0_v = h0_scratch.rearrange("c (q two) (l1 l0) -> two c l1 q l0", two=2, l0=L0)

            def store(k, slot):
                sp.wait_ge(staged, BANKS * (k + 1))
                for h2 in range(2):
                    for c in range(CH):
                        pt = 64 * h2 + L1 * c
                        sp.dma_start(h0_v[h2, c, :, bass.ds(k * QC, QC), :],
                                     stage[pt:pt + L1, slot, :, :]).then_inc(stored[slot], 16)

            with sp.Fori(0, CHUNKS // 2) as pair:
                for slot in range(2):
                    store(pair * 2 + slot, slot)
            for slot in range(2):
                sp.wait_ge(stored[slot], 16 * CH * CHUNKS)

        @block.gpsimd
        def _(pool):
            nc.gpsimd.iota(pos_i[:, 0:L0], pattern=[[1, L0]], base=0, channel_multiplier=0).then_inc(positions, 1)
            nc.gpsimd.iota(pos_i[:, L0:LT], pattern=[[L0, L1]], base=0, channel_multiplier=0).then_inc(positions, 1)
            nc.gpsimd.memset(half_pi[:], math.pi / 2).then_inc(positions, 1)
            pool.wait_ge(positions, 3)
            nc.gpsimd.tensor_copy(pos[:], pos_i[:]).then_inc(positions, 1)

            def decay_argument(k, slot):
                if not isinstance(k, int) or k >= 2:
                    pool.wait_ge(e_ready, 2 * k - 2)
                nc.gpsimd.tensor_tensor(decay[:, slot], a[:, bass.ds(k * QC, QC)].unsqueeze(2).broadcast_to([P, QC, LT]),
                                        pos[:].unsqueeze(1).broadcast_to([P, QC, LT]),
                                        ALU.mult).then_inc(decay_arg, 1)

            def imaginary_p(k, slot):
                qs = bass.ds(k * QC, QC)
                pool.wait_ge(e_ready, 2 * k + 2)
                if not isinstance(k, int) or k >= 2:
                    pool.wait_ge(sums_ready, k - 1)
                c_re = coef[:, 0, :, qs].rearrange("p c q -> p q c").unsqueeze(3).broadcast_to([P, QC, CH, L1])
                c_im = coef[:, 1, :, qs].rearrange("p c q -> p q c").unsqueeze(3).broadcast_to([P, QC, CH, L1])
                er = e_re[:, slot, :, L0:LT].unsqueeze(2).broadcast_to([P, QC, CH, L1])
                ei = e_nim[:, slot, :, L0:LT].unsqueeze(2).broadcast_to([P, QC, CH, L1])
                nc.gpsimd.tensor_tensor(p_t[:, 2], c_im, er, ALU.mult).then_inc(p_im_step, 1)
                nc.gpsimd.tensor_tensor(p_t[:, 3], c_re, ei, ALU.mult).then_inc(p_im_step, 1)
                pool.wait_ge(p_im_step, 3 * k + 2)
                nc.gpsimd.tensor_tensor(p_im[:, slot], p_t[:, 2], p_t[:, 3], ALU.subtract).then_inc(p_im_step, 1)
                pool.wait_ge(p_im_step, 3 * k + 3)

            pool.wait_ge(positions, 4)
            pool.wait_ge(ab_ready, 1)
            decay_argument(0, 0)
            pool.wait_ge(g_ready, 1)
            nc.gpsimd.tensor_tensor(prod[:, 2], coef[:, 0], bq(g[:, 1]), ALU.mult).then_inc(im_ready, 1)
            nc.gpsimd.tensor_tensor(prod[:, 3], coef[:, 1], bq(g[:, 0]), ALU.mult).then_inc(im_ready, 1)
            pool.wait_ge(im_ready, 2)
            pool.wait_ge(products_ready, 1)
            nc.gpsimd.tensor_tensor(coef[:, 1], prod[:, 2], prod[:, 3], ALU.add).then_inc(im_ready, 1)
            pool.wait_ge(im_ready, 3)
            decay_argument(1, 1)
            pool.wait_ge(coef_ready, 1)
            imaginary_p(0, 0)
            with pool.Fori(1, CHUNKS // 2) as pair:
                decay_argument(pair * 2, 0)
                imaginary_p(pair * 2 - 1, 1)
                decay_argument(pair * 2 + 1, 1)
                imaginary_p(pair * 2, 0)
            imaginary_p(CHUNKS - 1, 1)

        @block.scalar
        def _(act):
            act.wait_ge(positions, 3)
            act.wait_ge(angle_ready, 1)
            nc.scalar.activation(sine[:], half_angle[:], ACT.Sin).then_inc(trig_ready, 1)
            nc.scalar.activation(absolute[:], half_angle[:], ACT.Abs).then_inc(trig_ready, 1)
            act.wait_ge(trig_ready, 2)
            nc.scalar.activation(t[3][:, 0], absolute[:], ACT.Sin, bias=half_pi[:], scale=-1.0).then_inc(trig_ready, 1)

            def trigs(k, slot):
                act.wait_ge(phase_ready, k + 1)
                if not isinstance(k, int) or k >= 2:
                    act.wait_ge(e_ready, 2 * k - 2)
                nc.scalar.activation(nsin[:, slot], phase[:, slot], ACT.Sin, scale=-1.0).then_inc(trig_step, 1)
                nc.scalar.activation(cosine[:, slot], phase[:, slot], ACT.Abs).then_inc(trig_step, 1)
                act.wait_ge(trig_step, 4 * k + 2)
                nc.scalar.activation(cosine[:, slot], cosine[:, slot], ACT.Sin, bias=half_pi[:], scale=-1.0)\
                    .then_inc(trig_step, 1)
                act.wait_ge(decay_arg, k + 1)
                nc.scalar.activation(decay[:, slot], decay[:, slot], ACT.Exp).then_inc(trig_step, 1)

            def copy_out(k, slot):
                act.wait_ge(sums_ready, k + 1)
                if not isinstance(k, int) or k >= 2:
                    act.wait_ge(stored[slot], 16 * CH * (k - slot))
                for qb in range(BANKS):
                    nc.scalar.activation(stage[:, slot, QB * qb:QB * qb + QB, :],
                                         ps[:, BANKS * slot + qb, :].rearrange("p (q l) -> p q l", q=QB),
                                         ACT.Copy).then_inc(staged, 1)

            trigs(0, 0)
            trigs(1, 1)
            copy_out(0, 0)
            with act.Fori(1, CHUNKS // 2) as pair:
                trigs(pair * 2, 0)
                copy_out(pair * 2 - 1, 1)
                trigs(pair * 2 + 1, 1)
                copy_out(pair * 2, 0)
            copy_out(CHUNKS - 1, 1)

        @block.vector
        def _(dve):
            count = [0]

            def link(ins):
                count[0] += 1
                ins.then_inc(dve_step, 1)
                dve.wait_ge(dve_step, count[0])

            V = nc.vector

            def exp_parts(x, k, r, q, two_k):
                link(V.tensor_scalar(k, x, LOG2E, MAGIC, ALU.mult, ALU.add))
                link(V.tensor_scalar(k, k, MAGIC, None, ALU.subtract))
                link(V.tensor_scalar(k, k, -126.0, 127.0, ALU.max, ALU.min))
                link(V.scalar_tensor_tensor(r, k, -LN2_HI, x, ALU.mult, ALU.add))
                link(V.scalar_tensor_tensor(r, k, -LN2_LO, r, ALU.mult, ALU.add))
                link(V.tensor_scalar(q, r, 1.0 / math.factorial(8), None, ALU.mult))
                for n in range(7, 0, -1):
                    link(V.scalar_tensor_tensor(q, q, 1.0 / math.factorial(n), r, ALU.add, ALU.mult))
                link(V.tensor_scalar(two_k, k, 127.0, float(1 << 23), ALU.add, ALU.mult))

            def phases(k, slot, link):
                ph = phase[:, slot]
                link(V.tensor_tensor(ph, b[:, bass.ds(k * QC, QC)].unsqueeze(2).broadcast_to([P, QC, LT]),
                                     pos[:].unsqueeze(1).broadcast_to([P, QC, LT]), ALU.mult))
                link(V.tensor_scalar(turns[:], ph, 1 / TWO_PI, MAGIC, ALU.mult, ALU.add))
                link(V.tensor_scalar(turns[:], turns[:], MAGIC, None, ALU.subtract))
                link(V.scalar_tensor_tensor(ph, turns[:], -TWO_PI_HI, ph, ALU.mult, ALU.add))
                link(V.scalar_tensor_tensor(ph, turns[:], -TWO_PI_LO, ph, ALU.mult, ALU.add))
                link(V.tensor_scalar(ph, ph, -PI_IN, PI_IN, ALU.max, ALU.min))
                dve.sem_inc(phase_ready, 1)

            dve.wait_ge(loaded, 16 * 5)
            exp_parts(logs[:], t[0][:], t[1][:], t[2][:], ti[:])
            two_k = ti[:].bitcast(F32)
            link(V.tensor_tensor(t[2][:], t[2][:], two_k, ALU.mult))
            link(V.tensor_tensor(exps[:], t[2][:], two_k, ALU.add))
            link(V.scalar_tensor_tensor(a[:], exps[:, 1], -1.0, exps[:, 0], ALU.mult, ALU.mult))
            link(V.tensor_scalar(w_re[:], exps[:, 1], -1.0, None, ALU.mult))
            link(V.tensor_tensor(b[:], w_im[:], exps[:, 0], ALU.mult))
            dve.sem_inc(ab_ready, 1)
            link(V.tensor_scalar(half_angle[:], b[:], 0.5, None, ALU.mult))
            link(V.tensor_scalar(t[4][:, 0], half_angle[:], 1 / TWO_PI, MAGIC, ALU.mult, ALU.add))
            link(V.tensor_scalar(t[4][:, 0], t[4][:, 0], MAGIC, None, ALU.subtract))
            link(V.scalar_tensor_tensor(half_angle[:], t[4][:, 0], -TWO_PI_HI, half_angle[:], ALU.mult, ALU.add))
            link(V.scalar_tensor_tensor(half_angle[:], t[4][:, 0], -TWO_PI_LO, half_angle[:], ALU.mult, ALU.add))
            link(V.tensor_scalar(half_angle[:], half_angle[:], -PI_IN, PI_IN, ALU.max, ALU.min))
            dve.sem_inc(angle_ready, 1)
            dve.wait_ge(positions, 4)
            phases(0, 0, link)
            exp_parts(a[:], t[0][:, 0], t[1][:, 0], t[2][:, 0], ti[:, 0])
            two_k = ti[:, 0].bitcast(F32)
            link(V.tensor_tensor(t[2][:, 0], t[2][:, 0], two_k, ALU.mult))
            link(V.scalar_tensor_tensor(em1[:], two_k, -1.0, t[2][:, 0], ALU.add, ALU.add))
            link(V.tensor_tensor(t[4][:, 0], w_re[:], w_re[:], ALU.mult))
            link(V.tensor_tensor(t[4][:, 1], w_im[:], w_im[:], ALU.mult))
            link(V.tensor_tensor(t[4][:, 0], t[4][:, 0], t[4][:, 1], ALU.add))
            link(V.reciprocal(t[4][:, 1], t[4][:, 0]))
            link(V.tensor_scalar(t[4][:, 1], t[4][:, 1], 2.0, None, ALU.mult))
            inv = t[4][:, 1]
            dve.wait_ge(trig_ready, 3)
            s, c = sine[:], t[3][:, 0]
            u, er, ei = t[4][:, 0], t[0][:, 1], t[1][:, 1]
            link(V.scalar_tensor_tensor(u, s, -2.0, s, ALU.mult, ALU.mult))
            link(V.scalar_tensor_tensor(er, em1[:], 1.0, u, ALU.add, ALU.mult))
            link(V.tensor_tensor(er, er, em1[:], ALU.add))
            link(V.scalar_tensor_tensor(u, s, 2.0, c, ALU.mult, ALU.mult))
            link(V.scalar_tensor_tensor(ei, em1[:], 1.0, u, ALU.add, ALU.mult))
            x1, x2 = t[2][:, 0], t[2][:, 1]
            link(V.tensor_tensor(x1, er, w_re[:], ALU.mult))
            link(V.tensor_tensor(x2, ei, w_im[:], ALU.mult))
            link(V.tensor_tensor(x1, x1, x2, ALU.add))
            link(V.tensor_tensor(g[:, 0], x1, inv, ALU.mult))
            link(V.tensor_tensor(x1, ei, w_re[:], ALU.mult))
            link(V.tensor_tensor(x2, er, w_im[:], ALU.mult))
            link(V.tensor_tensor(x1, x1, x2, ALU.subtract))
            link(V.tensor_tensor(g[:, 1], x1, inv, ALU.mult))
            dve.sem_inc(g_ready, 1)
            link(V.tensor_tensor(prod[:, 0], coef[:, 0], bq(g[:, 0]), ALU.mult))
            link(V.tensor_tensor(prod[:, 1], coef[:, 1], bq(g[:, 1]), ALU.mult))
            dve.wait_ge(im_ready, 2)
            V.tensor_tensor(coef[:, 0], prod[:, 0], prod[:, 1], ALU.subtract).then_inc(coef_ready, 1)
            dve.sem_inc(products_ready, 1)
            dve.wait_ge(coef_ready, 1)
            dve.wait_ge(im_ready, 3)
            PHASE_STEPS, STEPS = 6, 9
            setup = count[0] - PHASE_STEPS

            def chunk_link(k, local):
                def link(ins):
                    local[0] += 1
                    ins.then_inc(dve_step, 1)
                    dve.wait_ge(dve_step, k * STEPS + (setup + PHASE_STEPS + local[0]))
                return link

            def middle(k, slot, link):
                dve.wait_ge(trig_step, 4 * k + 4)
                if not isinstance(k, int) or k >= 2:
                    dve.wait_ge(sums_ready, k - 1)
                V.tensor_tensor(e_re[:, slot], cosine[:, slot], decay[:, slot], ALU.mult).then_inc(e_ready, 1)
                V.tensor_tensor(e_nim[:, slot], nsin[:, slot], decay[:, slot], ALU.mult).then_inc(e_ready, 1)
                dve.wait_ge(e_ready, 2 * k + 2)
                qs = bass.ds(k * QC, QC)
                c_re = coef[:, 0, :, qs].rearrange("p c q -> p q c").unsqueeze(3).broadcast_to([P, QC, CH, L1])
                c_im = coef[:, 1, :, qs].rearrange("p c q -> p q c").unsqueeze(3).broadcast_to([P, QC, CH, L1])
                er = e_re[:, slot, :, L0:LT].unsqueeze(2).broadcast_to([P, QC, CH, L1])
                ei = e_nim[:, slot, :, L0:LT].unsqueeze(2).broadcast_to([P, QC, CH, L1])
                link(V.tensor_tensor(p_t[:, 0], c_re, er, ALU.mult))
                link(V.tensor_tensor(p_t[:, 1], c_im, ei, ALU.mult))
                link(V.tensor_tensor(p_re[:, slot], p_t[:, 0], p_t[:, 1], ALU.add))
                dve.sem_inc(p_re_ready, 1)

            def step(k, slot):
                link = chunk_link(k, [0])
                dve.wait_ge(trig_step, 4 * k)
                phases(k + 1, 1 - slot, link)
                middle(k, slot, link)

            link0 = chunk_link(0, [0])
            phases(1, 1, link0)
            middle(0, 0, link0)
            with dve.Fori(1, CHUNKS // 2) as pair:
                step(pair * 2 - 1, 1)
                step(pair * 2, 0)
            middle(CHUNKS - 1, 1, chunk_link(CHUNKS - 1, [0]))

        @block.tensor
        def _(pe):
            def sums(k, slot):
                pe.wait_ge(p_re_ready, k + 1)
                pe.wait_ge(p_im_step, 3 * k + 3)
                if not isinstance(k, int) or k >= 2:
                    pe.wait_ge(staged, BANKS * (k - 1))
                    pe.sem_inc(pe_idle, 1)
                for q in range(QC):
                    for part, (lhs, rhs) in enumerate(((p_re, e_re), (p_im, e_nim))):
                        for h2 in range(2):
                            rows = slice(64 * h2, 64 * h2 + 64)
                            last = nc.tensor.matmul(
                                ps[rows, BANKS * slot + q // QB, q % QB * L0:(q % QB + 1) * L0],
                                lhs[rows, slot, q].rearrange("p c l -> p (c l)"), rhs[rows, slot, q, 0:L0],
                                start=(part == 0), stop=(part == 1))
                last.then_inc(sums_ready, 1)

            for slot in range(2):
                sums(slot, slot)
            with pe.Fori(1, CHUNKS // 2) as pair:
                for slot in range(2):
                    sums(pair * 2 + slot, slot)


def mamba_stage(nc, io, h0_scratch, b_scratch, h1_scratch):
    BATCH, T, D = h0_scratch.shape
    KC = D // P
    TJ = T // P
    ED = io["w_in"].shape[1] // KC // 2
    DI = ED // P
    NS = io["a"].shape[1] // DI
    R = P
    WX = R + 2 * NS
    TAPS = io["conv_w"].shape[1] // DI
    HALF = DI // 2
    STEPS = 2 * NS
    SW = HALF * T
    BG = 4
    FILLS = 16
    DA_SLOTS = 4
    B0 = P - 2 * NS

    with ExitStack() as ctx:
        def sb(name, shape, dt=F32):
            return ctx.enter_context(nc.sbuf_tensor(name, shape, dt))

        def sem(name):
            return ctx.enter_context(nc.semaphore(name))

        w_in = sb("ma_w_in", [P, KC, 2 * ED])
        w_x = sb("ma_w_x", [P, DI, WX])
        w_dt = sb("ma_w_dt", [P, ED])
        w_out = sb("ma_w_out", [P, DI, D])
        norm_w = sb("ma_norm_w", [P, KC])
        conv_w = sb("ma_conv_w", [P, DI, TAPS])
        conv_b = sb("ma_conv_b", [P, DI])
        b_dt = sb("ma_b_dt", [P, DI])
        a_w = sb("ma_a", [P, DI, NS])
        d_w = sb("ma_d", [P, DI])
        ident = sb("ma_ident", [P, P])
        minus_half = sb("ma_minus_half", [P, TJ])
        minus_one = sb("ma_minus_one", [P, TJ])
        one = sb("ma_one", [P, TJ])
        eps = sb("ma_eps", [P, TJ])

        hin = sb("ma_hin", [P, TJ, D])
        stats = sb("ma_stats", [P, TJ, 6])
        mv = sb("ma_mv", [P, TJ, 2])
        ln = sb("ma_ln", [P, 8, TJ])
        res = sb("ma_res", [P, 2, TJ, D])
        u_t = sb("ma_u_t", [P, KC, T])
        xc = sb("ma_xc", [P, DI, TAPS - 1 + T])
        gate = sb("ma_gate", [P, 2, DI, T])
        t1 = sb("ma_t1", [P, DI, T])
        t2 = sb("ma_t2", [P, DI, T])
        u = t1[:].rearrange("p i t -> p (i t)")[:, 0:TJ * D].rearrange("p (j d) -> p j d", j=TJ)
        xs = sb("ma_xs", [P, 2, DI, T])
        dt_lr = sb("ma_dt_lr", [P, T])
        bc_t = sb("ma_bc_t", [P, T])
        c_tok = sb("ma_c_tok", [P, 2, TJ, NS])
        dt = sb("ma_dt", [P, DI, T])
        dtx = sb("ma_dtx", [P, DI, T])
        b_all = sb("ma_b_all", [P, 2, BG, T])
        da = sb("ma_da", [P, DA_SLOTS, HALF, T])
        dbx = sb("ma_dbx", [P, 2, HALF, T])
        hs = sb("ma_hs", [P, 2, HALF, T])
        y = sb("ma_y", [P, TJ, ED])
        yg = sb("ma_yg", [P, DI, T])
        ps_h = ctx.enter_context(nc.psum_tensor("ma_ps_h", [P, 2, TJ, 512], F32))
        ps_p = ctx.enter_context(nc.psum_tensor("ma_ps_p", [P, 4, 512], F32))

        small = sem("ma_small")
        w_in_loaded = sem("ma_w_in_loaded")
        weights = sem("ma_weights")
        consts = sem("ma_consts")
        hin_loaded = sem("ma_hin_loaded")
        stats_step = sem("ma_stats_step")
        ln_step = sem("ma_ln_step")
        u_ready = sem("ma_u_ready")
        res_ready = sem("ma_res_ready")
        filled = sem("ma_filled")
        emptied = sem("ma_emptied")
        conv_step = sem("ma_conv_step")
        first_step = sem("ma_first_step")
        c_turned = sem("ma_c_turned")
        act_idle = sem("ma_act_idle")
        dve_idle = sem("ma_dve_idle")
        sp_idle = sem("ma_sp_idle")
        xs_ready = sem("ma_xs_ready")
        dtlr_ready = sem("ma_dtlr_ready")
        c_ready = sem("ma_c_ready")
        b_stored = sem("ma_b_stored")
        b_loaded = [sem(f"ma_b_loaded{i}") for i in range(2)]
        soft_arg = sem("ma_soft_arg")
        soft_log = sem("ma_soft_log")
        soft_corr = sem("ma_soft_corr")
        soft_step = sem("ma_soft_step")
        dt_ready = sem("ma_dt_ready")
        da_ready = sem("ma_da_ready")
        dbx_ready = sem("ma_dbx_ready")
        scanned = sem("ma_scanned")
        turned = sem("ma_turned")
        started = sem("ma_started")
        summed = sem("ma_summed")
        y_turned = sem("ma_y_turned")
        gated = sem("ma_gated")
        out_ready = sem("ma_out_ready")
        h1_ready = sem("ma_h1_ready")
        h1_stored = sem("ma_h1_stored")

        LOADS = 3
        SMALL = 6
        LN_OPS = 9
        CONV_OPS = 2 * TAPS - 1
        PROJECT = (0, 3, 7, 11)
        SUMS = STEPS - 2
        PRIME = DA_SLOTS

        block = ctx.enter_context(nc.Block())

        @block.sync
        def _(sp):
            def load(dst, name, signal):
                flat = dst[:] if len(dst.shape) == 2 else dst[:].rearrange("p a b -> p (a b)")
                sp.dma_start(flat, io[name]).then_inc(signal, 16)

            def load_hin(m):
                row = bass.ds(m % BATCH if isinstance(m, int) else sp.snap(m % BATCH), 1)
                if not isinstance(m, int) or m:
                    sp.wait_ge(res_ready, TJ * m)
                    sp.sem_inc(sp_idle, 1)
                sp.dma_start(hin[:], h0_scratch[row].rearrange("o (j p) d -> (o p) j d", p=P))\
                    .then_inc(hin_loaded, 16)

            def store_b(m):
                sp.wait_ge(emptied, FILLS * m + 12)
                sp.dma_start(b_scratch, bc_t[B0:B0 + NS, :]).then_inc(b_stored, 16)
                sp.wait_ge(b_stored, 16 * (m + 1))
                sp.sem_inc(sp_idle, 1)

            def load_b(m, g):
                if g:
                    sp.wait_ge(scanned, STEPS * m + 2 * BG * (g - 1) + PRIME)
                sp.dma_start(b_all[:, g % 2].rearrange("p n t -> p (n t)"),
                             b_scratch[g * BG:(g + 1) * BG, :].rearrange("n t -> (n t)").unsqueeze(0)
                             .partition_broadcast(P)).then_inc(b_loaded[g % 2], 16)

            load_hin(0)
            for dst, name in ((norm_w, "norm_w"), (conv_w, "conv_w"), (conv_b, "conv_b"), (b_dt, "b_dt"), (a_w, "a"),
                              (d_w, "d")):
                load(dst, name, small)
            load(w_in, "w_in", w_in_loaded)
            load(w_x, "w_x", weights)
            load(w_dt, "w_dt", weights)
            load(w_out, "w_out", weights)
            load_hin(1)
            store_b(0)
            load_b(0, 0)
            load_b(0, 1)
            with sp.Fori(0, BATCH) as b:
                sp.wait_ge(h1_ready, TJ * (b + 1))
                sp.dma_start(h1_scratch[bass.ds(b, 1)].rearrange("o (j p) d -> (o p) j d", p=P),
                             res[:, bass.ds((b + 1) % 2, 1)].rearrange("p o j d -> p (o j) d")).then_inc(h1_stored, 16)
                load_b(b, 2)
                load_hin(b + 2)
                load_b(b, 3)
                sp.wait_ge(b_loaded[0], 16 * (2 * b + 2))
                sp.wait_ge(b_loaded[1], 16 * (2 * b + 2))
                store_b(b + 1)
                sp.wait_ge(scanned, STEPS * b + 2 * BG * 3 + PRIME)
                load_b(b + 1, 0)
                load_b(b + 1, 1)
            sp.wait_ge(h1_ready, TJ * (BATCH + 1))
            sp.dma_start(h1_scratch[BATCH].rearrange("(j p) d -> p j d", p=P),
                         res[:, (BATCH + 1) % 2]).then_inc(h1_stored, 16)
            sp.wait_ge(h1_stored, 16 * (BATCH + 1))
            sp.wait_ge(b_stored, 16 * (BATCH + 1))
            sp.wait_ge(b_loaded[0], 16 * (2 * BATCH + 1))
            sp.wait_ge(b_loaded[1], 16 * (2 * BATCH + 1))

        @block.gpsimd
        def _(pool):
            G = nc.gpsimd
            G.memset(ident[:], 0.0).then_inc(consts, 1)
            G.memset(minus_half[:], -0.5).then_inc(consts, 1)
            G.memset(xc[:, :, 0:TAPS - 1], 0.0).then_inc(consts, 1)
            G.memset(da[:, :, :, 0:1], 0.0).then_inc(consts, 1)
            G.memset(yg[:], 0.0).then_inc(consts, 1)
            G.memset(res[:, 1], 0.0).then_inc(consts, 1)
            G.memset(minus_one[:], -1.0).then_inc(consts, 1)
            G.memset(one[:], 1.0).then_inc(consts, 1)
            G.memset(eps[:], EPS).then_inc(consts, 1)
            pool.wait_ge(consts, 9)
            G.affine_select(out=ident[:], in_=ident[:], compare_op=ALU.not_equal, fill=1.0, base=0,
                            pattern=[[-1, P]], channel_multiplier=1).then_inc(consts, 1)
            pool.wait_ge(consts, 10)
            pool.wait_ge(small, 16 * SMALL)

            def norm_scalars(m):
                n = [0]

                def link(ins):
                    n[0] += 1
                    ins.then_inc(ln_step, 1)
                    pool.wait_ge(ln_step, m * (LN_OPS + 1) + n[0])

                pool.wait_ge(stats_step, 2 * TJ * (m + 1))
                pool.wait_ge(res_ready, TJ * m)
                mean, var = mv[:, :, 0], mv[:, :, 1]
                link(G.tensor_tensor(ln[:, 0], var, eps[:], ALU.add))
                link(G.tensor_tensor(ln[:, 1], ln[:, 0], minus_half[:], ALU.pow))
                link(G.tensor_tensor(ln[:, 2], var, ln[:, 1], ALU.mult))
                link(G.tensor_tensor(ln[:, 3], ln[:, 2], ln[:, 1], ALU.mult))
                link(G.tensor_tensor(ln[:, 4], ln[:, 3], minus_half[:], ALU.pow))
                link(G.tensor_tensor(ln[:, 5], ln[:, 1], ln[:, 4], ALU.mult))
                link(G.tensor_tensor(ln[:, 6], mean, ln[:, 1], ALU.mult))
                link(G.tensor_tensor(ln[:, 6], ln[:, 6], minus_one[:], ALU.mult))
                link(G.tensor_tensor(ln[:, 0], ln[:, 1], one[:], ALU.add))
                G.tensor_tensor(ln[:, 7], ln[:, 6], ln[:, 4], ALU.mult).then_inc(ln_step, 1)
                assert n[0] == LN_OPS

            def convolve(m):
                pool.wait_ge(soft_step, m)
                for h in range(2):
                    ch = slice(h * HALF, (h + 1) * HALF)
                    pool.wait_ge(emptied, FILLS * m + 4 + 2 * h)
                    for k in range(TAPS):
                        w = conv_w[:, ch, k:k + 1].broadcast_to([P, HALF, T])
                        G.tensor_tensor((t2 if k else t1)[:, ch], xc[:, ch, k:k + T], w, ALU.mult).then_inc(conv_step, 1)
                        if k:
                            pool.wait_ge(conv_step, CONV_OPS * (2 * m + h) + 2 * k)
                            G.tensor_tensor(t1[:, ch], t1[:, ch], t2[:, ch], ALU.add).then_inc(conv_step, 1)
                            pool.wait_ge(conv_step, CONV_OPS * (2 * m + h) + 2 * k + 1)

            def soft_correction(m):
                pool.wait_ge(soft_log, 4 * (m + 1))
                G.tensor_tensor(t1[:], t1[:], yg[:], ALU.subtract).then_inc(soft_corr, 1)
                pool.wait_ge(soft_corr, 2 * m + 1)
                G.tensor_tensor(t1[:], t1[:], xc[:, :, TAPS - 1:], ALU.add).then_inc(soft_corr, 1)

            norm_scalars(0)
            soft_correction(0)
            norm_scalars(1)
            with pool.Fori(0, BATCH) as b:
                convolve(b + 1)
                soft_correction(b + 1)
                norm_scalars(b + 2)

        @block.scalar
        def _(act):
            A = nc.scalar
            act.wait_ge(small, 16 * SMALL)
            act.wait_ge(consts, 10)

            def settle():
                act.sem_inc(act_idle, 1)

            def prep_norm(m):
                act.wait_ge(ln_step, (LN_OPS + 1) * (m + 1))
                act.wait_ge(soft_step, m)
                for j in range(TJ):
                    A.activation(u[:, j], hin[:, j], ACT.Identity, scale=ln[:, 5, j:j + 1],
                                 bias=ln[:, 7, j:j + 1]).then_inc(u_ready, 1)

            def prep_u_t(m):
                for f in range(2):
                    act.wait_ge(filled, FILLS * m + f + 1)
                    for i in range(2):
                        kc = 2 * f + i
                        last = A.activation(u_t[:, kc], ps_p[:, f, i * T:(i + 1) * T], ACT.Copy, scale=norm_w[:, kc:kc + 1])
                    last.then_inc(emptied, 1)

            def prep_x(m, i):
                act.wait_ge(filled, FILLS * m + 3 + i)
                if i == 0:
                    act.wait_ge(soft_step, m)
                A.activation(xc[:, 2 * i:2 * i + 2, TAPS - 1:], ps_p[:, i % 2].rearrange("p (i t) -> p i t", i=2),
                             ACT.Copy).then_inc(emptied, 1)

            def prep_z(m, i):
                act.wait_ge(filled, FILLS * m + 7 + i)
                settle()
                A.activation(gate[:, bass.ds(m % 2, 1), 2 * i:2 * i + 2, :].rearrange("p o i t -> p (o i t)"),
                             ps_p[:, i % 2], ACT.Copy).then_inc(emptied, 1)

            def prep_res(m):
                act.wait_ge(h1_stored, 16 * m)
                act.wait_ge(u_ready, TJ * (m + 1))
                settle()
                for j in range(TJ):
                    A.activation(res[:, bass.ds(m % 2, 1), j, :].rearrange("p o d -> p (o d)"), hin[:, j], ACT.Identity,
                                 scale=ln[:, 0, j:j + 1], bias=ln[:, 6, j:j + 1]).then_inc(res_ready, 1)

            def prep_silu(m):
                act.wait_ge(emptied, FILLS * m + 10)
                act.wait_ge(conv_step, 2 * CONV_OPS * (m + 1))
                settle()
                g = gate[:, bass.ds(m % 2, 1)].rearrange("p o i t -> p (o i t)")
                A.activation(g, g, ACT.Silu).then_inc(xs_ready, 1)
                for i in range(DI):
                    A.activation(xs[:, bass.ds(m % 2, 1), i, :].rearrange("p o t -> p (o t)"), t1[:, i], ACT.Silu,
                                 bias=conv_b[:, i:i + 1]).then_inc(xs_ready, 1)

            def prep_bc(m):
                act.wait_ge(filled, FILLS * m + 11)
                A.activation(dt_lr[:], ps_p[:, 0, 0:T], ACT.Copy).then_inc(emptied, 1)
                act.wait_ge(filled, FILLS * m + 12)
                act.wait_ge(b_stored, 16 * m)
                A.activation(bc_t[:], ps_p[:, 1, 0:T], ACT.Copy).then_inc(emptied, 1)

            def prep_c(m):
                act.wait_ge(c_turned, m + 1)
                settle()
                A.activation(c_tok[:, bass.ds(m % 2, 1)].rearrange("p o j n -> p (o j) n"),
                             ps_p[:, 0, 0:TJ * P].rearrange("p (j r) -> p j r", j=TJ)[:, :, B0 + NS:],
                             ACT.Copy).then_inc(c_ready, 1)

            def prep_soft_arg(m, i):
                act.wait_ge(filled, FILLS * m + 13 + i)
                for k in range(2):
                    src = ps_p[:, i % 2, k * T:(k + 1) * T]
                    c = 2 * i + k
                    A.activation(t1[:, c], src, ACT.Abs, bias=b_dt[:, c:c + 1]).then_inc(soft_arg, 1)
                    ins = A.activation(t2[:, c], src, ACT.Relu, bias=b_dt[:, c:c + 1])
                    ins.then_inc(emptied if k else soft_arg, 1)

            def prep_soft_log(m):
                act.wait_ge(soft_arg, 12 * (m + 1))
                A.activation(t1[:], t1[:], ACT.Exp, scale=-1.0).then_inc(soft_log, 1)
                act.wait_ge(soft_log, 4 * m + 1)
                A.activation(xc[:, :, TAPS - 1:], t1[:], ACT.Ln, bias=1.0).then_inc(soft_log, 1)
                if not isinstance(m, int):
                    act.wait_ge(out_ready, TJ * m)
                A.activation(yg[:], t1[:], ACT.Identity, bias=1.0).then_inc(soft_log, 1)
                act.wait_ge(soft_log, 4 * m + 3)
                A.activation(yg[:], yg[:], ACT.Identity, bias=minus_one[:, 0:1]).then_inc(soft_log, 1)

            def exps(b, s):
                n, half = s // 2, s % 2
                act.wait_ge(scanned, STEPS * b + s + PRIME - DA_SLOTS + 1)
                if s == 0:
                    act.wait_ge(dt_ready, 2 * b + 1)
                for i in range(HALF):
                    c = half * HALF + i
                    A.activation(da[:, s % DA_SLOTS, i, 1:T], dt[:, c, 1:T], ACT.Exp, scale=a_w[:, c, n:n + 1]).then_inc(da_ready, 1)

            def start_sum(b, s):
                for j in range(TJ):
                    act.wait_ge(turned, TJ * (STEPS * b + s) + j + 1)
                    if s == 0 and j == 0:
                        act.wait_ge(y_turned, 4 * b + START)
                    act.wait_ge(c_ready, b + 1)
                    settle()
                    A.activation(y[:, j, s * SW // TJ:(s + 1) * SW // TJ], ps_h[:, s, j], ACT.Copy,
                                 scale=c_tok[:, bass.ds(b % 2, 1), j, 0:1].rearrange("p o n -> p (o n)"))\
                        .then_inc(started, 1)

            pieces = {1: [prep_norm], 3: [prep_u_t], 18: [prep_res], 20: [prep_silu], 24: [prep_bc], 26: [prep_c],
                      30: [prep_soft_log]}
            for i in range(4):
                pieces.setdefault((5, 7, 9, 11)[i], []).append(lambda m, i=i: prep_x(m, i))
                pieces.setdefault((13, 15, 17, 19)[i], []).append(lambda m, i=i: prep_z(m, i))
                pieces.setdefault(27 + i // 2 * 2, []).append(lambda m, i=i: prep_soft_arg(m, i))
            for s in sorted(pieces):
                for piece in pieces[s]:
                    piece(0)
            with act.Fori(0, BATCH) as b:
                for s in range(STEPS):
                    exps(b, s)
                    if s in (3, 4):
                        start_sum(b, s - 3)
                    for piece in pieces.get(s, []):
                        piece(b + 1)

        @block.vector
        def _(dve):
            V = nc.vector
            dve.sem_inc(scanned, PRIME)
            dve.wait_ge(small, 16 * SMALL)
            dve.wait_ge(consts, 10)

            def prep_stats(m):
                dve.wait_ge(hin_loaded, 16 * (m + 1))
                dve.wait_ge(ln_step, (LN_OPS + 1) * m)
                for j in range(TJ):
                    V.bn_stats(stats[:, j], hin[:, j]).then_inc(stats_step, 1)
                dve.wait_ge(stats_step, 2 * TJ * m + TJ)
                dve.sem_inc(dve_idle, 1)
                for j in range(TJ):
                    V.bn_aggr(mv[:, j], stats[:, j]).then_inc(stats_step, 1)

            def step_size(m):
                dve.wait_ge(soft_corr, 2 * (m + 1))
                V.tensor_tensor(dt[:], t2[:], t1[:], ALU.add).then_inc(dt_ready, 1)

            def weigh_input(m):
                dve.wait_ge(xs_ready, (DI + 1) * (m + 1))
                dve.wait_ge(dt_ready, 2 * m + 1)
                dve.sem_inc(soft_step, 1)
                V.tensor_tensor(dtx[:], dt[:], xs[:, bass.ds(m % 2, 1)].rearrange("p o i t -> p (o i) t"),
                                ALU.mult).then_inc(dt_ready, 1)

            def drive(b, s):
                n, half = s // 2, s % 2
                if s == 0:
                    dve.wait_ge(dt_ready, 2 * b + 2)
                if s % (2 * BG) == 0:
                    g = s // (2 * BG)
                    dve.wait_ge(b_loaded[g % 2], 16 * (2 * b + g // 2 + 1))
                dve.wait_ge(scanned, STEPS * b + s + PRIME - 1)
                V.tensor_tensor(dbx[:, s % 2], dtx[:, half * HALF:(half + 1) * HALF],
                                b_all[:, n // BG % 2, n % BG].unsqueeze(1).broadcast_to([P, HALF, T]),
                                ALU.mult).then_inc(dbx_ready, 1)

            def scan(b, s):
                dve.wait_ge(dbx_ready, STEPS * b + s + 1)
                dve.wait_ge(da_ready, HALF * (STEPS * b + s + 1))
                if s >= 2:
                    dve.wait_ge(turned, TJ * (STEPS * b + s - 1))
                V.tensor_tensor_scan(hs[:, s % 2].rearrange("p i t -> p (i t)"), da[:, s % DA_SLOTS].rearrange("p i t -> p (i t)"),
                                     dbx[:, s % 2].rearrange("p i t -> p (i t)"), 0.0, ALU.mult, ALU.add)\
                    .then_inc(scanned, 1)

            def weigh(b, s, j):
                n, half = s // 2, s % 2
                if n == 0:
                    return
                dve.wait_ge(turned, TJ * (STEPS * b + s) + j + 1)
                out = y[:, j, half * SW // TJ:(half + 1) * SW // TJ]
                c = c_tok[:, bass.ds(b % 2, 1), j, n:n + 1].rearrange("p o n -> p (o n)")
                if n == 1:
                    dve.wait_ge(started, TJ * (2 * b + s - 2) + j + 1)
                else:
                    dve.wait_ge(summed, TJ * (SUMS * b + s - 4) + j + 1)
                V.scalar_tensor_tensor(out, ps_h[:, s % 2, j], c, out, ALU.mult, ALU.add).then_inc(summed, 1)

            def gate_y(b):
                for i in range(DI):
                    if i % 2 == 0:
                        dve.wait_ge(y_turned, 4 * b + i // 2 + 1 + START)
                    if i == 0:
                        dve.wait_ge(out_ready, TJ * (b + 1))
                    V.scalar_tensor_tensor(yg[:, i], xs[:, bass.ds(b % 2, 1), i, :].rearrange("p o t -> p (o t)"),
                                           d_w[:, i:i + 1], ps_p[:, i // 2, i % 2 * T:(i % 2 + 1) * T],
                                           ALU.mult, ALU.add).then_inc(gated, 1)
                dve.wait_ge(gated, (DI + 1) * b + DI + START)
                V.tensor_tensor(yg[:], yg[:], gate[:, bass.ds(b % 2, 1)].rearrange("p o i t -> p (o i) t"),
                                ALU.mult).then_inc(gated, 1)

            def add_res(b, j):
                dve.wait_ge(out_ready, TJ * b + j + 1)
                r = res[:, bass.ds((b + 1) % 2, 1), j, :].rearrange("p o d -> p (o d)")
                V.tensor_tensor(r, ps_p[:, 2 + j], r, ALU.add).then_inc(h1_ready, 1)

            def first_convolve():
                n = 0
                for i in range(DI):
                    if i % 2 == 0:
                        dve.wait_ge(emptied, 3 + i // 2)
                    V.tensor_scalar(t1[:, i], xc[:, i, 0:T], conv_w[:, i, 0:1], None, ALU.mult).then_inc(first_step, 1)
                    for k in range(1, TAPS):
                        n += 1
                        dve.wait_ge(first_step, n)
                        V.scalar_tensor_tensor(t1[:, i], xc[:, i, k:k + T], conv_w[:, i, k:k + 1], t1[:, i],
                                               ALU.mult, ALU.add).then_inc(first_step, 1)
                    n += 1
                dve.wait_ge(first_step, TAPS * DI)
                dve.sem_inc(conv_step, 2 * CONV_OPS)

            prep_stats(0)
            first_convolve()
            step_size(0)
            weigh_input(0)
            prep_stats(1)
            dve.sem_inc(gated, START)
            with dve.Fori(0, BATCH) as b:
                for s in range(STEPS):
                    drive(b, s)
                    if s >= 2:
                        weigh(b, s - 2, 0)
                    scan(b, s)
                    if s >= 2:
                        weigh(b, s - 2, 1)
                    if s == PROJECT[1] + 2:
                        add_res(b, 0)
                    if s == PROJECT[3] + 2:
                        add_res(b, 1)
                weigh(b, STEPS - 2, 0)
                weigh(b, STEPS - 2, 1)
                step_size(b + 1)
                weigh(b, STEPS - 1, 0)
                weigh(b, STEPS - 1, 1)
                weigh_input(b + 1)
                prep_stats(b + 2)
                gate_y(b)
            for j in range(TJ):
                add_res(BATCH, j)

        @block.tensor
        def _(pe):
            M = nc.tensor.matmul
            for signal in (y_turned,):
                pe.sem_inc(signal, START)
            pe.wait_ge(consts, 10)

            def fill_wait(m, f):
                if f < 2:
                    return
                if f == 12:
                    pe.wait_ge(c_ready, m + 1)
                else:
                    pe.wait_ge(emptied, FILLS * m + f - 1)

            def fill_u(m):
                pe.wait_ge(u_ready, TJ * (m + 1))
                for f in range(2):
                    fill_wait(m, f)
                    for i in range(2):
                        kc = 2 * f + i
                        for j in range(TJ):
                            last = nc.tensor.transpose(ps_p[:, f, i * T + j * P:i * T + (j + 1) * P],
                                                       u[:, j, kc * P:(kc + 1) * P], ident[:])
                    last.then_inc(filled, 1)

            def fill_in(m, i):
                if i == 0:
                    pe.wait_ge(emptied, FILLS * m + 2)
                fill_wait(m, 2 + i)
                for k in range(2):
                    r = (2 * i + k) * P
                    for kc in range(KC):
                        last = M(ps_p[:, i % 2, k * T:(k + 1) * T], w_in[:, kc, r:r + P], u_t[:, kc],
                                 start=(kc == 0), stop=(kc == KC - 1))
                last.then_inc(filled, 1)

            def fill_x(m, f):
                pe.wait_ge(xs_ready, (DI + 1) * (m + 1))
                r = (0, WX - P)[f]
                fill_wait(m, 10 + f)
                for i in range(DI):
                    last = M(ps_p[:, f, 0:T], w_x[:, i, r:r + P],
                             xs[:, bass.ds(m % 2, 1), i, :].rearrange("p o t -> p (o t)"),
                             start=(i == 0), stop=(i == DI - 1))
                last.then_inc(filled, 1)

            def turn_c(m):
                pe.wait_ge(emptied, FILLS * m + 12)
                for j in range(TJ):
                    last = nc.tensor.transpose(ps_p[:, 0, j * P:(j + 1) * P], bc_t[:, j * P:(j + 1) * P], ident[:])
                last.then_inc(c_turned, 1)

            def fill_dt(m, i):
                fill_wait(m, 12 + i)
                for k in range(2):
                    c = 2 * i + k
                    last = M(ps_p[:, i % 2, k * T:(k + 1) * T], w_dt[:, c * P:(c + 1) * P], dt_lr[:], start=True, stop=True)
                last.then_inc(filled, 1)

            def turn(b, s):
                pe.wait_ge(scanned, STEPS * b + s + 1 + PRIME)
                for j in range(TJ):
                    if s in (2, 3):
                        pe.wait_ge(started, TJ * (2 * b + s - 2) + j + 1)
                    elif s > 3:
                        pe.wait_ge(summed, TJ * (SUMS * b + s - 4) + j + 1)
                    for i in range(HALF):
                        last = nc.tensor.transpose(ps_h[:, s % 2, j, i * P:(i + 1) * P], hs[:, s % 2, i, j * P:(j + 1) * P],
                                                   ident[:])
                    last.then_inc(turned, 1)

            def turn_y(b):
                pe.wait_ge(summed, TJ * SUMS * (b + 1))
                pe.wait_ge(emptied, FILLS * (b + 2))
                pe.wait_ge(h1_ready, TJ * (b + 1))
                for i in range(DI):
                    for j in range(TJ):
                        last = nc.tensor.transpose(ps_p[:, i // 2, i % 2 * T + j * P:i % 2 * T + (j + 1) * P],
                                                   y[:, j, i * P:(i + 1) * P], ident[:])
                    if i % 2:
                        last.then_inc(y_turned, 1)

            def project_out(b, j, part):
                if j == 0 and part == 0:
                    pe.wait_ge(gated, (DI + 1) * b + START)
                for i in range(part * DI // 2, (part + 1) * DI // 2):
                    last = M(ps_p[:, 2 + j], yg[:, i, j * P:(j + 1) * P], w_out[:, i], start=(i == 0), stop=(i == DI - 1))
                if part:
                    last.then_inc(out_ready, 1)

            pieces = {1: [fill_u], 20: [lambda m: fill_x(m, 0)], 21: [lambda m: fill_x(m, 1)], 23: [turn_c]}
            for i in range(8):
                pieces.setdefault((4, 6, 8, 9, 12, 13, 15, 17)[i], []).append(lambda m, i=i: fill_in(m, i))
            for i in range(4):
                pieces.setdefault((24, 24, 25, 26)[i], []).append(lambda m, i=i: fill_dt(m, i))
            for k, s in enumerate(PROJECT):
                pieces.setdefault(s, []).append(lambda m, k=k: project_out(m - 1, k // 2, k % 2))
            for s in sorted(pieces):
                if s == 4:
                    pe.wait_ge(w_in_loaded, 16)
                if s == 20:
                    pe.wait_ge(weights, 16 * LOADS)
                for piece in pieces[s]:
                    if s not in PROJECT:
                        piece(0)
            with pe.Fori(0, BATCH) as b:
                for s in range(STEPS):
                    for piece in pieces.get(s, []):
                        piece(b + 1)
                    turn(b, s)
                turn_y(b)
            for j in range(TJ):
                for part in range(2):
                    project_out(BATCH, j, part)


def expert_stage(nc, io, h1_scratch, out):
    BATCH, T, D = out.shape
    KC = D // P
    TJ = T // P
    NT = BATCH * TJ
    E = io["sim"].shape[1] // KC
    HD = P
    W3 = 3 * HD
    SCALE = 1.0 / math.sqrt(HD)
    NEG = -1e9

    with ExitStack() as outer:
        def sb_in(stack, name, shape, dt=F32):
            return stack.enter_context(nc.sbuf_tensor(name, shape, dt))

        def sem(name):
            return outer.enter_context(nc.semaphore(name))

        w = sb_in(outer, "ff_w", [P, NT, E])
        ident = sb_in(outer, "ff_ident", [P, P])
        consts = sem("ff_consts")
        done_experts = sem("ff_done_experts")
        act_idle, pool_idle, dve_idle, sp_idle = (sem(f"ff_idle_{n}") for n in ("act", "pool", "dve", "sp"))
        qkv = sb_in(outer, "ff_qkv", [P, NT, W3])

        with ExitStack() as mid:
            x_hi = sb_in(mid, "ff_x_hi", [P, KC, NT, P], F32R)
            x_lo = sb_in(mid, "ff_x_lo", [P, KC, NT, P], F32R)
            rank = sb_in(mid, "ff_rank", [P, E])
            col = sb_in(mid, "ff_col", [P, 4, NT])

            with ExitStack() as ctx:
                ps = ctx.enter_context(nc.psum_tensor("ff_ps1", [P, 8, 512], F32))

                def sb(name, shape, dt=F32):
                    return sb_in(ctx, name, shape, dt)

                minus_half = sb("ff_minus_half", [P, E])
                minus_one = sb("ff_minus_one", [P, TJ])
                width = sb("ff_width", [P, TJ])
                eps = sb("ff_eps", [P, TJ])
                ones = sb("ff_ones", [P, P])
                rank_i = sb("ff_rank_i", [P, E], I32)
                sim = sb("ff_sim", [P, KC, E])
                sim_sq = sb("ff_sim_sq", [P, KC, E])
                sim_rn = sb("ff_sim_rn", [P, E])
                sim_hi = sb("ff_sim_hi", [P, KC, E], F32R)
                sim_lo = sb("ff_sim_lo", [P, KC, E], F32R)
                gates = sb("ff_gates", [P, E])
                hin = sb("ff_hin", [P, 2, TJ, D])
                stats = sb("ff_stats", [P, 2, TJ, 6])
                mv = sb("ff_mv", [P, 2, TJ, 2])
                ln = sb("ff_ln", [P, 2, 4, TJ])
                xn = sb("ff_xn", [P, 2, TJ, D])
                rn = sb("ff_rn", [P, NT])
                logits_t = qkv[0:E, :, 0:P]

                loaded = sem("ff_loaded")
                hin_loaded = [sem(f"ff_hin_loaded{i}") for i in range(2)]
                stats_step = sem("ff_stats_step")
                ln_step = sem("ff_ln_step")
                scalars_ready = sem("ff_scalars_ready")
                xn_ready = sem("ff_xn_ready")
                filled = sem("ff_filled")
                hi_ready = sem("ff_hi_ready")
                lo_ready = sem("ff_lo_ready")
                sim_step = sem("ff_sim_step")
                sim_summed = sem("ff_sim_summed")
                sim_norm = sem("ff_sim_norm")
                gate_step = sem("ff_gate_step")
                logits_ready = sem("ff_logits_ready")
                logits_copied = sem("ff_logits_copied")
                logits_turned = sem("ff_logits_turned")
                logits_done = sem("ff_logits_done")
                LN_OPS = 8
                HALVES = BATCH // 2

                def batches(eng, step):
                    step(0, 0)
                    step(1, 1)
                    with eng.Fori(1, HALVES - 1) as b2:
                        step(2 * b2, 0)
                        step(2 * b2 + 1, 1)
                    step(BATCH - 2, 0)
                    step(BATCH - 1, 1)

                def late(m):
                    return not isinstance(m, int) or m >= 2

                block = ctx.enter_context(nc.Block())

                @block.sync
                def _(sp):
                    sp.dma_start(sim[:].rearrange("p k e -> p (k e)"), io["sim"]).then_inc(loaded, 16)
                    sp.dma_start(gates[:], io["gates"].partition_broadcast(P)).then_inc(loaded, 16)

                    def load(m, o):
                        row = bass.ds(sp.snap(m + 1) if late(m) and not isinstance(m, int) else m + 1, 1)
                        if late(m):
                            sp.wait_ge(xn_ready, TJ * (m - 1))
                            sp.sem_inc(sp_idle, 1)
                        sp.dma_start(hin[:, o], h1_scratch[row]
                                     .rearrange("o (j p) d -> (o p) j d", p=P)).then_inc(hin_loaded[o], 16)

                    batches(sp, load)

                @block.gpsimd
                def _(pool):
                    G = nc.gpsimd
                    G.memset(ident[:], 0.0).then_inc(consts, 1)
                    G.memset(ones[:], 1.0).then_inc(consts, 1)
                    G.memset(minus_half[:], -0.5).then_inc(consts, 1)
                    G.memset(minus_one[:], -1.0).then_inc(consts, 1)
                    G.memset(width[:], float(D)).then_inc(consts, 1)
                    G.memset(eps[:], EPS).then_inc(consts, 1)
                    G.iota(rank_i[:], pattern=[[-1, E]], base=E, channel_multiplier=0).then_inc(consts, 1)
                    pool.wait_ge(consts, 7)
                    G.affine_select(out=ident[:], in_=ident[:], compare_op=ALU.not_equal, fill=1.0, base=0,
                                    pattern=[[-1, P]], channel_multiplier=1).then_inc(consts, 1)
                    G.tensor_copy(rank[:], rank_i[:]).then_inc(consts, 1)
                    pool.wait_ge(consts, 9)
                    pool.wait_ge(sim_step, 2)
                    G.tensor_tensor(sim_rn[:], sim_rn[:], minus_half[:, 0:E], ALU.pow).then_inc(sim_norm, 1)

                    def scalars(m, o):
                        n = [0]

                        def link(ins):
                            n[0] += 1
                            ins.then_inc(ln_step, 1)
                            pool.wait_ge(ln_step, m * LN_OPS + n[0])

                        pool.wait_ge(stats_step, 2 * TJ * (m + 1))
                        if late(m):
                            pool.wait_ge(xn_ready, TJ * (m - 1))
                        pool.sem_inc(pool_idle, 1)
                        mean, var = mv[:, o, :, 0], mv[:, o, :, 1]
                        half = minus_half[:, 0:TJ]
                        link(G.tensor_tensor(ln[:, o, 0], var, eps[:], ALU.add))
                        link(G.tensor_tensor(ln[:, o, 0], ln[:, o, 0], half, ALU.pow))
                        link(G.tensor_tensor(ln[:, o, 1], mean, ln[:, o, 0], ALU.mult))
                        link(G.tensor_tensor(ln[:, o, 1], ln[:, o, 1], minus_one[:, 0:TJ], ALU.mult))
                        pool.sem_inc(scalars_ready, 1)
                        link(G.tensor_tensor(ln[:, o, 2], var, ln[:, o, 0], ALU.mult))
                        link(G.tensor_tensor(ln[:, o, 2], ln[:, o, 2], ln[:, o, 0], ALU.mult))
                        link(G.tensor_tensor(ln[:, o, 2], ln[:, o, 2], width[:, 0:TJ], ALU.mult))
                        pool.sem_inc(pool_idle, 1)
                        link(G.tensor_tensor(rn[:, bass.ds(m * TJ, TJ)], ln[:, o, 2], half, ALU.pow))
                        assert n[0] == LN_OPS

                    batches(pool, scalars)

                @block.scalar
                def _(act):
                    A = nc.scalar
                    act.wait_ge(loaded, 32)
                    act.wait_ge(consts, 9)
                    A.activation(gates[:], gates[:], ACT.Exp, scale=-1.0).then_inc(gate_step, 1)
                    act.wait_ge(sim_step, 3)
                    A.activation(sim_hi[:], sim_sq[:], ACT.Copy).then_inc(sim_norm, 1)

                    def norm(m, o):
                        act.wait_ge(scalars_ready, m + 1)
                        if late(m):
                            act.wait_ge(filled, TJ * (m - 1))
                        for j in range(TJ):
                            A.activation(xn[:, o, j], hin[:, o, j], ACT.Identity, scale=ln[:, o, 0, j:j + 1],
                                         bias=ln[:, o, 1, j:j + 1]).then_inc(xn_ready, 1)

                    def place(m, o):
                        for j in range(TJ):
                            act.wait_ge(filled, TJ * m + j + 1)
                            act.sem_inc(act_idle, 1)
                            A.activation(x_hi[:, :, bass.ds(m * TJ + j, 1), :].rearrange("p k o t -> p (k o) t"),
                                         ps[:, o * TJ + j].rearrange("p (k t) -> p k t", k=KC),
                                         ACT.Copy).then_inc(hi_ready, 1)

                    def copy_logits(m, o):
                        act.wait_ge(logits_ready, m + 1)
                        act.sem_inc(act_idle, 1)
                        A.activation(logits_t[:, bass.ds(TJ * m, TJ), :],
                                     ps[0:E, 2 * TJ + o, 0:T].rearrange("p (j t) -> p j t", j=TJ),
                                     ACT.Copy).then_inc(logits_copied, 1)

                    def step(m, o):
                        if not isinstance(m, int) or m + 1 < BATCH:
                            norm(m + 1, 1 - o)
                        place(m, o)
                        if not isinstance(m, int) or m > 0:
                            copy_logits(m - 1, 1 - o)

                    norm(0, 0)
                    batches(act, step)
                    copy_logits(BATCH - 1, 1)

                @block.vector
                def _(dve):
                    V = nc.vector
                    dve.wait_ge(loaded, 32)
                    dve.wait_ge(consts, 9)
                    V.tensor_tensor(sim_sq[:], sim[:], sim[:], ALU.mult).then_inc(sim_step, 1)
                    dve.wait_ge(sim_summed, 1)
                    V.tensor_scalar(sim_rn[:], ps[:, 0, 0:E], 1e-24, None, ALU.max).then_inc(sim_step, 1)
                    dve.wait_ge(sim_norm, 1)
                    V.tensor_tensor(sim_sq[:], sim[:], sim_rn[:].unsqueeze(1).broadcast_to([P, KC, E]),
                                    ALU.mult).then_inc(sim_step, 1)
                    dve.wait_ge(sim_norm, 2)
                    V.tensor_tensor(sim_lo[:], sim_sq[:], sim_hi[:].bitcast(F32), ALU.subtract).then_inc(sim_step, 1)
                    dve.wait_ge(gate_step, 1)
                    V.tensor_scalar(gates[:], gates[:], 1.0, None, ALU.add).then_inc(gate_step, 1)
                    dve.wait_ge(gate_step, 2)
                    V.reciprocal(gates[:], gates[:]).then_inc(gate_step, 1)

                    def moments(m, o):
                        dve.wait_ge(hin_loaded[o], 16 * ((m - o) // 2 + 1) if isinstance(m, int) else 8 * (m - o) + 16)
                        if late(m):
                            dve.wait_ge(ln_step, LN_OPS * (m - 1))
                        for j in range(TJ):
                            V.bn_stats(stats[:, o, j], hin[:, o, j]).then_inc(stats_step, 1)
                        dve.wait_ge(stats_step, 2 * TJ * m + TJ)
                        dve.sem_inc(dve_idle, 1)
                        for j in range(TJ):
                            V.bn_aggr(mv[:, o, j], stats[:, o, j]).then_inc(stats_step, 1)

                    def place_rest(m, o):
                        for j in range(TJ):
                            tile = m * TJ + j
                            dve.wait_ge(hi_ready, tile + 1)
                            V.tensor_tensor(x_lo[:, :, bass.ds(tile, 1), :].rearrange("p k o t -> p (k o) t"),
                                            ps[:, o * TJ + j].rearrange("p (k t) -> p k t", k=KC),
                                            x_hi[:, :, bass.ds(tile, 1), :].rearrange("p k o t -> p (k o) t").bitcast(F32),
                                            ALU.subtract).then_inc(lo_ready, 1)

                    def step(m, o):
                        if not isinstance(m, int) or m + 1 < BATCH:
                            moments(m + 1, 1 - o)
                        place_rest(m, o)

                    moments(0, 0)
                    batches(dve, step)
                    dve.wait_ge(ln_step, LN_OPS * BATCH)
                    dve.wait_ge(logits_turned, 1)
                    V.tensor_tensor(w[:], ps[:, 7].rearrange("p (t e) -> p t e", e=E),
                                    rn[:].unsqueeze(2).broadcast_to([P, NT, E]), ALU.mult).then_inc(logits_done, 1)
                    dve.wait_ge(logits_done, 1)
                    V.tensor_tensor(w[:], w[:], gates[:].unsqueeze(1).broadcast_to([P, NT, E]),
                                    ALU.subtract).then_inc(logits_done, 1)

                @block.tensor
                def _(pe):
                    pe.wait_ge(consts, 9)
                    pe.wait_ge(sim_step, 1)
                    for k in range(KC):
                        last = nc.tensor.matmul(ps[:, 0, 0:E], ones[:], sim_sq[:, k], start=(k == 0), stop=(k == KC - 1))
                    last.then_inc(sim_summed, 1)
                    pe.wait_ge(sim_step, 4)

                    def turn(m, o):
                        for j in range(TJ):
                            pe.wait_ge(xn_ready, TJ * m + j + 1)
                            if late(m):
                                pe.wait_ge(lo_ready, TJ * (m - 1))
                            for k in range(KC):
                                last = nc.tensor.transpose(ps[:, o * TJ + j, k * P:(k + 1) * P],
                                                           xn[:, o, j, k * P:(k + 1) * P], ident[:])
                            last.then_inc(filled, 1)

                    def multiply(m, o):
                        pe.wait_ge(lo_ready, TJ * (m + 1))
                        if late(m):
                            pe.wait_ge(logits_copied, m - 1)
                        first = True
                        for a, x in ((sim_hi, x_hi), (sim_lo, x_hi), (sim_hi, x_lo)):
                            for k in range(KC):
                                last = nc.tensor.matmul(ps[0:E, 2 * TJ + o, 0:T], a[:, k],
                                                        x[:, k, bass.ds(TJ * m, TJ), :].rearrange("p j t -> p (j t)"),
                                                        start=first, stop=(x is x_lo and k == KC - 1))
                                first = False
                        last.then_inc(logits_ready, 1)

                    def step(m, o):
                        if not isinstance(m, int) or m + 1 < BATCH:
                            turn(m + 1, 1 - o)
                        multiply(m, o)

                    turn(0, 0)
                    batches(pe, step)
                    pe.wait_ge(logits_copied, BATCH)
                    for i in range(NT):
                        last = nc.tensor.transpose(ps[:, 7, i * E:(i + 1) * E], logits_t[:, i], ident[0:E, 0:E])
                    last.then_inc(logits_turned, 1)

            with ExitStack() as ctx:
                ps = ctx.enter_context(nc.psum_tensor("ff_ps2", [P, 8, 512], F32))
                KH = KC // 2
                raw = sb_in(ctx, "ff_raw", [P, KH, W3])
                e_hi = sb_in(ctx, "ff_e_hi", [P, 2, KC, W3], F32R)
                e_lo = sb_in(ctx, "ff_e_lo", [P, 2, KC, W3], F32R)
                raw_loaded = sem("ff_raw_loaded")
                raw_hi = sem("ff_raw_hi")
                raw_lo = sem("ff_raw_lo")
                route_step = sem("ff_route_step")
                route_exp = sem("ff_route_exp")
                cleared = sem("ff_cleared")
                ROUTE_EXP = 25
                room = [t[:, 1].bitcast(F32).rearrange("p k n -> p (k n)") for t in (e_hi, e_lo)]
                r = [room[i // 3][:, i % 3 * NT * E:(i % 3 + 1) * NT * E].rearrange("p (t e) -> p t e", e=E)
                     for i in range(5)]
                mixed = sem("ff_mixed")
                added = sem("ff_added")
                BANKS = 8
                block = ctx.enter_context(nc.Block())

                @block.sync
                def _(sp):
                    for signal in (raw_lo,):
                        sp.sem_inc(signal, START)
                    with sp.Fori(0, E) as e:
                        for h in range(2):
                            cols = bass.ds(sp.snap((2 * e + h) * KH * W3), KH * W3)
                            sp.wait_ge(raw_lo, 2 * e + h + START)
                            sp.dma_start(raw[:].rearrange("p k n -> p (k n)"),
                                         io["w_qkv"][:, cols]).then_inc(raw_loaded, 16)

                @block.gpsimd
                def _(pool):
                    nc.gpsimd.memset(qkv[:], 0.0).then_inc(cleared, 1)
                    pool.wait_ge(cleared, 1)

                @block.scalar
                def _(act):
                    def high(e, h):
                        act.wait_ge(raw_loaded, 16 * (2 * e + h + 1))
                        act.wait_ge(done_experts, e + 1)
                        act.sem_inc(act_idle, 1)
                        nc.scalar.activation(e_hi[:, bass.ds(e % 2, 1), h * KH:(h + 1) * KH].rearrange("p o k n -> p (o k) n"),
                                             raw[:], ACT.Copy).then_inc(raw_hi, 1)

                    high(0, 0)
                    high(0, 1)
                    act.wait_ge(route_step, ROUTE_EXP)
                    nc.scalar.activation(r[0], r[0], ACT.Exp).then_inc(route_exp, 1)
                    act.wait_ge(route_step, ROUTE_EXP + 4)
                    with act.Fori(1, E) as e:
                        for h in range(2):
                            high(e, h)

                @block.vector
                def _(dve):
                    V = nc.vector
                    dve.sem_inc(added, BANKS)

                    def split(e, h):
                        dve.wait_ge(raw_hi, 2 * e + h + 1)
                        hi = e_hi[:, bass.ds(e % 2, 1), h * KH:(h + 1) * KH].rearrange("p o k n -> p (o k) n")
                        lo = e_lo[:, bass.ds(e % 2, 1), h * KH:(h + 1) * KH].rearrange("p o k n -> p (o k) n")
                        V.tensor_tensor(lo, raw[:], hi.bitcast(F32), ALU.subtract).then_inc(raw_lo, 1)

                    def add(e, i):
                        dve.wait_ge(mixed, NT * e + i + 1)
                        V.scalar_tensor_tensor(qkv[:, i], ps[:, i % BANKS, 0:W3], w[:, i, bass.ds(e, 1)], qkv[:, i],
                                               ALU.mult, ALU.add).then_inc(added, 1)

                    split(0, 0)
                    split(0, 1)
                    n = [0]

                    def link(ins):
                        n[0] += 1
                        ins.then_inc(route_step, 1)
                        dve.wait_ge(route_step, n[0])

                    def by_token(x):
                        return x.unsqueeze(2).broadcast_to([P, NT, E])

                    def by_expert(x):
                        return x.unsqueeze(1).broadcast_to([P, NT, E])

                    logits, gated, mask, pick, key = r
                    first, top, none = col[:, 0], col[:, 1], col[:, 2]
                    link(V.tensor_copy(logits, w[:]))
                    link(V.tensor_scalar(mask, logits, 0.0, None, ALU.is_gt))
                    link(V.tensor_scalar(gated, logits, 0.0, None, ALU.max))
                    link(V.tensor_reduce(none, mask, AX.X, ALU.max))
                    link(V.tensor_scalar(none, none, -1.0, 1.0, ALU.mult, ALU.add))
                    for k in range(2):
                        link(V.tensor_reduce(top, logits, AX.X, ALU.max))
                        link(V.tensor_tensor(key, logits, by_token(top), ALU.is_equal))
                        link(V.tensor_tensor(key, key, by_expert(rank[:]), ALU.mult))
                        link(V.tensor_reduce(first, key, AX.X, ALU.max))
                        link(V.tensor_tensor(key, by_expert(rank[:]), by_token(first), ALU.is_equal))
                        if k == 0:
                            link(V.tensor_copy(pick, key))
                            link(V.scalar_tensor_tensor(logits, key, -1e30, logits, ALU.mult, ALU.add))
                    link(V.tensor_tensor(pick, pick, key, ALU.add))
                    link(V.tensor_tensor(pick, pick, by_token(none), ALU.mult))
                    link(V.tensor_tensor(mask, mask, pick, ALU.add))
                    link(V.tensor_tensor(gated, gated, mask, ALU.mult))
                    link(V.tensor_scalar(key, mask, 1.0, -NEG, ALU.subtract, ALU.mult))
                    link(V.tensor_tensor(gated, gated, key, ALU.add))
                    link(V.tensor_reduce(top, gated, AX.X, ALU.max))
                    link(V.tensor_tensor(logits, gated, by_token(top), ALU.subtract))
                    assert n[0] == ROUTE_EXP, n[0]
                    dve.wait_ge(route_exp, 1)
                    link(V.tensor_reduce(top, logits, AX.X, ALU.add))
                    link(V.reciprocal(first, top))
                    link(V.tensor_tensor(logits, logits, mask, ALU.mult))
                    link(V.tensor_tensor(w[:], logits, by_token(first), ALU.mult))
                    dve.wait_ge(route_step, n[0])
                    dve.wait_ge(cleared, 1)
                    with dve.Fori(0, E - 1) as e:
                        for i in range(NT):
                            if i in (4, 8):
                                split(e + 1, i // 4 - 1)
                            add(e, i)
                    for i in range(NT):
                        add(E - 1, i)

                @block.tensor
                def _(pe):
                    pe.sem_inc(done_experts, 2)
                    with pe.Fori(0, E) as e:
                        pe.wait_ge(raw_lo, 2 * e + 2 + START)
                        for i in range(NT):
                            pe.wait_ge(added, NT * e + i + 1)
                            first = True
                            for a, s in ((x_hi, e_hi), (x_hi, e_lo), (x_lo, e_hi)):
                                for k in range(KC):
                                    last = nc.tensor.matmul(ps[:, i % BANKS, 0:W3], a[:, k, i],
                                                            s[:, bass.ds(e % 2, 1), k, :].rearrange("p o n -> p (o n)"),
                                                            start=first, stop=(a is x_lo and k == KC - 1))
                                    first = False
                            last.then_inc(mixed, 1)
                        pe.wait_ge(mixed, NT * (e + 1))
                        pe.sem_inc(done_experts, 1)

        with ExitStack() as ctx:
            def sb(name, shape, dt=F32):
                return sb_in(ctx, name, shape, dt)

            EL = 4
            PRODUCTS = TJ * E
            BANKS = 4
            ps_o = ctx.enter_context(nc.psum_tensor("ff_ps_o", [P, BANKS, 512], F32))
            ps_a = ctx.enter_context(nc.psum_tensor("ff_ps_a", [P, 4, 512], F32))
            o_raw = sb("ff_o_raw", [P, E, D])
            o_hi = sb("ff_o_hi", [P, E, D], F32R)
            o_lo = sb("ff_o_lo", [P, E, D], F32R)
            keep = sb("ff_keep", [P, 3 * P])
            hide = sb("ff_hide", [P, 3 * P])
            now = sb("ff_now", [P, TJ, W3])
            qk_t = sb("ff_qk_t", [P, 2, T])
            score = sb("ff_score", [P, 3 * P])
            prob = sb("ff_prob", [P, 3 * P])
            prob_t = sb("ff_prob_t", [P, 3 * P])
            top = sb("ff_top", [P, TJ])
            total = sb("ff_total", [P, TJ])
            head_hi = sb("ff_head_hi", [P, 2, T], F32R)
            head_lo = sb("ff_head_lo", [P, 2, T], F32R)
            h1 = sb("ff_h1", [P, 2, TJ, D])
            o_loaded = [sem(f"ff_o_loaded{i}") for i in range(E // EL)]
            o_hi_ready = sem("ff_o_hi_ready")
            o_lo_ready = sem("ff_o_lo_ready")
            masks = sem("ff_masks")
            copied = sem("ff_copied")
            qk_turned = sem("ff_qk_turned")
            qk_t_ready = sem("ff_qk_t_ready")
            scored = sem("ff_scored")
            score_step = sem("ff_score_step")
            prob_ready = sem("ff_prob_ready")
            inv_ready = sem("ff_inv_ready")
            prob_scaled = sem("ff_prob_scaled")
            prob_turned = sem("ff_prob_turned")
            prob_t_ready = sem("ff_prob_t_ready")
            head_summed = sem("ff_head_summed")
            head_hi_ready = sem("ff_head_hi_ready")
            head_lo_ready = sem("ff_head_lo_ready")
            multiplied = sem("ff_multiplied")
            summed = sem("ff_summed")
            h1_loaded = sem("ff_h1_loaded")
            out_stored = sem("ff_out_stored")
            SCORE_OPS = 5
            block = ctx.enter_context(nc.Block())

            @block.sync
            def _(sp):
                sp.sem_inc(out_stored, START)

                def load_h1(row, slot):
                    sp.dma_start(h1[:, slot].rearrange("p o j d -> p (o j) d"),
                                 h1_scratch[row].rearrange("o (j p) d -> (o p) j d", p=P)).then_inc(h1_loaded, 16)

                for e in range(0, E, EL):
                    sp.dma_start(o_raw[:, e:e + EL].rearrange("p e d -> p (e d)"),
                                 io["w_o"][:, e * D:(e + EL) * D]).then_inc(o_loaded[e // EL], 16)
                load_h1(bass.ds(1, 1), bass.ds(0, 1))
                with sp.Fori(0, BATCH) as b:
                    row, slot = bass.ds(sp.snap((b + 1) % BATCH + 1), 1), bass.ds(sp.snap((b + 1) % 2), 1)
                    sp.wait_ge(h1_loaded, 16 * (b + 1))
                    sp.sem_inc(sp_idle, 1)
                    sp.wait_ge(out_stored, 16 * b + START)
                    sp.sem_inc(sp_idle, 1)
                    load_h1(row, slot)
                    sp.wait_ge(summed, PRODUCTS * (b + 1) + BANKS)
                    sp.sem_inc(sp_idle, 1)
                    sp.dma_start(out[bass.ds(b, 1)].rearrange("o (j p) d -> (o p) j d", p=P),
                                 h1[:, bass.ds(b % 2, 1)].rearrange("p o j d -> p (o j) d")).then_inc(out_stored, 16)
                sp.wait_ge(h1_loaded, 16 * (BATCH + 1))
                sp.wait_ge(out_stored, 16 * BATCH + START)

            @block.gpsimd
            def _(pool):
                G = nc.gpsimd
                G.memset(keep[:], 1.0).then_inc(masks, 1)
                G.memset(hide[:], 0.0).then_inc(masks, 1)
                pool.wait_ge(masks, 2)
                for c in (0, 2 * P):
                    for m, fill in ((keep, 0.0), (hide, NEG)):
                        G.affine_select(out=m[:, c:c + P], in_=m[:, c:c + P], compare_op=ALU.is_ge, fill=fill, base=0,
                                        pattern=[[-1, P]], channel_multiplier=1).then_inc(masks, 1)

            @block.scalar
            def _(act):
                A = nc.scalar

                def copy_now(m, slot):
                    act.wait_ge(head_summed, m)
                    act.sem_inc(act_idle, 1)
                    A.activation(now[:], qkv[:, bass.ds((TJ * m) % NT, TJ)], ACT.Copy).then_inc(copied, 1)

                def place_qk_t(m, slot):
                    act.wait_ge(scored, m)
                    act.wait_ge(qk_turned, m + 1)
                    A.activation(qk_t[:].rearrange("p a t -> p (a t)"), ps_a[:, 0], ACT.Copy).then_inc(qk_t_ready, 1)

                def exponentials(m, slot):
                    act.wait_ge(score_step, SCORE_OPS * (m + 1))
                    act.wait_ge(prob_turned, m)
                    A.activation(prob[:, 0:P], score[:, 0:P], ACT.Exp, bias=top[:, 0:1],
                                 accum_out=total[:, 0:1]).then_inc(prob_ready, 1)
                    A.activation(prob[:, P:], score[:, P:], ACT.Exp, bias=top[:, 1:2],
                                 accum_out=total[:, 1:2]).then_inc(prob_ready, 1)

                def scale_prob(m, slot):
                    act.wait_ge(inv_ready, m + 1)
                    A.activation(prob[:, 0:P], prob[:, 0:P], ACT.Copy, scale=total[:, 0:1]).then_inc(prob_scaled, 1)
                    A.activation(prob[:, P:], prob[:, P:], ACT.Copy, scale=total[:, 1:2]).then_inc(prob_scaled, 1)

                def place_prob_t(m, slot):
                    act.wait_ge(head_summed, m)
                    act.wait_ge(prob_turned, m + 1)
                    A.activation(prob_t[:], ps_a[:, 2, 0:3 * P], ACT.Copy).then_inc(prob_t_ready, 1)

                def place_head(m, slot):
                    if not isinstance(m, int):
                        act.wait_ge(summed, PRODUCTS * (m - 1) + BANKS)
                    act.wait_ge(head_summed, m + 1)
                    A.activation(head_hi[:, slot], ps_a[:, 3, 0:T], ACT.Copy).then_inc(head_hi_ready, 1)

                for step in (copy_now, place_qk_t, exponentials, scale_prob, place_prob_t, place_head):
                    step(0, 0)
                for e in range(E):
                    act.wait_ge(o_loaded[e // EL], 16)
                    A.activation(o_hi[:, e], o_raw[:, e], ACT.Copy).then_inc(o_hi_ready, 1)
                with act.Fori(0, BATCH // 2) as pair:
                    for slot in range(2):
                        for step in (copy_now, place_qk_t, exponentials, scale_prob, place_prob_t, place_head):
                            step(pair * 2 + slot + 1, 1 - slot)

            @block.vector
            def _(dve):
                V = nc.vector
                dve.sem_inc(summed, BANKS)
                dve.wait_ge(masks, 6)

                def mask_scores(m, slot):
                    n = [0]

                    def link(ins):
                        n[0] += 1
                        ins.then_inc(score_step, 1)
                        dve.wait_ge(score_step, SCORE_OPS * m + n[0])

                    dve.wait_ge(scored, m + 1)
                    dve.wait_ge(prob_ready, TJ * m)
                    link(V.scalar_tensor_tensor(score[:], ps_a[:, 1, 0:3 * P], SCALE, keep[:], ALU.mult, ALU.mult))
                    link(V.tensor_tensor(score[:], score[:], hide[:], ALU.add))
                    link(V.tensor_reduce(top[:, 0:1], score[:, 0:P], AX.X, ALU.max))
                    link(V.tensor_reduce(top[:, 1:2], score[:, P:], AX.X, ALU.max))
                    link(V.tensor_scalar(top[:], top[:], -1.0, None, ALU.mult))
                    assert n[0] == SCORE_OPS

                def invert(m, slot):
                    dve.wait_ge(prob_ready, TJ * (m + 1))
                    V.reciprocal(total[:], total[:]).then_inc(inv_ready, 1)

                def place_rest(m, slot):
                    dve.wait_ge(head_hi_ready, m + 1)
                    V.tensor_tensor(head_lo[:, slot], ps_a[:, 3, 0:T], head_hi[:, slot].bitcast(F32), ALU.subtract)\
                        .then_inc(head_lo_ready, 1)

                def add(b, slot, i):
                    e, j = i // TJ, i % TJ
                    dve.wait_ge(multiplied, PRODUCTS * b + i + 1)
                    if i < TJ:
                        dve.wait_ge(h1_loaded, 16 * (b + 1))
                    else:
                        dve.wait_ge(summed, PRODUCTS * b + i - TJ + 1 + BANKS)
                    weight = w[:, bass.ds(TJ * b + j, 1), e:e + 1].rearrange("p o e -> p (o e)")
                    V.scalar_tensor_tensor(h1[:, slot, j], ps_o[:, i % BANKS], weight, h1[:, slot, j],
                                           ALU.mult, ALU.add).then_inc(summed, 1)

                for step in (mask_scores, invert, place_rest):
                    step(0, 0)
                for e in range(E):
                    dve.wait_ge(o_hi_ready, e + 1)
                    V.tensor_tensor(o_lo[:, e], o_raw[:, e], o_hi[:, e].bitcast(F32), ALU.subtract)\
                        .then_inc(o_lo_ready, 1)
                with dve.Fori(0, BATCH // 2) as pair:
                    for slot in range(2):
                        b = pair * 2 + slot
                        for i in range(PRODUCTS):
                            for before, step in ((8, mask_scores), (13, invert), (25, place_rest)):
                                if before == i:
                                    step(b + 1, 1 - slot)
                            add(b, slot, i)

            @block.tensor
            def _(pe):
                M = nc.tensor.matmul

                def turn_qk(m, slot):
                    pe.wait_ge(qk_t_ready, m)
                    pe.wait_ge(copied, m + 1)
                    for a in range(2):
                        for j in range(TJ):
                            last = nc.tensor.transpose(ps_a[:, 0, a * T + j * P:a * T + (j + 1) * P],
                                                       now[:, j, a * HD:(a + 1) * HD], ident[:])
                    last.then_inc(qk_turned, 1)

                def score_tokens(m, slot):
                    pe.wait_ge(qk_t_ready, m + 1)
                    pe.wait_ge(score_step, SCORE_OPS * m)
                    M(ps_a[:, 1, 0:P], qk_t[:, 0, 0:P], qk_t[:, 1, 0:P], start=True, stop=True)
                    M(ps_a[:, 1, P:3 * P], qk_t[:, 0, P:], qk_t[:, 1], start=True, stop=True).then_inc(scored, 1)

                def turn_prob(m, slot):
                    pe.wait_ge(prob_scaled, TJ * (m + 1))
                    pe.wait_ge(prob_t_ready, m)
                    for k in range(3):
                        last = nc.tensor.transpose(ps_a[:, 2, k * P:(k + 1) * P], prob[:, k * P:(k + 1) * P], ident[:])
                    last.then_inc(prob_turned, 1)

                def sum_values(m, slot):
                    pe.wait_ge(head_lo_ready, m)
                    pe.wait_ge(prob_t_ready, m + 1)
                    for j, k, c in ((0, 0, 0), (1, 0, 1), (1, 1, 2)):
                        last = M(ps_a[:, 3, j * P:(j + 1) * P], now[:, k, 2 * HD:], prob_t[:, c * P:(c + 1) * P],
                                 start=(k == 0), stop=(k == j))
                    last.then_inc(head_summed, 1)

                def multiply(b, slot, i):
                    e, j = i // TJ, i % TJ
                    if i == 0:
                        pe.wait_ge(head_lo_ready, b + 1)
                    if j == 0:
                        pe.wait_ge(o_lo_ready, e + 1)
                    pe.wait_ge(summed, PRODUCTS * b + i + 1)
                    for a, s in ((head_hi, o_hi), (head_hi, o_lo), (head_lo, o_hi)):
                        last = M(ps_o[:, i % BANKS], a[:, slot, j * P:(j + 1) * P], s[:, e],
                                 start=(a is head_hi and s is o_hi), stop=(a is head_lo))
                    last.then_inc(multiplied, 1)

                for step in (turn_qk, score_tokens, turn_prob, sum_values):
                    step(0, 0)
                with pe.Fori(0, BATCH // 2) as pair:
                    for slot in range(2):
                        b = pair * 2 + slot
                        for i in range(PRODUCTS):
                            for before, step in ((2, turn_qk), (5, score_tokens), (16, turn_prob), (20, sum_values)):
                                if before == i:
                                    step(b + 1, 1 - slot)
                            multiply(b, slot, i)


def program(nc, io, out):
    batch, tokens, width = out.shape
    states = 16
    h0_scratch = nc.dram_tensor("h0_scratch", (batch, tokens, width), F32).ap()
    b_scratch = nc.dram_tensor("b_scratch", (states, tokens), F32).ap()
    h1_scratch = nc.dram_tensor("h1_scratch", (batch + 1, tokens, width), F32).ap()
    token_stage(nc, io, h0_scratch)
    mamba_stage(nc, io, h0_scratch, b_scratch, h1_scratch)
    expert_stage(nc, io, h1_scratch, out)


def _rows(w):
    return w.reshape(w.shape[0] // P, P, -1).transpose(1, 0, 2).reshape(P, -1)


def _layout(x, log_dt, log_w_real, w_imag, norm_w, w_in, conv_w, conv_b, w_x, w_dt, b_dt, a, d, w_out,
            sim, gates, q_proj, k_proj, v_proj, o_proj):
    import numpy as np

    ch, h, n, _ = x.shape
    experts, width, head = q_proj.shape
    pairs = h // 2

    def by_pair(w):
        return w.reshape(pairs, 2, n).transpose(1, 2, 0).reshape(2 * n, pairs)

    qkv = np.stack([q_proj, k_proj, v_proj], axis=2).reshape(experts, width // P, P, 3 * head)
    return {
        "xT": x.reshape(ch, pairs, 2, n, 2).transpose(2, 3, 4, 0, 1).reshape(2 * n, 2 * ch * pairs),
        "log_dt": log_dt.reshape(pairs, 2).T,
        "log_w_real": by_pair(log_w_real),
        "w_imag": by_pair(w_imag),
        "norm_w": _rows(norm_w),
        "w_in": _rows(w_in.T),
        "conv_w": _rows(conv_w),
        "conv_b": _rows(conv_b),
        "w_x": _rows(w_x.T),
        "w_dt": w_dt.T,
        "b_dt": _rows(b_dt),
        "a": _rows(a),
        "d": _rows(d),
        "w_out": _rows(w_out.T),
        "sim": _rows(sim),
        "gates": gates.reshape(1, experts),
        "w_qkv": qkv.transpose(2, 0, 1, 3).reshape(P, -1),
        "w_o": o_proj.transpose(1, 0, 2).reshape(head, -1),
    }


def kernel(x, L0_tok_log_dt, L0_tok_log_w_real, L0_tok_w_imag, L0_attn_norm_w, L0_attn_W_in, L0_attn_conv_w,
           L0_attn_conv_b, L0_attn_W_x, L0_attn_W_dt, L0_attn_b_dt, L0_attn_A, L0_attn_D, L0_attn_W_out,
           L0_ffn_sim_matrix, L0_ffn_gates, L0_ffn_q_proj, L0_ffn_k_proj, L0_ffn_v_proj, L0_ffn_o_proj):
    import numpy as np
    import concourse.bacc as bacc
    from concourse.bass_utils import run_bass_kernel_spmd

    given = (x, L0_tok_log_dt, L0_tok_log_w_real, L0_tok_w_imag, L0_attn_norm_w, L0_attn_W_in, L0_attn_conv_w,
             L0_attn_conv_b, L0_attn_W_x, L0_attn_W_dt, L0_attn_b_dt, L0_attn_A, L0_attn_D, L0_attn_W_out,
             L0_ffn_sim_matrix, L0_ffn_gates, L0_ffn_q_proj, L0_ffn_k_proj, L0_ffn_v_proj, L0_ffn_o_proj)
    laid = _layout(*(np.asarray(v) for v in given))
    nc = bacc.Bacc("TRN2", target_bir_lowering=False, num_devices=1)
    arrays, io = {}, {}
    for name, v in laid.items():
        v = np.ascontiguousarray(v)
        arrays[f"in_{name}"] = v
        io[name] = nc.dram_tensor(f"in_{name}", v.shape, mybir.dt.from_np(v.dtype), kind="ExternalInput").ap()
    ch, h = x.shape[0], x.shape[1]
    width = L0_ffn_q_proj.shape[1]
    out = nc.dram_tensor("out_0", (ch, h, width), F32, kind="ExternalOutput").ap()
    program(nc, io, out)
    result = run_bass_kernel_spmd(nc, [arrays], core_ids=[0])
    return result.results[0]["out_0"]
```

```python
import math
from contextlib import ExitStack

import concourse.bass as bass
from concourse import mybir

P = 128
F32 = mybir.dt.float32
F32R = mybir.dt.float32r
I32 = mybir.dt.int32
ALU = mybir.AluOpType
ACT = mybir.ActivationFunctionType
AX = mybir.AxisListType

MAGIC = 1.5 * 2 ** 23
LOG2E = 1.0 / math.log(2.0)
LN2_HI = 0.693359375
LN2_LO = math.log(2.0) - LN2_HI
TWO_PI = 2 * math.pi
TWO_PI_HI = 6.28125
TWO_PI_LO = TWO_PI - TWO_PI_HI
PI_IN = 3.1415925
EPS = 1e-5
START = 1


def token_stage(nc, io, h0_scratch):
    H, N = io["w_imag"].shape[1] * 2, 64
    Q = H // 2
    CH = io["xT"].shape[1] // (2 * Q)
    LEN = h0_scratch.shape[2]
    L0 = P
    L1 = LEN // L0
    LT = L0 + L1
    QC = 16
    CHUNKS = Q // QC
    QB = 512 // L0
    BANKS = QC // QB

    with ExitStack() as ctx:
        def sb(name, shape, dt=F32):
            return ctx.enter_context(nc.sbuf_tensor(name, shape, dt))

        def sem(name):
            return ctx.enter_context(nc.semaphore(name))

        coef = sb("tk_coef", [P, 2, CH, Q])
        prod = sb("tk_prod", [P, 4, CH, Q])
        logs = sb("tk_logs", [P, 2, Q])
        w_im = sb("tk_w_im", [P, Q])
        exps = sb("tk_exps", [P, 2, Q])
        w_re = sb("tk_w_re", [P, Q])
        a = sb("tk_a", [P, Q])
        b = sb("tk_b", [P, Q])
        em1 = sb("tk_em1", [P, Q])
        t = [sb(f"tk_t{i}", [P, 2, Q]) for i in range(5)]
        ti = sb("tk_ti", [P, 2, Q], I32)
        g = sb("tk_g", [P, 2, Q])
        pos_i = sb("tk_pos_i", [P, LT], I32)
        pos = sb("tk_pos", [P, LT])
        phase = sb("tk_phase", [P, 2, QC, LT])
        turns = sb("tk_turns", [P, QC, LT])
        decay = sb("tk_decay", [P, 2, QC, LT])
        nsin = sb("tk_nsin", [P, 2, QC, LT])
        cosine = sb("tk_cosine", [P, 2, QC, LT])
        e_re = sb("tk_e_re", [P, 2, QC, LT])
        e_nim = sb("tk_e_nim", [P, 2, QC, LT])
        p_t = prod[:].rearrange("p i c q -> p i (c q)")[:, :, 0:QC * CH * L1]\
            .rearrange("p i (q c l) -> p i q c l", q=QC, c=CH)
        p_re = sb("tk_p_re", [P, 2, QC, CH, L1])
        p_im = sb("tk_p_im", [P, 2, QC, CH, L1])
        stage = sb("tk_stage", [P, 2, QC, L0])
        half_angle = sb("tk_half_angle", [P, Q])
        sine = sb("tk_sine", [P, Q])
        absolute = sb("tk_absolute", [P, Q])
        half_pi = sb("tk_half_pi", [P, 1])
        ps = ctx.enter_context(nc.psum_tensor("tk_ps", [P, 8, 512], F32))

        loaded = sem("tk_loaded")
        c_loaded = sem("tk_c_loaded")
        positions = sem("tk_positions")
        angle_ready = sem("tk_angle_ready")
        trig_ready = sem("tk_trig_ready")
        ab_ready = sem("tk_ab_ready")
        g_ready = sem("tk_g_ready")
        products_ready = sem("tk_products_ready")
        im_ready = sem("tk_im_ready")
        coef_ready = sem("tk_coef_ready")
        phase_ready = sem("tk_phase_ready")
        trig_step = sem("tk_trig_step")
        decay_ready = sem("tk_decay_ready")
        e_ready = sem("tk_e_ready")
        p_im_step = sem("tk_p_im_step")
        p_re_ready = sem("tk_p_re_ready")
        sums_ready = sem("tk_sums_ready")
        staged = sem("tk_staged")
        stored = [sem(f"tk_stored{i}") for i in range(2)]
        dve_step = sem("tk_dve_step")
        act_idle = sem("tk_act_idle")
        pe_idle = sem("tk_pe_idle")

        def bq(x):
            return x.unsqueeze(1).broadcast_to([P, CH, Q])

        block = ctx.enter_context(nc.Block())

        @block.sync
        def _(sp):
            sp.dma_start(logs[0:64, 0, :], io["log_dt"][0:1, :].partition_broadcast(64)).then_inc(loaded, 16)
            sp.dma_start(logs[64:P, 0, :], io["log_dt"][1:2, :].partition_broadcast(64)).then_inc(loaded, 16)
            sp.dma_start(logs[:, 1, :], io["log_w_real"]).then_inc(loaded, 16)
            sp.dma_start(w_im[:], io["w_imag"]).then_inc(loaded, 16)
            sp.dma_start(coef[:].rearrange("p r c q -> p (r c q)"), io["xT"]).then_inc(c_loaded, 16)
            h0_v = h0_scratch.rearrange("c (q two) (l1 l0) -> two c l1 q l0", two=2, l0=L0)

            def store(k, slot):
                sp.wait_ge(staged, BANKS * (k + 1))
                for h2 in range(2):
                    for c in range(CH):
                        pt = 64 * h2 + L1 * c
                        sp.dma_start(h0_v[h2, c, :, bass.ds(k * QC, QC), :],
                                     stage[pt:pt + L1, slot, :, :]).then_inc(stored[slot], 16)

            with sp.Fori(0, CHUNKS // 2) as pair:
                for slot in range(2):
                    store(pair * 2 + slot, slot)
            for slot in range(2):
                sp.wait_ge(stored[slot], 16 * CH * CHUNKS)

        @block.gpsimd
        def _(pool):
            nc.gpsimd.iota(pos_i[:, 0:L0], pattern=[[1, L0]], base=0, channel_multiplier=0).then_inc(positions, 1)
            nc.gpsimd.iota(pos_i[:, L0:LT], pattern=[[L0, L1]], base=0, channel_multiplier=0).then_inc(positions, 1)
            nc.gpsimd.memset(half_pi[:], math.pi / 2).then_inc(positions, 1)
            pool.wait_ge(positions, 3)
            nc.gpsimd.tensor_copy(pos[:], pos_i[:]).then_inc(positions, 1)

            def imaginary_p(k, slot):
                qs = bass.ds(k * QC, QC)
                pool.wait_ge(e_ready, 2 * k + 2)
                if not isinstance(k, int) or k >= 2:
                    pool.wait_ge(sums_ready, k - 1)
                c_re = coef[:, 0, :, qs].rearrange("p c q -> p q c").unsqueeze(3).broadcast_to([P, QC, CH, L1])
                c_im = coef[:, 1, :, qs].rearrange("p c q -> p q c").unsqueeze(3).broadcast_to([P, QC, CH, L1])
                er = e_re[:, slot, :, L0:LT].unsqueeze(2).broadcast_to([P, QC, CH, L1])
                ei = e_nim[:, slot, :, L0:LT].unsqueeze(2).broadcast_to([P, QC, CH, L1])
                nc.gpsimd.tensor_tensor(p_t[:, 2], c_im, er, ALU.mult).then_inc(p_im_step, 1)
                nc.gpsimd.tensor_tensor(p_t[:, 3], c_re, ei, ALU.mult).then_inc(p_im_step, 1)
                pool.wait_ge(p_im_step, 3 * k + 2)
                nc.gpsimd.tensor_tensor(p_im[:, slot], p_t[:, 2], p_t[:, 3], ALU.subtract).then_inc(p_im_step, 1)
                pool.wait_ge(p_im_step, 3 * k + 3)

            pool.wait_ge(g_ready, 1)
            pool.wait_ge(c_loaded, 16)
            nc.gpsimd.tensor_tensor(prod[:, 2], coef[:, 0], bq(g[:, 1]), ALU.mult).then_inc(im_ready, 1)
            nc.gpsimd.tensor_tensor(prod[:, 3], coef[:, 1], bq(g[:, 0]), ALU.mult).then_inc(im_ready, 1)
            pool.wait_ge(im_ready, 2)
            pool.wait_ge(products_ready, 1)
            nc.gpsimd.tensor_tensor(coef[:, 1], prod[:, 2], prod[:, 3], ALU.add).then_inc(im_ready, 1)
            pool.wait_ge(im_ready, 3)
            pool.wait_ge(coef_ready, 1)
            imaginary_p(0, 0)
            with pool.Fori(1, CHUNKS // 2) as pair:
                imaginary_p(pair * 2 - 1, 1)
                imaginary_p(pair * 2, 0)
            imaginary_p(CHUNKS - 1, 1)

        @block.scalar
        def _(act):
            act.wait_ge(positions, 3)
            act.wait_ge(angle_ready, 1)
            nc.scalar.activation(sine[:], half_angle[:], ACT.Sin).then_inc(trig_ready, 1)
            nc.scalar.activation(absolute[:], half_angle[:], ACT.Abs).then_inc(trig_ready, 1)
            act.wait_ge(trig_ready, 2)
            nc.scalar.activation(t[3][:, 0], absolute[:], ACT.Sin, bias=half_pi[:], scale=-1.0).then_inc(trig_ready, 1)

            def exps(k, slot):
                if not isinstance(k, int) or k >= 2:
                    act.wait_ge(e_ready, 2 * k - 2)
                    act.sem_inc(act_idle, 1)
                for q in range(QC):
                    last = nc.scalar.activation(decay[:, slot, q], pos[:], ACT.Exp,
                                                scale=a[:, bass.ds(k * QC + q, 1)])
                last.then_inc(decay_ready, 1)

            def sines(k, slot):
                act.wait_ge(phase_ready, k + 1)
                nc.scalar.activation(nsin[:, slot], phase[:, slot], ACT.Sin, scale=-1.0).then_inc(trig_step, 1)
                nc.scalar.activation(cosine[:, slot], phase[:, slot], ACT.Abs).then_inc(trig_step, 1)
                act.wait_ge(trig_step, 3 * k + 2)
                nc.scalar.activation(cosine[:, slot], cosine[:, slot], ACT.Sin, bias=half_pi[:], scale=-1.0)\
                    .then_inc(trig_step, 1)

            def copy_out(k, slot):
                act.wait_ge(sums_ready, k + 1)
                if not isinstance(k, int) or k >= 2:
                    act.wait_ge(stored[slot], 16 * CH * (k - slot))
                for qb in range(BANKS):
                    nc.scalar.activation(stage[:, slot, QB * qb:QB * qb + QB, :],
                                         ps[:, BANKS * slot + qb, :].rearrange("p (q l) -> p q l", q=QB),
                                         ACT.Copy).then_inc(staged, 1)

            act.wait_ge(positions, 4)
            act.wait_ge(ab_ready, 1)
            def step(k, slot):
                sines(k, slot)
                if not isinstance(k, int) or k + 1 < CHUNKS:
                    exps(k + 1, 1 - slot)
                if not isinstance(k, int) or k > 0:
                    copy_out(k - 1, 1 - slot)

            exps(0, 0)
            step(0, 0)
            step(1, 1)
            with act.Fori(1, CHUNKS // 2 - 1) as pair:
                step(pair * 2, 0)
                step(pair * 2 + 1, 1)
            step(CHUNKS - 2, 0)
            step(CHUNKS - 1, 1)
            copy_out(CHUNKS - 1, 1)

        @block.vector
        def _(dve):
            count = [0]

            def link(ins):
                count[0] += 1
                ins.then_inc(dve_step, 1)
                dve.wait_ge(dve_step, count[0])

            V = nc.vector

            def exp_parts(x, k, r, q, two_k):
                link(V.tensor_scalar(k, x, LOG2E, MAGIC, ALU.mult, ALU.add))
                link(V.tensor_scalar(k, k, MAGIC, None, ALU.subtract))
                link(V.tensor_scalar(k, k, -126.0, 127.0, ALU.max, ALU.min))
                link(V.scalar_tensor_tensor(r, k, -LN2_HI, x, ALU.mult, ALU.add))
                link(V.scalar_tensor_tensor(r, k, -LN2_LO, r, ALU.mult, ALU.add))
                link(V.tensor_scalar(q, r, 1.0 / math.factorial(8), None, ALU.mult))
                for n in range(7, 0, -1):
                    link(V.scalar_tensor_tensor(q, q, 1.0 / math.factorial(n), r, ALU.add, ALU.mult))
                link(V.tensor_scalar(two_k, k, 127.0, float(1 << 23), ALU.add, ALU.mult))

            def phases(k, slot, link):
                ph = phase[:, slot]
                link(V.tensor_tensor(ph, b[:, bass.ds(k * QC, QC)].unsqueeze(2).broadcast_to([P, QC, LT]),
                                     pos[:].unsqueeze(1).broadcast_to([P, QC, LT]), ALU.mult))
                link(V.tensor_scalar(turns[:], ph, 1 / TWO_PI, MAGIC, ALU.mult, ALU.add))
                link(V.tensor_scalar(turns[:], turns[:], MAGIC, None, ALU.subtract))
                link(V.scalar_tensor_tensor(ph, turns[:], -TWO_PI_HI, ph, ALU.mult, ALU.add))
                link(V.scalar_tensor_tensor(ph, turns[:], -TWO_PI_LO, ph, ALU.mult, ALU.add))
                link(V.tensor_scalar(ph, ph, -PI_IN, PI_IN, ALU.max, ALU.min))
                dve.sem_inc(phase_ready, 1)

            dve.wait_ge(loaded, 16 * 4)
            exp_parts(logs[:], t[0][:], t[1][:], t[2][:], ti[:])
            two_k = ti[:].bitcast(F32)
            link(V.tensor_tensor(t[2][:], t[2][:], two_k, ALU.mult))
            link(V.tensor_tensor(exps[:], t[2][:], two_k, ALU.add))
            link(V.scalar_tensor_tensor(a[:], exps[:, 1], -1.0, exps[:, 0], ALU.mult, ALU.mult))
            link(V.tensor_scalar(w_re[:], exps[:, 1], -1.0, None, ALU.mult))
            link(V.tensor_tensor(b[:], w_im[:], exps[:, 0], ALU.mult))
            dve.sem_inc(ab_ready, 1)
            link(V.tensor_scalar(half_angle[:], b[:], 0.5, None, ALU.mult))
            link(V.tensor_scalar(t[4][:, 0], half_angle[:], 1 / TWO_PI, MAGIC, ALU.mult, ALU.add))
            link(V.tensor_scalar(t[4][:, 0], t[4][:, 0], MAGIC, None, ALU.subtract))
            link(V.scalar_tensor_tensor(half_angle[:], t[4][:, 0], -TWO_PI_HI, half_angle[:], ALU.mult, ALU.add))
            link(V.scalar_tensor_tensor(half_angle[:], t[4][:, 0], -TWO_PI_LO, half_angle[:], ALU.mult, ALU.add))
            link(V.tensor_scalar(half_angle[:], half_angle[:], -PI_IN, PI_IN, ALU.max, ALU.min))
            dve.sem_inc(angle_ready, 1)
            dve.wait_ge(positions, 4)
            phases(0, 0, link)
            exp_parts(a[:], t[0][:, 0], t[1][:, 0], t[2][:, 0], ti[:, 0])
            two_k = ti[:, 0].bitcast(F32)
            link(V.tensor_tensor(t[2][:, 0], t[2][:, 0], two_k, ALU.mult))
            link(V.scalar_tensor_tensor(em1[:], two_k, -1.0, t[2][:, 0], ALU.add, ALU.add))
            link(V.tensor_tensor(t[4][:, 0], w_re[:], w_re[:], ALU.mult))
            link(V.tensor_tensor(t[4][:, 1], w_im[:], w_im[:], ALU.mult))
            link(V.tensor_tensor(t[4][:, 0], t[4][:, 0], t[4][:, 1], ALU.add))
            link(V.reciprocal(t[4][:, 1], t[4][:, 0]))
            link(V.tensor_scalar(t[4][:, 1], t[4][:, 1], 2.0, None, ALU.mult))
            inv = t[4][:, 1]
            dve.wait_ge(trig_ready, 3)
            s, c = sine[:], t[3][:, 0]
            u, er, ei = t[4][:, 0], t[0][:, 1], t[1][:, 1]
            link(V.scalar_tensor_tensor(u, s, -2.0, s, ALU.mult, ALU.mult))
            link(V.scalar_tensor_tensor(er, em1[:], 1.0, u, ALU.add, ALU.mult))
            link(V.tensor_tensor(er, er, em1[:], ALU.add))
            link(V.scalar_tensor_tensor(u, s, 2.0, c, ALU.mult, ALU.mult))
            link(V.scalar_tensor_tensor(ei, em1[:], 1.0, u, ALU.add, ALU.mult))
            x1, x2 = t[2][:, 0], t[2][:, 1]
            link(V.tensor_tensor(x1, er, w_re[:], ALU.mult))
            link(V.tensor_tensor(x2, ei, w_im[:], ALU.mult))
            link(V.tensor_tensor(x1, x1, x2, ALU.add))
            link(V.tensor_tensor(g[:, 0], x1, inv, ALU.mult))
            link(V.tensor_tensor(x1, ei, w_re[:], ALU.mult))
            link(V.tensor_tensor(x2, er, w_im[:], ALU.mult))
            link(V.tensor_tensor(x1, x1, x2, ALU.subtract))
            link(V.tensor_tensor(g[:, 1], x1, inv, ALU.mult))
            dve.sem_inc(g_ready, 1)
            dve.wait_ge(c_loaded, 16)
            link(V.tensor_tensor(prod[:, 0], coef[:, 0], bq(g[:, 0]), ALU.mult))
            link(V.tensor_tensor(prod[:, 1], coef[:, 1], bq(g[:, 1]), ALU.mult))
            dve.wait_ge(im_ready, 2)
            V.tensor_tensor(coef[:, 0], prod[:, 0], prod[:, 1], ALU.subtract).then_inc(coef_ready, 1)
            dve.sem_inc(products_ready, 1)
            dve.wait_ge(coef_ready, 1)
            dve.wait_ge(im_ready, 3)
            PHASE_STEPS, STEPS = 6, 9
            setup = count[0] - PHASE_STEPS

            def chunk_link(k, local):
                def link(ins):
                    local[0] += 1
                    ins.then_inc(dve_step, 1)
                    dve.wait_ge(dve_step, k * STEPS + (setup + PHASE_STEPS + local[0]))
                return link

            def middle(k, slot, link):
                dve.wait_ge(trig_step, 3 * k + 3)
                dve.wait_ge(decay_ready, k + 1)
                if not isinstance(k, int) or k >= 2:
                    dve.wait_ge(sums_ready, k - 1)
                V.tensor_tensor(e_re[:, slot], cosine[:, slot], decay[:, slot], ALU.mult).then_inc(e_ready, 1)
                V.tensor_tensor(e_nim[:, slot], nsin[:, slot], decay[:, slot], ALU.mult).then_inc(e_ready, 1)
                dve.wait_ge(e_ready, 2 * k + 2)
                qs = bass.ds(k * QC, QC)
                c_re = coef[:, 0, :, qs].rearrange("p c q -> p q c").unsqueeze(3).broadcast_to([P, QC, CH, L1])
                c_im = coef[:, 1, :, qs].rearrange("p c q -> p q c").unsqueeze(3).broadcast_to([P, QC, CH, L1])
                er = e_re[:, slot, :, L0:LT].unsqueeze(2).broadcast_to([P, QC, CH, L1])
                ei = e_nim[:, slot, :, L0:LT].unsqueeze(2).broadcast_to([P, QC, CH, L1])
                link(V.tensor_tensor(p_t[:, 0], c_re, er, ALU.mult))
                link(V.tensor_tensor(p_t[:, 1], c_im, ei, ALU.mult))
                link(V.tensor_tensor(p_re[:, slot], p_t[:, 0], p_t[:, 1], ALU.add))
                dve.sem_inc(p_re_ready, 1)

            def step(k, slot):
                link = chunk_link(k, [0])
                dve.wait_ge(trig_step, 3 * k)
                phases(k + 1, 1 - slot, link)
                middle(k, slot, link)

            link0 = chunk_link(0, [0])
            phases(1, 1, link0)
            middle(0, 0, link0)
            with dve.Fori(1, CHUNKS // 2) as pair:
                step(pair * 2 - 1, 1)
                step(pair * 2, 0)
            middle(CHUNKS - 1, 1, chunk_link(CHUNKS - 1, [0]))

        @block.tensor
        def _(pe):
            def sums(k, slot):
                pe.wait_ge(p_re_ready, k + 1)
                pe.wait_ge(p_im_step, 3 * k + 3)
                if not isinstance(k, int) or k >= 2:
                    pe.wait_ge(staged, BANKS * (k - 1))
                    pe.sem_inc(pe_idle, 1)
                for q in range(QC):
                    for part, (lhs, rhs) in enumerate(((p_re, e_re), (p_im, e_nim))):
                        for h2 in range(2):
                            rows = slice(64 * h2, 64 * h2 + 64)
                            last = nc.tensor.matmul(
                                ps[rows, BANKS * slot + q // QB, q % QB * L0:(q % QB + 1) * L0],
                                lhs[rows, slot, q].rearrange("p c l -> p (c l)"), rhs[rows, slot, q, 0:L0],
                                start=(part == 0), stop=(part == 1))
                last.then_inc(sums_ready, 1)

            for slot in range(2):
                sums(slot, slot)
            with pe.Fori(1, CHUNKS // 2) as pair:
                for slot in range(2):
                    sums(pair * 2 + slot, slot)


def mamba_stage(nc, io, h0_scratch, b_scratch, h1_scratch):
    BATCH, T, D = h0_scratch.shape
    KC = D // P
    TJ = T // P
    ED = io["w_in"].shape[1] // KC // 2
    DI = ED // P
    NS = io["a"].shape[1] // DI
    R = P
    WX = R + 2 * NS
    TAPS = io["conv_w"].shape[1] // DI
    HALF = DI // 2
    STEPS = 2 * NS
    SW = HALF * T
    BG = 2
    GROUPS = NS // BG
    FILLS = 16
    DA_SLOTS = 4
    B0 = P - 2 * NS

    with ExitStack() as ctx:
        def sb(name, shape, dt=F32):
            return ctx.enter_context(nc.sbuf_tensor(name, shape, dt))

        def sem(name):
            return ctx.enter_context(nc.semaphore(name))

        w_in = sb("ma_w_in", [P, KC, 2 * ED])
        w_x = sb("ma_w_x", [P, DI, WX])
        w_dt = sb("ma_w_dt", [P, ED])
        w_out = sb("ma_w_out", [P, DI, D])
        norm_w = sb("ma_norm_w", [P, KC])
        conv_w = sb("ma_conv_w", [P, DI, TAPS])
        conv_b = sb("ma_conv_b", [P, DI])
        b_dt = sb("ma_b_dt", [P, DI])
        a_w = sb("ma_a", [P, DI, NS])
        d_w = sb("ma_d", [P, DI])
        ident = sb("ma_ident", [P, P])
        minus_half = sb("ma_minus_half", [P, TJ])
        minus_one = sb("ma_minus_one", [P, TJ])
        one = sb("ma_one", [P, TJ])
        eps = sb("ma_eps", [P, TJ])

        hin = sb("ma_hin", [P, TJ, D])
        stats = sb("ma_stats", [P, TJ, 6])
        mv = sb("ma_mv", [P, TJ, 2])
        ln = sb("ma_ln", [P, 8, TJ])
        res = sb("ma_res", [P, 2, TJ, D])
        u_t = sb("ma_u_t", [P, KC, T])
        xc = sb("ma_xc", [P, DI, TAPS - 1 + T])
        gate = sb("ma_gate", [P, 2, DI, T])
        t1 = sb("ma_t1", [P, DI, T])
        t2 = sb("ma_t2", [P, DI, T])
        u = t1[:].rearrange("p i t -> p (i t)")[:, 0:TJ * D].rearrange("p (j d) -> p j d", j=TJ)
        xs = sb("ma_xs", [P, 2, DI, T])
        dt_lr = sb("ma_dt_lr", [P, T])
        bc_t = sb("ma_bc_t", [P, T])
        bc_tok = sb("ma_bc_tok", [P, 2, TJ, 2 * NS])
        dtx_t = sb("ma_dtx_t", [P, TJ, HALF * P])
        b_diag = sb("ma_b_diag", [P, 2, TJ, P])
        dt = sb("ma_dt", [P, DI, T])
        dtx = sb("ma_dtx", [P, DI, T])
        b_all = sb("ma_b_all", [P, 2, BG, T])
        da = sb("ma_da", [P, DA_SLOTS, HALF, T])
        dbx = sb("ma_dbx", [P, 2, HALF, T])
        hs = sb("ma_hs", [P, 2, HALF, T])
        y = sb("ma_y", [P, TJ, ED])
        yg = sb("ma_yg", [P, DI, T])
        ps_h = ctx.enter_context(nc.psum_tensor("ma_ps_h", [P, 2, TJ, 512], F32))
        ps_p = ctx.enter_context(nc.psum_tensor("ma_ps_p", [P, 4, 512], F32))

        small = sem("ma_small")
        w_in_loaded = [sem(f"ma_w_in_loaded{i}") for i in range(2)]
        weights = sem("ma_weights")
        consts = sem("ma_consts")
        hin_loaded = sem("ma_hin_loaded")
        stats_step = sem("ma_stats_step")
        ln_step = sem("ma_ln_step")
        u_ready = sem("ma_u_ready")
        res_ready = sem("ma_res_ready")
        filled = sem("ma_filled")
        emptied = sem("ma_emptied")
        conv_step = sem("ma_conv_step")
        first_step = sem("ma_first_step")
        c_turned = sem("ma_c_turned")
        dtx_turned = sem("ma_dtx_turned")
        diag_ready = sem("ma_diag_ready")
        pe_driven = sem("ma_pe_driven")
        act_idle = sem("ma_act_idle")
        dve_idle = sem("ma_dve_idle")
        sp_idle = sem("ma_sp_idle")
        xs_ready = sem("ma_xs_ready")
        dtlr_ready = sem("ma_dtlr_ready")
        c_ready = sem("ma_c_ready")
        b_stored = sem("ma_b_stored")
        b_loaded = [sem(f"ma_b_loaded{i}") for i in range(2)]
        soft_arg = sem("ma_soft_arg")
        soft_log = sem("ma_soft_log")
        soft_one = sem("ma_soft_one")
        soft_corr = sem("ma_soft_corr")
        soft_step = sem("ma_soft_step")
        dt_ready = sem("ma_dt_ready")
        da_ready = sem("ma_da_ready")
        dbx_ready = sem("ma_dbx_ready")
        scanned = sem("ma_scanned")
        turned = sem("ma_turned")
        started = sem("ma_started")
        summed = sem("ma_summed")
        y_turned = sem("ma_y_turned")
        gate_ready = sem("ma_gate_ready")
        gated = sem("ma_gated")
        out_ready = sem("ma_out_ready")
        h1_ready = sem("ma_h1_ready")
        h1_stored = sem("ma_h1_stored")

        LOADS = 3
        SMALL = 6
        LN_OPS = 9
        CONV_OPS = 2 * TAPS - 1
        PROJECT = (0, 3, 7, 10)
        PE_STEPS = list(range(17, STEPS, 2))
        DVE_STEPS = [s for s in range(STEPS) if s not in PE_STEPS]
        Z_FILLS = (6, 7, 14, 15)
        START_SUM, GATE, SOFT = 3, 12, 28
        SUMS = STEPS - 2
        PRIME = DA_SLOTS

        block = ctx.enter_context(nc.Block())

        @block.sync
        def _(sp):
            def load(dst, name, signal):
                flat = dst[:] if len(dst.shape) == 2 else dst[:].rearrange("p a b -> p (a b)")
                sp.dma_start(flat, io[name]).then_inc(signal, 16)

            def load_hin(m):
                row = bass.ds(m % BATCH if isinstance(m, int) else sp.snap(m % BATCH), 1)
                if not isinstance(m, int) or m:
                    sp.wait_ge(res_ready, TJ * m)
                    sp.sem_inc(sp_idle, 1)
                sp.dma_start(hin[:], h0_scratch[row].rearrange("o (j p) d -> (o p) j d", p=P))\
                    .then_inc(hin_loaded, 16)

            def store_b(m):
                sp.wait_ge(emptied, FILLS * m + 10)
                sp.dma_start(b_scratch, bc_t[B0:B0 + NS, :]).then_inc(b_stored, 16)
                sp.wait_ge(b_stored, 16 * (m + 1))
                sp.sem_inc(sp_idle, 1)

            def load_b(m, g):
                if g:
                    sp.wait_ge(scanned, STEPS * m + 2 * BG * (g - 1) + PRIME)
                sp.dma_start(b_all[:, g % 2].rearrange("p n t -> p (n t)"),
                             b_scratch[g * BG:(g + 1) * BG, :].rearrange("n t -> (n t)").unsqueeze(0)
                             .partition_broadcast(P)).then_inc(b_loaded[g % 2], 16)

            load_hin(0)
            for dst, name in ((norm_w, "norm_w"), (conv_w, "conv_w"), (conv_b, "conv_b"), (b_dt, "b_dt"), (a_w, "a"),
                              (d_w, "d")):
                load(dst, name, small)
            w_in_v = io["w_in"].rearrange("p (k n) -> p k n", k=KC)
            for part in range(2):
                cols = slice(part * ED, (part + 1) * ED)
                sp.dma_start(w_in[:, :, cols], w_in_v[:, :, cols]).then_inc(w_in_loaded[part], 16)
            load(w_x, "w_x", weights)
            load(w_dt, "w_dt", weights)
            load(w_out, "w_out", weights)
            load_hin(1)
            store_b(0)
            load_b(0, 0)
            load_b(0, 1)
            with sp.Fori(0, BATCH) as b:
                load_b(b, 2)
                load_b(b, 3)
                sp.wait_ge(h1_ready, TJ * (b + 1))
                sp.dma_start(h1_scratch[bass.ds(b, 1)].rearrange("o (j p) d -> (o p) j d", p=P),
                             res[:, bass.ds((b + 1) % 2, 1)].rearrange("p o j d -> p (o j) d")).then_inc(h1_stored, 16)
                for g in range(4, GROUPS):
                    load_b(b, g)
                    if g == GROUPS - 3:
                        load_hin(b + 2)
                for slot in range(2):
                    sp.wait_ge(b_loaded[slot], 16 * (GROUPS // 2) * (b + 1))
                store_b(b + 1)
                sp.wait_ge(scanned, STEPS * b + 2 * BG * (GROUPS - 1) + PRIME)
                load_b(b + 1, 0)
                load_b(b + 1, 1)
            sp.wait_ge(h1_ready, TJ * (BATCH + 1))
            sp.dma_start(h1_scratch[BATCH].rearrange("(j p) d -> p j d", p=P),
                         res[:, (BATCH + 1) % 2]).then_inc(h1_stored, 16)
            sp.wait_ge(h1_stored, 16 * (BATCH + 1))
            sp.wait_ge(b_stored, 16 * (BATCH + 1))
            for slot in range(2):
                sp.wait_ge(b_loaded[slot], 16 * (GROUPS // 2 * BATCH + 1))

        @block.gpsimd
        def _(pool):
            G = nc.gpsimd
            G.memset(ident[:], 0.0).then_inc(consts, 1)
            G.memset(minus_half[:], -0.5).then_inc(consts, 1)
            G.memset(xc[:, :, 0:TAPS - 1], 0.0).then_inc(consts, 1)
            G.memset(da[:, :, :, 0:1], 0.0).then_inc(consts, 1)
            G.memset(yg[:], 0.0).then_inc(consts, 1)
            G.memset(res[:, 1], 0.0).then_inc(consts, 1)
            G.memset(minus_one[:], -1.0).then_inc(consts, 1)
            G.memset(one[:], 1.0).then_inc(consts, 1)
            G.memset(eps[:], EPS).then_inc(consts, 1)
            pool.wait_ge(consts, 9)
            G.affine_select(out=ident[:], in_=ident[:], compare_op=ALU.not_equal, fill=1.0, base=0,
                            pattern=[[-1, P]], channel_multiplier=1).then_inc(consts, 1)
            pool.wait_ge(consts, 10)
            pool.wait_ge(small, 16 * SMALL)

            def norm_scalars(m):
                n = [0]

                def link(ins):
                    n[0] += 1
                    ins.then_inc(ln_step, 1)
                    pool.wait_ge(ln_step, m * (LN_OPS + 1) + n[0])

                pool.wait_ge(stats_step, 2 * TJ * (m + 1))
                pool.wait_ge(res_ready, TJ * m)
                mean, var = mv[:, :, 0], mv[:, :, 1]
                link(G.tensor_tensor(ln[:, 0], var, eps[:], ALU.add))
                link(G.tensor_tensor(ln[:, 1], ln[:, 0], minus_half[:], ALU.pow))
                link(G.tensor_tensor(ln[:, 2], var, ln[:, 1], ALU.mult))
                link(G.tensor_tensor(ln[:, 3], ln[:, 2], ln[:, 1], ALU.mult))
                link(G.tensor_tensor(ln[:, 4], ln[:, 3], minus_half[:], ALU.pow))
                link(G.tensor_tensor(ln[:, 5], ln[:, 1], ln[:, 4], ALU.mult))
                link(G.tensor_tensor(ln[:, 6], mean, ln[:, 1], ALU.mult))
                link(G.tensor_tensor(ln[:, 6], ln[:, 6], minus_one[:], ALU.mult))
                link(G.tensor_tensor(ln[:, 0], ln[:, 1], one[:], ALU.add))
                G.tensor_tensor(ln[:, 7], ln[:, 6], ln[:, 4], ALU.mult).then_inc(ln_step, 1)
                assert n[0] == LN_OPS

            def convolve(m):
                pool.wait_ge(soft_step, m)
                for h in range(2):
                    ch = slice(h * HALF, (h + 1) * HALF)
                    pool.wait_ge(emptied, FILLS * m + 4 + 2 * h)
                    for k in range(TAPS):
                        w = conv_w[:, ch, k:k + 1].broadcast_to([P, HALF, T])
                        G.tensor_tensor((t2 if k else t1)[:, ch], xc[:, ch, k:k + T], w, ALU.mult).then_inc(conv_step, 1)
                        if k:
                            pool.wait_ge(conv_step, CONV_OPS * (2 * m + h) + 2 * k)
                            G.tensor_tensor(t1[:, ch], t1[:, ch], t2[:, ch], ALU.add).then_inc(conv_step, 1)
                            pool.wait_ge(conv_step, CONV_OPS * (2 * m + h) + 2 * k + 1)

            def soft_correction(m):
                pool.wait_ge(soft_one, m + 1)
                G.tensor_tensor(yg[:], t1[:], yg[:], ALU.subtract).then_inc(soft_corr, 1)
                pool.wait_ge(soft_log, 2 * (m + 1))
                pool.wait_ge(soft_corr, 2 * m + 1)
                G.tensor_tensor(t1[:], yg[:], xc[:, :, TAPS - 1:], ALU.add).then_inc(soft_corr, 1)

            norm_scalars(0)
            soft_correction(0)
            norm_scalars(1)
            with pool.Fori(0, BATCH) as b:
                convolve(b + 1)
                soft_correction(b + 1)
                norm_scalars(b + 2)

        @block.scalar
        def _(act):
            A = nc.scalar
            act.wait_ge(small, 16 * SMALL)
            act.wait_ge(consts, 10)

            def settle():
                act.sem_inc(act_idle, 1)

            def prep_norm(m):
                act.wait_ge(ln_step, (LN_OPS + 1) * (m + 1))
                act.wait_ge(soft_step, m)
                for j in range(TJ):
                    A.activation(u[:, j], hin[:, j], ACT.Identity, scale=ln[:, 5, j:j + 1],
                                 bias=ln[:, 7, j:j + 1]).then_inc(u_ready, 1)

            def prep_u_t(m):
                for f in range(2):
                    act.wait_ge(filled, FILLS * m + f + 1)
                    for i in range(2):
                        kc = 2 * f + i
                        last = A.activation(u_t[:, kc], ps_p[:, f, i * T:(i + 1) * T], ACT.Copy, scale=norm_w[:, kc:kc + 1])
                    last.then_inc(emptied, 1)

            def prep_x(m, i):
                act.wait_ge(filled, FILLS * m + 3 + i)
                if i == 0:
                    act.wait_ge(soft_step, m)
                A.activation(xc[:, 2 * i:2 * i + 2, TAPS - 1:], ps_p[:, i % 2].rearrange("p (i t) -> p i t", i=2),
                             ACT.Copy).then_inc(emptied, 1)

            def prep_z(m, i):
                act.wait_ge(filled, FILLS * m + Z_FILLS[i] + 1)
                settle()
                A.activation(gate[:, bass.ds(m % 2, 1), 2 * i:2 * i + 2, :].rearrange("p o i t -> p (o i t)"),
                             ps_p[:, i % 2], ACT.Copy).then_inc(emptied, 1)

            def prep_res(m):
                act.wait_ge(h1_stored, 16 * m)
                act.wait_ge(u_ready, TJ * (m + 1))
                settle()
                for j in range(TJ):
                    A.activation(res[:, bass.ds(m % 2, 1), j, :].rearrange("p o d -> p (o d)"), hin[:, j], ACT.Identity,
                                 scale=ln[:, 0, j:j + 1], bias=ln[:, 6, j:j + 1]).then_inc(res_ready, 1)

            def prep_silu(m):
                act.wait_ge(conv_step, 2 * CONV_OPS * (m + 1))
                settle()
                for i in range(DI):
                    A.activation(xs[:, bass.ds(m % 2, 1), i, :].rearrange("p o t -> p (o t)"), t1[:, i], ACT.Silu,
                                 bias=conv_b[:, i:i + 1]).then_inc(xs_ready, 1)

            def gate_silu(b):
                act.wait_ge(emptied, FILLS * (b + 1))
                settle()
                g = gate[:, bass.ds(b % 2, 1)].rearrange("p o i t -> p (o i t)")
                A.activation(g, g, ACT.Silu).then_inc(gate_ready, 1)

            def prep_bc(m):
                act.wait_ge(filled, FILLS * m + 9)
                A.activation(dt_lr[:], ps_p[:, 0, 0:T], ACT.Copy).then_inc(emptied, 1)
                act.wait_ge(filled, FILLS * m + 10)
                act.wait_ge(b_stored, 16 * m)
                A.activation(bc_t[:], ps_p[:, 1, 0:T], ACT.Copy).then_inc(emptied, 1)

            def prep_c(m):
                act.wait_ge(c_turned, m + 1)
                settle()
                A.activation(bc_tok[:, bass.ds(m % 2, 1)].rearrange("p o j n -> p (o j) n"),
                             ps_p[:, 0, 0:TJ * P].rearrange("p (j r) -> p j r", j=TJ)[:, :, B0:],
                             ACT.Copy).then_inc(c_ready, 1)

            def prep_soft_arg(m, i):
                act.wait_ge(filled, FILLS * m + 11 + i)
                for k in range(2):
                    src = ps_p[:, i % 2, k * T:(k + 1) * T]
                    c = 2 * i + k
                    A.activation(t1[:, c], src, ACT.Abs, bias=b_dt[:, c:c + 1]).then_inc(soft_arg, 1)
                    ins = A.activation(t2[:, c], src, ACT.Relu, bias=b_dt[:, c:c + 1])
                    ins.then_inc(emptied if k else soft_arg, 1)

            def prep_soft_exp(m):
                act.wait_ge(soft_arg, 12 * (m + 1))
                A.activation(t1[:], t1[:], ACT.Exp, scale=-1.0).then_inc(soft_log, 1)

            def prep_soft_log(m):
                act.wait_ge(soft_log, 2 * m + 1)
                A.activation(xc[:, :, TAPS - 1:], t1[:], ACT.Ln, bias=1.0).then_inc(soft_log, 1)

            def exps(b, s):
                n, half = s // 2, s % 2
                act.wait_ge(scanned, STEPS * b + s + PRIME - DA_SLOTS + 1)
                if s == 0:
                    act.wait_ge(dt_ready, 2 * b + 1)
                for i in range(HALF):
                    c = half * HALF + i
                    A.activation(da[:, s % DA_SLOTS, i, 1:T], dt[:, c, 1:T], ACT.Exp, scale=a_w[:, c, n:n + 1]).then_inc(da_ready, 1)

            def start_sum(b, s):
                for j in range(TJ):
                    act.wait_ge(turned, TJ * (STEPS * b + s) + j + 1)
                    if s == 0 and j == 0:
                        act.wait_ge(y_turned, 4 * b + START)
                    act.wait_ge(c_ready, b + 1)
                    settle()
                    A.activation(y[:, j, s * SW // TJ:(s + 1) * SW // TJ], ps_h[:, s, j], ACT.Copy,
                                 scale=bc_tok[:, bass.ds(b % 2, 1), j, NS:NS + 1].rearrange("p o n -> p (o n)"))\
                        .then_inc(started, 1)

            def place_dtx_t(b):
                act.wait_ge(dtx_turned, b + 1)
                for j in range(TJ):
                    A.activation(dtx_t[:, j], ps_p[:, 2 + j], ACT.Copy).then_inc(diag_ready, 1)

            def place_diag(b, k):
                n = PE_STEPS[k] // 2
                if k >= 2:
                    act.wait_ge(pe_driven, len(PE_STEPS) * b + k - 1)
                settle()
                for j in range(TJ):
                    A.activation(b_diag[:, k % 2, j], ident[:], ACT.Copy,
                                 scale=bc_tok[:, bass.ds(b % 2, 1), j, n:n + 1].rearrange("p o n -> p (o n)"))\
                        .then_inc(diag_ready, 1)

            pieces = {1: [prep_norm], 3: [prep_u_t], 18: [prep_silu], 20: [prep_res], 22: [prep_bc], 23: [prep_c],
                      28: [prep_soft_exp], 30: [prep_soft_log]}
            for i in range(4):
                pieces.setdefault((5, 7, 9, 11)[i], []).append(lambda m, i=i: prep_x(m, i))
                pieces.setdefault((15, 16, 30, 31)[i], []).append(lambda m, i=i: prep_z(m, i))
                pieces.setdefault((25, 25, 27, 27)[i], []).append(lambda m, i=i: prep_soft_arg(m, i))
            for s in sorted(pieces):
                for piece in pieces[s]:
                    piece(0)
            with act.Fori(0, BATCH) as b:
                for s in range(STEPS):
                    exps(b, s)
                    if s == PE_STEPS[0] - 2:
                        place_diag(b, 0)
                    if s == PE_STEPS[0] + 1:
                        place_dtx_t(b)
                    if s - 1 in PE_STEPS[:-1]:
                        place_diag(b, PE_STEPS.index(s - 1) + 1)
                    if s == GATE:
                        gate_silu(b)
                    if s in (START_SUM, START_SUM + 1):
                        start_sum(b, s - START_SUM)
                    for piece in pieces.get(s, []):
                        piece(b + 1)

        @block.vector
        def _(dve):
            V = nc.vector
            dve.sem_inc(scanned, PRIME)
            dve.wait_ge(small, 16 * SMALL)
            dve.wait_ge(consts, 10)

            def prep_stats(m):
                dve.wait_ge(hin_loaded, 16 * (m + 1))
                dve.wait_ge(ln_step, (LN_OPS + 1) * m)
                for j in range(TJ):
                    V.bn_stats(stats[:, j], hin[:, j]).then_inc(stats_step, 1)
                dve.wait_ge(stats_step, 2 * TJ * m + TJ)
                dve.sem_inc(dve_idle, 1)
                for j in range(TJ):
                    V.bn_aggr(mv[:, j], stats[:, j]).then_inc(stats_step, 1)

            def soft_start(m):
                dve.wait_ge(soft_log, 2 * m + 1)
                if not isinstance(m, int):
                    dve.wait_ge(out_ready, TJ * m)
                V.tensor_scalar(yg[:], t1[:], 1.0, 1.0, ALU.add, ALU.subtract).then_inc(soft_one, 1)

            def step_size(m):
                dve.wait_ge(soft_corr, 2 * (m + 1))
                V.tensor_tensor(dt[:], t2[:], t1[:], ALU.add).then_inc(dt_ready, 1)

            def weigh_input(m):
                dve.wait_ge(xs_ready, DI * (m + 1))
                dve.wait_ge(dt_ready, 2 * m + 1)
                dve.sem_inc(soft_step, 1)
                V.tensor_tensor(dtx[:], dt[:], xs[:, bass.ds(m % 2, 1)].rearrange("p o i t -> p (o i) t"),
                                ALU.mult).then_inc(dt_ready, 1)

            def drive(b, s):
                n, half = s // 2, s % 2
                if s in PE_STEPS:
                    return
                if s == 0:
                    dve.wait_ge(dt_ready, 2 * b + 2)
                if s % (2 * BG) == 0:
                    g = s // (2 * BG)
                    dve.wait_ge(b_loaded[g % 2], 16 * (GROUPS // 2 * b + g // 2 + 1))
                dve.wait_ge(scanned, STEPS * b + s + PRIME - 1)
                V.tensor_tensor(dbx[:, s % 2], dtx[:, half * HALF:(half + 1) * HALF],
                                b_all[:, n // BG % 2, n % BG].unsqueeze(1).broadcast_to([P, HALF, T]),
                                ALU.mult).then_inc(dbx_ready, 1)

            def scan(b, s):
                if s in PE_STEPS:
                    dve.wait_ge(pe_driven, len(PE_STEPS) * b + PE_STEPS.index(s) + 1)
                    drive_in = ps_p[:, 2:4].rearrange("p k t -> p (k t)")
                else:
                    dve.wait_ge(dbx_ready, len(DVE_STEPS) * b + DVE_STEPS.index(s) + 1)
                    drive_in = dbx[:, s % 2].rearrange("p i t -> p (i t)")
                dve.wait_ge(da_ready, HALF * (STEPS * b + s + 1))
                if s >= 2:
                    dve.wait_ge(turned, TJ * (STEPS * b + s - 1))
                V.tensor_tensor_scan(hs[:, s % 2].rearrange("p i t -> p (i t)"), da[:, s % DA_SLOTS].rearrange("p i t -> p (i t)"),
                                     drive_in, 0.0, ALU.mult, ALU.add)\
                    .then_inc(scanned, 1)

            def weigh(b, s, j):
                n, half = s // 2, s % 2
                if n == 0:
                    return
                dve.wait_ge(turned, TJ * (STEPS * b + s) + j + 1)
                out = y[:, j, half * SW // TJ:(half + 1) * SW // TJ]
                c = bc_tok[:, bass.ds(b % 2, 1), j, NS + n:NS + n + 1].rearrange("p o n -> p (o n)")
                if n == 1:
                    dve.wait_ge(started, TJ * (2 * b + s - 2) + j + 1)
                else:
                    dve.wait_ge(summed, TJ * (SUMS * b + s - 4) + j + 1)
                V.scalar_tensor_tensor(out, ps_h[:, s % 2, j], c, out, ALU.mult, ALU.add).then_inc(summed, 1)

            def gate_y(b):
                for i in range(DI):
                    if i % 2 == 0:
                        dve.wait_ge(y_turned, 4 * b + i // 2 + 1 + START)
                    if i == 0:
                        dve.wait_ge(out_ready, TJ * (b + 1))
                    V.scalar_tensor_tensor(yg[:, i], xs[:, bass.ds(b % 2, 1), i, :].rearrange("p o t -> p (o t)"),
                                           d_w[:, i:i + 1], ps_p[:, i // 2, i % 2 * T:(i % 2 + 1) * T],
                                           ALU.mult, ALU.add).then_inc(gated, 1)
                dve.wait_ge(gate_ready, b + 1)
                dve.wait_ge(gated, (DI + 1) * b + DI + START)
                V.tensor_tensor(yg[:], yg[:], gate[:, bass.ds(b % 2, 1)].rearrange("p o i t -> p (o i) t"),
                                ALU.mult).then_inc(gated, 1)

            def add_res(b, j):
                dve.wait_ge(out_ready, TJ * b + j + 1)
                r = res[:, bass.ds((b + 1) % 2, 1), j, :].rearrange("p o d -> p (o d)")
                V.tensor_tensor(r, ps_p[:, 2 + j], r, ALU.add).then_inc(h1_ready, 1)

            def first_convolve():
                n = 0
                for i in range(DI):
                    if i % 2 == 0:
                        dve.wait_ge(emptied, 3 + i // 2)
                    V.tensor_scalar(t1[:, i], xc[:, i, 0:T], conv_w[:, i, 0:1], None, ALU.mult).then_inc(first_step, 1)
                    for k in range(1, TAPS):
                        n += 1
                        dve.wait_ge(first_step, n)
                        V.scalar_tensor_tensor(t1[:, i], xc[:, i, k:k + T], conv_w[:, i, k:k + 1], t1[:, i],
                                               ALU.mult, ALU.add).then_inc(first_step, 1)
                    n += 1
                dve.wait_ge(first_step, TAPS * DI)
                dve.sem_inc(conv_step, 2 * CONV_OPS)

            prep_stats(0)
            first_convolve()
            soft_start(0)
            step_size(0)
            weigh_input(0)
            prep_stats(1)
            dve.sem_inc(gated, START)
            with dve.Fori(0, BATCH) as b:
                for s in range(STEPS):
                    drive(b, s)
                    if s >= 2:
                        weigh(b, s - 2, 0)
                    scan(b, s)
                    if s >= 2:
                        weigh(b, s - 2, 1)
                    if s == SOFT:
                        soft_start(b + 1)
                    if s == PROJECT[1] + 2:
                        add_res(b, 0)
                    if s == PROJECT[3] + 2:
                        add_res(b, 1)
                weigh(b, STEPS - 2, 0)
                weigh(b, STEPS - 2, 1)
                step_size(b + 1)
                weigh(b, STEPS - 1, 0)
                weigh(b, STEPS - 1, 1)
                weigh_input(b + 1)
                prep_stats(b + 2)
                gate_y(b)
            for j in range(TJ):
                add_res(BATCH, j)

        @block.tensor
        def _(pe):
            M = nc.tensor.matmul
            for signal in (y_turned,):
                pe.sem_inc(signal, START)
            pe.wait_ge(consts, 10)

            def fill_wait(m, f):
                if f < 2:
                    return
                if f == 10:
                    pe.wait_ge(c_ready, m + 1)
                else:
                    pe.wait_ge(emptied, FILLS * m + f - 1)

            def fill_u(m):
                pe.wait_ge(u_ready, TJ * (m + 1))
                for f in range(2):
                    fill_wait(m, f)
                    for i in range(2):
                        kc = 2 * f + i
                        for j in range(TJ):
                            last = nc.tensor.transpose(ps_p[:, f, i * T + j * P:i * T + (j + 1) * P],
                                                       u[:, j, kc * P:(kc + 1) * P], ident[:])
                    last.then_inc(filled, 1)

            def fill_in(m, i):
                f = 2 + i if i < 4 else Z_FILLS[i - 4]
                if i == 0:
                    pe.wait_ge(emptied, FILLS * m + 2)
                fill_wait(m, f)
                for k in range(2):
                    r = (2 * i + k) * P
                    for kc in range(KC):
                        last = M(ps_p[:, i % 2, k * T:(k + 1) * T], w_in[:, kc, r:r + P], u_t[:, kc],
                                 start=(kc == 0), stop=(kc == KC - 1))
                last.then_inc(filled, 1)

            def fill_x(m, f):
                pe.wait_ge(xs_ready, DI * (m + 1))
                r = (0, WX - P)[f]
                fill_wait(m, 8 + f)
                for i in range(DI):
                    last = M(ps_p[:, f, 0:T], w_x[:, i, r:r + P],
                             xs[:, bass.ds(m % 2, 1), i, :].rearrange("p o t -> p (o t)"),
                             start=(i == 0), stop=(i == DI - 1))
                last.then_inc(filled, 1)

            def turn_c(m):
                pe.wait_ge(emptied, FILLS * m + 10)
                for j in range(TJ):
                    last = nc.tensor.transpose(ps_p[:, 0, j * P:(j + 1) * P], bc_t[:, j * P:(j + 1) * P], ident[:])
                last.then_inc(c_turned, 1)

            def fill_dt(m, i):
                fill_wait(m, 10 + i)
                for k in range(2):
                    c = 2 * i + k
                    last = M(ps_p[:, i % 2, k * T:(k + 1) * T], w_dt[:, c * P:(c + 1) * P], dt_lr[:], start=True, stop=True)
                last.then_inc(filled, 1)

            def turn(b, s):
                pe.wait_ge(scanned, STEPS * b + s + 1 + PRIME)
                for j in range(TJ):
                    if s in (2, 3):
                        pe.wait_ge(started, TJ * (2 * b + s - 2) + j + 1)
                    elif s > 3:
                        pe.wait_ge(summed, TJ * (SUMS * b + s - 4) + j + 1)
                    for i in range(HALF):
                        last = nc.tensor.transpose(ps_h[:, s % 2, j, i * P:(i + 1) * P], hs[:, s % 2, i, j * P:(j + 1) * P],
                                                   ident[:])
                    last.then_inc(turned, 1)

            def turn_y(b):
                pe.wait_ge(summed, TJ * SUMS * (b + 1))
                pe.wait_ge(emptied, FILLS * (b + 2))
                pe.wait_ge(h1_ready, TJ * (b + 1))
                for i in range(DI):
                    for j in range(TJ):
                        last = nc.tensor.transpose(ps_p[:, i // 2, i % 2 * T + j * P:i % 2 * T + (j + 1) * P],
                                                   y[:, j, i * P:(i + 1) * P], ident[:])
                    if i % 2:
                        last.then_inc(y_turned, 1)

            def project_out(b, j, part):
                if j == 0 and part == 0:
                    pe.wait_ge(gated, (DI + 1) * b + START)
                for i in range(part * DI // 2, (part + 1) * DI // 2):
                    last = M(ps_p[:, 2 + j], yg[:, i, j * P:(j + 1) * P], w_out[:, i], start=(i == 0), stop=(i == DI - 1))
                if part:
                    last.then_inc(out_ready, 1)

            def turn_dtx(b):
                pe.wait_ge(h1_ready, TJ * (b + 1))
                pe.wait_ge(dt_ready, 2 * b + 2)
                for j in range(TJ):
                    for i in range(HALF):
                        last = nc.tensor.transpose(ps_p[:, 2 + j, i * P:(i + 1) * P], dtx[:, HALF + i, j * P:(j + 1) * P],
                                                   ident[:])
                last.then_inc(dtx_turned, 1)

            def pe_drive(b, k):
                pe.wait_ge(diag_ready, TJ * ((len(PE_STEPS) + 1) * b + k + 2))
                if k:
                    pe.wait_ge(scanned, STEPS * b + PE_STEPS[k - 1] + 1 + PRIME)
                for i in range(HALF):
                    for j in range(TJ):
                        last = M(ps_p[:, 2 + i // 2, i % 2 * T + j * P:i % 2 * T + (j + 1) * P],
                                 dtx_t[:, j, i * P:(i + 1) * P], b_diag[:, k % 2, j], start=True, stop=True)
                last.then_inc(pe_driven, 1)

            pieces = {1: [fill_u], 17: [lambda m: fill_x(m, 0)], 19: [lambda m: fill_x(m, 1)], 21: [turn_c]}
            for i in range(8):
                pieces.setdefault((4, 6, 8, 9, 12, 13, 26, 28)[i], []).append(lambda m, i=i: fill_in(m, i))
            for i in range(4):
                pieces.setdefault((21, 22, 23, 24)[i], []).append(lambda m, i=i: fill_dt(m, i))
            for k, s in enumerate(PROJECT):
                pieces.setdefault(s, []).append(lambda m, k=k: project_out(m - 1, k // 2, k % 2))
            for s in sorted(pieces):
                if s == 4:
                    pe.wait_ge(w_in_loaded[0], 16)
                if s == 12:
                    pe.wait_ge(w_in_loaded[1], 16)
                if s == 17:
                    pe.wait_ge(weights, 16 * LOADS)
                for piece in pieces[s]:
                    if s not in PROJECT:
                        piece(0)
            with pe.Fori(0, BATCH) as b:
                for s in range(STEPS):
                    if s == PE_STEPS[0] - 3:
                        turn_dtx(b)
                    if s + 1 in PE_STEPS:
                        pe_drive(b, PE_STEPS.index(s + 1))
                    for piece in pieces.get(s, []):
                        piece(b + 1)
                    turn(b, s)
                turn_y(b)
            for j in range(TJ):
                for part in range(2):
                    project_out(BATCH, j, part)


def expert_stage(nc, io, h1_scratch, out):
    BATCH, T, D = out.shape
    KC = D // P
    TJ = T // P
    NT = BATCH * TJ
    E = io["sim"].shape[1] // KC
    HD = P
    W3 = 3 * HD
    SCALE = 1.0 / math.sqrt(HD)
    NEG = -1e9

    with ExitStack() as outer:
        def sb_in(stack, name, shape, dt=F32):
            return stack.enter_context(nc.sbuf_tensor(name, shape, dt))

        def sem(name):
            return outer.enter_context(nc.semaphore(name))

        w = sb_in(outer, "ff_w", [P, NT, E])
        ident = sb_in(outer, "ff_ident", [P, P])
        consts = sem("ff_consts")
        done_experts = sem("ff_done_experts")
        act_idle, pool_idle, dve_idle, sp_idle = (sem(f"ff_idle_{n}") for n in ("act", "pool", "dve", "sp"))
        qkv = sb_in(outer, "ff_qkv", [P, NT, W3])

        with ExitStack() as mid:
            x_hi = sb_in(mid, "ff_x_hi", [P, KC, NT, P], F32R)
            x_lo = sb_in(mid, "ff_x_lo", [P, KC, NT, P], F32R)
            rank = sb_in(mid, "ff_rank", [P, E])
            col = sb_in(mid, "ff_col", [P, 4, NT])

            with ExitStack() as ctx:
                ps = ctx.enter_context(nc.psum_tensor("ff_ps1", [P, 8, 512], F32))

                def sb(name, shape, dt=F32):
                    return sb_in(ctx, name, shape, dt)

                HIN = 4
                minus_half = sb("ff_minus_half", [P, E])
                minus_one = sb("ff_minus_one", [P, TJ])
                width = sb("ff_width", [P, TJ])
                eps = sb("ff_eps", [P, TJ])
                ones = sb("ff_ones", [P, P])
                rank_i = sb("ff_rank_i", [P, E], I32)
                sim = sb("ff_sim", [P, KC, E])
                sim_sq = sb("ff_sim_sq", [P, KC, E])
                sim_rn = sb("ff_sim_rn", [P, E])
                sim_hi = sb("ff_sim_hi", [P, KC, E], F32R)
                sim_lo = sb("ff_sim_lo", [P, KC, E], F32R)
                gates = sb("ff_gates", [P, E])
                hin = sb("ff_hin", [P, HIN, TJ, D])
                stats = sb("ff_stats", [P, HIN, TJ, 6])
                mv = sb("ff_mv", [P, HIN, TJ, 2])
                ln = sb("ff_ln", [P, HIN, 4, TJ])
                xn = sb("ff_xn", [P, 2, TJ, D])
                rn = sb("ff_rn", [P, NT])
                logits_t = qkv[0:E, :, 0:P]

                loaded = sem("ff_loaded")
                hin_loaded = [sem(f"ff_hin_loaded{i}") for i in range(HIN)]
                stats_step = sem("ff_stats_step")
                ln_step = sem("ff_ln_step")
                scalars_ready = sem("ff_scalars_ready")
                xn_ready = sem("ff_xn_ready")
                filled = sem("ff_filled")
                hi_ready = sem("ff_hi_ready")
                lo_ready = sem("ff_lo_ready")
                sim_step = sem("ff_sim_step")
                sim_summed = sem("ff_sim_summed")
                sim_norm = sem("ff_sim_norm")
                gate_step = sem("ff_gate_step")
                logits_ready = sem("ff_logits_ready")
                logits_copied = sem("ff_logits_copied")
                logits_turned = sem("ff_logits_turned")
                logits_done = sem("ff_logits_done")
                LN_OPS = 8

                def batches(eng, step):
                    for q in range(HIN):
                        step(q, q)
                    with eng.Fori(1, BATCH // HIN - 1) as turn:
                        for q in range(HIN):
                            step(HIN * turn + q, q)
                    for q in range(HIN):
                        step(BATCH - HIN + q, q)

                def late(m, slots=2):
                    return not isinstance(m, int) or m >= slots

                block = ctx.enter_context(nc.Block())

                @block.sync
                def _(sp):
                    sp.dma_start(sim[:].rearrange("p k e -> p (k e)"), io["sim"]).then_inc(loaded, 16)
                    sp.dma_start(gates[:], io["gates"].partition_broadcast(P)).then_inc(loaded, 16)

                    def load(m, q):
                        row = bass.ds(m + 1 if isinstance(m, int) else sp.snap(m + 1), 1)
                        if late(m, HIN):
                            sp.wait_ge(xn_ready, TJ * (m - HIN + 1))
                            sp.sem_inc(sp_idle, 1)
                        sp.dma_start(hin[:, q], h1_scratch[row]
                                     .rearrange("o (j p) d -> (o p) j d", p=P)).then_inc(hin_loaded[q], 16)

                    batches(sp, load)

                @block.gpsimd
                def _(pool):
                    G = nc.gpsimd
                    G.memset(ident[:], 0.0).then_inc(consts, 1)
                    G.memset(ones[:], 1.0).then_inc(consts, 1)
                    G.memset(minus_half[:], -0.5).then_inc(consts, 1)
                    G.memset(minus_one[:], -1.0).then_inc(consts, 1)
                    G.memset(width[:], float(D)).then_inc(consts, 1)
                    G.memset(eps[:], EPS).then_inc(consts, 1)
                    G.iota(rank_i[:], pattern=[[-1, E]], base=E, channel_multiplier=0).then_inc(consts, 1)
                    pool.wait_ge(consts, 7)
                    G.affine_select(out=ident[:], in_=ident[:], compare_op=ALU.not_equal, fill=1.0, base=0,
                                    pattern=[[-1, P]], channel_multiplier=1).then_inc(consts, 1)
                    G.tensor_copy(rank[:], rank_i[:]).then_inc(consts, 1)
                    pool.wait_ge(consts, 9)
                    pool.wait_ge(sim_step, 2)
                    G.tensor_tensor(sim_rn[:], sim_rn[:], minus_half[:, 0:E], ALU.pow).then_inc(sim_norm, 1)

                    def scalars(m, q):
                        n = [0]

                        def link(ins):
                            n[0] += 1
                            ins.then_inc(ln_step, 1)
                            pool.wait_ge(ln_step, m * LN_OPS + n[0])

                        pool.wait_ge(stats_step, 2 * TJ * (m + 1))
                        if late(m, HIN):
                            pool.wait_ge(xn_ready, TJ * (m - HIN + 1))
                        pool.sem_inc(pool_idle, 1)
                        mean, var = mv[:, q, :, 0], mv[:, q, :, 1]
                        half = minus_half[:, 0:TJ]
                        link(G.tensor_tensor(ln[:, q, 0], var, eps[:], ALU.add))
                        link(G.tensor_tensor(ln[:, q, 0], ln[:, q, 0], half, ALU.pow))
                        link(G.tensor_tensor(ln[:, q, 1], mean, ln[:, q, 0], ALU.mult))
                        link(G.tensor_tensor(ln[:, q, 1], ln[:, q, 1], minus_one[:, 0:TJ], ALU.mult))
                        pool.sem_inc(scalars_ready, 1)
                        link(G.tensor_tensor(ln[:, q, 2], var, ln[:, q, 0], ALU.mult))
                        link(G.tensor_tensor(ln[:, q, 2], ln[:, q, 2], ln[:, q, 0], ALU.mult))
                        link(G.tensor_tensor(ln[:, q, 2], ln[:, q, 2], width[:, 0:TJ], ALU.mult))
                        pool.sem_inc(pool_idle, 1)
                        link(G.tensor_tensor(rn[:, bass.ds(m * TJ, TJ)], ln[:, q, 2], half, ALU.pow))
                        assert n[0] == LN_OPS

                    batches(pool, scalars)

                @block.scalar
                def _(act):
                    A = nc.scalar
                    act.wait_ge(loaded, 32)
                    act.wait_ge(consts, 9)
                    A.activation(gates[:], gates[:], ACT.Exp, scale=-1.0).then_inc(gate_step, 1)
                    act.wait_ge(sim_step, 3)
                    A.activation(sim_hi[:], sim_sq[:], ACT.Copy).then_inc(sim_norm, 1)

                    def norm(m, q):
                        o = q % 2
                        act.wait_ge(scalars_ready, m + 1)
                        if late(m):
                            act.wait_ge(filled, TJ * (m - 1))
                        for j in range(TJ):
                            A.activation(xn[:, o, j], hin[:, q, j], ACT.Identity, scale=ln[:, q, 0, j:j + 1],
                                         bias=ln[:, q, 1, j:j + 1]).then_inc(xn_ready, 1)

                    def place(m, o):
                        for j in range(TJ):
                            act.wait_ge(filled, TJ * m + j + 1)
                            act.sem_inc(act_idle, 1)
                            A.activation(x_hi[:, :, bass.ds(m * TJ + j, 1), :].rearrange("p k o t -> p (k o) t"),
                                         ps[:, o * TJ + j].rearrange("p (k t) -> p k t", k=KC),
                                         ACT.Copy).then_inc(hi_ready, 1)

                    def copy_logits(m, o):
                        act.wait_ge(logits_ready, m + 1)
                        act.sem_inc(act_idle, 1)
                        A.activation(logits_t[:, bass.ds(TJ * m, TJ), :],
                                     ps[0:E, 2 * TJ + o, 0:T].rearrange("p (j t) -> p j t", j=TJ),
                                     ACT.Copy).then_inc(logits_copied, 1)

                    def step(m, q):
                        o = q % 2
                        if not isinstance(m, int) or m + 1 < BATCH:
                            norm(m + 1, (q + 1) % HIN)
                        place(m, o)
                        if not isinstance(m, int) or m > 0:
                            copy_logits(m - 1, 1 - o)

                    norm(0, 0)
                    batches(act, step)
                    copy_logits(BATCH - 1, 1)

                @block.vector
                def _(dve):
                    V = nc.vector
                    dve.wait_ge(loaded, 32)
                    dve.wait_ge(consts, 9)
                    V.tensor_tensor(sim_sq[:], sim[:], sim[:], ALU.mult).then_inc(sim_step, 1)
                    dve.wait_ge(sim_summed, 1)
                    V.tensor_scalar(sim_rn[:], ps[:, 0, 0:E], 1e-24, None, ALU.max).then_inc(sim_step, 1)
                    dve.wait_ge(sim_norm, 1)
                    V.tensor_tensor(sim_sq[:], sim[:], sim_rn[:].unsqueeze(1).broadcast_to([P, KC, E]),
                                    ALU.mult).then_inc(sim_step, 1)
                    dve.wait_ge(sim_norm, 2)
                    V.tensor_tensor(sim_lo[:], sim_sq[:], sim_hi[:].bitcast(F32), ALU.subtract).then_inc(sim_step, 1)
                    dve.wait_ge(gate_step, 1)
                    V.tensor_scalar(gates[:], gates[:], 1.0, None, ALU.add).then_inc(gate_step, 1)
                    dve.wait_ge(gate_step, 2)
                    V.reciprocal(gates[:], gates[:]).then_inc(gate_step, 1)

                    def moments(m, q):
                        dve.wait_ge(hin_loaded[q], 16 // HIN * (m - q) + 16)
                        if late(m, HIN):
                            dve.wait_ge(ln_step, LN_OPS * (m - HIN + 1))
                        for j in range(TJ):
                            V.bn_stats(stats[:, q, j], hin[:, q, j]).then_inc(stats_step, 1)
                        dve.wait_ge(stats_step, 2 * TJ * m + TJ)
                        dve.sem_inc(dve_idle, 1)
                        for j in range(TJ):
                            V.bn_aggr(mv[:, q, j], stats[:, q, j]).then_inc(stats_step, 1)

                    def place_rest(m, o):
                        for j in range(TJ):
                            tile = m * TJ + j
                            dve.wait_ge(hi_ready, tile + 1)
                            V.tensor_tensor(x_lo[:, :, bass.ds(tile, 1), :].rearrange("p k o t -> p (k o) t"),
                                            ps[:, o * TJ + j].rearrange("p (k t) -> p k t", k=KC),
                                            x_hi[:, :, bass.ds(tile, 1), :].rearrange("p k o t -> p (k o) t").bitcast(F32),
                                            ALU.subtract).then_inc(lo_ready, 1)

                    def step(m, q):
                        if not isinstance(m, int) or m + 2 < BATCH:
                            moments(m + 2, (q + 2) % HIN)
                        place_rest(m, q % 2)

                    moments(0, 0)
                    moments(1, 1)
                    batches(dve, step)
                    dve.wait_ge(ln_step, LN_OPS * BATCH)
                    dve.wait_ge(logits_turned, 1)
                    V.tensor_tensor(w[:], ps[:, 7].rearrange("p (t e) -> p t e", e=E),
                                    rn[:].unsqueeze(2).broadcast_to([P, NT, E]), ALU.mult).then_inc(logits_done, 1)
                    dve.wait_ge(logits_done, 1)
                    V.tensor_tensor(w[:], w[:], gates[:].unsqueeze(1).broadcast_to([P, NT, E]),
                                    ALU.subtract).then_inc(logits_done, 1)

                @block.tensor
                def _(pe):
                    pe.wait_ge(consts, 9)
                    pe.wait_ge(sim_step, 1)
                    for k in range(KC):
                        last = nc.tensor.matmul(ps[:, 0, 0:E], ones[:], sim_sq[:, k], start=(k == 0), stop=(k == KC - 1))
                    last.then_inc(sim_summed, 1)
                    pe.wait_ge(sim_step, 4)

                    def turn(m, o):
                        for j in range(TJ):
                            pe.wait_ge(xn_ready, TJ * m + j + 1)
                            if late(m):
                                pe.wait_ge(lo_ready, TJ * (m - 1))
                            for k in range(KC):
                                last = nc.tensor.transpose(ps[:, o * TJ + j, k * P:(k + 1) * P],
                                                           xn[:, o, j, k * P:(k + 1) * P], ident[:])
                            last.then_inc(filled, 1)

                    def multiply(m, o):
                        pe.wait_ge(lo_ready, TJ * (m + 1))
                        if late(m):
                            pe.wait_ge(logits_copied, m - 1)
                        first = True
                        for a, x in ((sim_hi, x_hi), (sim_lo, x_hi), (sim_hi, x_lo)):
                            for k in range(KC):
                                last = nc.tensor.matmul(ps[0:E, 2 * TJ + o, 0:T], a[:, k],
                                                        x[:, k, bass.ds(TJ * m, TJ), :].rearrange("p j t -> p (j t)"),
                                                        start=first, stop=(x is x_lo and k == KC - 1))
                                first = False
                        last.then_inc(logits_ready, 1)

                    def step(m, q):
                        o = q % 2
                        if not isinstance(m, int) or m + 1 < BATCH:
                            turn(m + 1, 1 - o)
                        multiply(m, o)

                    turn(0, 0)
                    batches(pe, step)
                    pe.wait_ge(logits_copied, BATCH)
                    for i in range(NT):
                        last = nc.tensor.transpose(ps[:, 7, i * E:(i + 1) * E], logits_t[:, i], ident[0:E, 0:E])
                    last.then_inc(logits_turned, 1)

            with ExitStack() as ctx:
                ps = ctx.enter_context(nc.psum_tensor("ff_ps2", [P, 8, 512], F32))
                KH = KC // 2
                raw = sb_in(ctx, "ff_raw", [P, KH, W3])
                e_hi = sb_in(ctx, "ff_e_hi", [P, 2, KC, W3], F32R)
                e_lo = sb_in(ctx, "ff_e_lo", [P, 2, KC, W3], F32R)
                raw_loaded = sem("ff_raw_loaded")
                raw_hi = sem("ff_raw_hi")
                raw_lo = sem("ff_raw_lo")
                route_step = sem("ff_route_step")
                route_exp = sem("ff_route_exp")
                cleared = sem("ff_cleared")
                ROUTE_EXP = 25
                room = [t[:, 1].bitcast(F32).rearrange("p k n -> p (k n)") for t in (e_hi, e_lo)]
                r = [room[i // 3][:, i % 3 * NT * E:(i % 3 + 1) * NT * E].rearrange("p (t e) -> p t e", e=E)
                     for i in range(5)]
                mixed = sem("ff_mixed")
                added = sem("ff_added")
                BANKS = 8
                block = ctx.enter_context(nc.Block())

                @block.sync
                def _(sp):
                    for signal in (raw_lo,):
                        sp.sem_inc(signal, START)
                    with sp.Fori(0, E) as e:
                        for h in range(2):
                            cols = bass.ds(sp.snap((2 * e + h) * KH * W3), KH * W3)
                            sp.wait_ge(raw_lo, 2 * e + h + START)
                            sp.dma_start(raw[:].rearrange("p k n -> p (k n)"),
                                         io["w_qkv"][:, cols]).then_inc(raw_loaded, 16)

                @block.gpsimd
                def _(pool):
                    nc.gpsimd.memset(qkv[:], 0.0).then_inc(cleared, 1)
                    pool.wait_ge(cleared, 1)

                @block.scalar
                def _(act):
                    def high(e, h):
                        act.wait_ge(raw_loaded, 16 * (2 * e + h + 1))
                        act.wait_ge(done_experts, e + 1)
                        act.sem_inc(act_idle, 1)
                        nc.scalar.activation(e_hi[:, bass.ds(e % 2, 1), h * KH:(h + 1) * KH].rearrange("p o k n -> p (o k) n"),
                                             raw[:], ACT.Copy).then_inc(raw_hi, 1)

                    high(0, 0)
                    high(0, 1)
                    act.wait_ge(route_step, ROUTE_EXP)
                    nc.scalar.activation(r[0], r[0], ACT.Exp).then_inc(route_exp, 1)
                    act.wait_ge(route_step, ROUTE_EXP + 4)
                    with act.Fori(1, E) as e:
                        for h in range(2):
                            high(e, h)

                @block.vector
                def _(dve):
                    V = nc.vector
                    dve.sem_inc(added, BANKS)

                    def split(e, h):
                        dve.wait_ge(raw_hi, 2 * e + h + 1)
                        hi = e_hi[:, bass.ds(e % 2, 1), h * KH:(h + 1) * KH].rearrange("p o k n -> p (o k) n")
                        lo = e_lo[:, bass.ds(e % 2, 1), h * KH:(h + 1) * KH].rearrange("p o k n -> p (o k) n")
                        V.tensor_tensor(lo, raw[:], hi.bitcast(F32), ALU.subtract).then_inc(raw_lo, 1)

                    def add(e, i):
                        dve.wait_ge(mixed, NT * e + i + 1)
                        V.scalar_tensor_tensor(qkv[:, i], ps[:, i % BANKS, 0:W3], w[:, i, bass.ds(e, 1)], qkv[:, i],
                                               ALU.mult, ALU.add).then_inc(added, 1)

                    split(0, 0)
                    split(0, 1)
                    n = [0]

                    def link(ins):
                        n[0] += 1
                        ins.then_inc(route_step, 1)
                        dve.wait_ge(route_step, n[0])

                    def by_token(x):
                        return x.unsqueeze(2).broadcast_to([P, NT, E])

                    def by_expert(x):
                        return x.unsqueeze(1).broadcast_to([P, NT, E])

                    logits, gated, mask, pick, key = r
                    first, top, none = col[:, 0], col[:, 1], col[:, 2]
                    link(V.tensor_copy(logits, w[:]))
                    link(V.tensor_scalar(mask, logits, 0.0, None, ALU.is_gt))
                    link(V.tensor_scalar(gated, logits, 0.0, None, ALU.max))
                    link(V.tensor_reduce(none, mask, AX.X, ALU.max))
                    link(V.tensor_scalar(none, none, -1.0, 1.0, ALU.mult, ALU.add))
                    for k in range(2):
                        link(V.tensor_reduce(top, logits, AX.X, ALU.max))
                        link(V.tensor_tensor(key, logits, by_token(top), ALU.is_equal))
                        link(V.tensor_tensor(key, key, by_expert(rank[:]), ALU.mult))
                        link(V.tensor_reduce(first, key, AX.X, ALU.max))
                        link(V.tensor_tensor(key, by_expert(rank[:]), by_token(first), ALU.is_equal))
                        if k == 0:
                            link(V.tensor_copy(pick, key))
                            link(V.scalar_tensor_tensor(logits, key, -1e30, logits, ALU.mult, ALU.add))
                    link(V.tensor_tensor(pick, pick, key, ALU.add))
                    link(V.tensor_tensor(pick, pick, by_token(none), ALU.mult))
                    link(V.tensor_tensor(mask, mask, pick, ALU.add))
                    link(V.tensor_tensor(gated, gated, mask, ALU.mult))
                    link(V.tensor_scalar(key, mask, 1.0, -NEG, ALU.subtract, ALU.mult))
                    link(V.tensor_tensor(gated, gated, key, ALU.add))
                    link(V.tensor_reduce(top, gated, AX.X, ALU.max))
                    link(V.tensor_tensor(logits, gated, by_token(top), ALU.subtract))
                    assert n[0] == ROUTE_EXP, n[0]
                    dve.wait_ge(route_exp, 1)
                    link(V.tensor_reduce(top, logits, AX.X, ALU.add))
                    link(V.reciprocal(first, top))
                    link(V.tensor_tensor(logits, logits, mask, ALU.mult))
                    link(V.tensor_tensor(w[:], logits, by_token(first), ALU.mult))
                    dve.wait_ge(route_step, n[0])
                    dve.wait_ge(cleared, 1)
                    with dve.Fori(0, E - 1) as e:
                        for i in range(NT):
                            if i in (4, 8):
                                split(e + 1, i // 4 - 1)
                            add(e, i)
                    for i in range(NT):
                        add(E - 1, i)

                @block.tensor
                def _(pe):
                    pe.sem_inc(done_experts, 2)
                    with pe.Fori(0, E) as e:
                        pe.wait_ge(raw_lo, 2 * e + 2 + START)
                        for i in range(NT):
                            pe.wait_ge(added, NT * e + i + 1)
                            first = True
                            for a, s in ((x_hi, e_hi), (x_hi, e_lo), (x_lo, e_hi)):
                                for k in range(KC):
                                    last = nc.tensor.matmul(ps[:, i % BANKS, 0:W3], a[:, k, i],
                                                            s[:, bass.ds(e % 2, 1), k, :].rearrange("p o n -> p (o n)"),
                                                            start=first, stop=(a is x_lo and k == KC - 1))
                                    first = False
                            last.then_inc(mixed, 1)
                        pe.wait_ge(mixed, NT * (e + 1))
                        pe.sem_inc(done_experts, 1)

        with ExitStack() as ctx:
            def sb(name, shape, dt=F32):
                return sb_in(ctx, name, shape, dt)

            EL = 4
            PRODUCTS = TJ * E
            BANKS = 4
            ACT_P = [i for i in range(PRODUCTS) if i // TJ % 4 == 1]
            DVE_P = [i for i in range(PRODUCTS) if i not in ACT_P]
            SIDE = len(ACT_P) - TJ
            FREE = TJ + START
            ps_o = ctx.enter_context(nc.psum_tensor("ff_ps_o", [P, BANKS, 512], F32))
            ps_a = ctx.enter_context(nc.psum_tensor("ff_ps_a", [P, 4, 512], F32))
            o_raw = sb("ff_o_raw", [P, E, D])
            o_hi = sb("ff_o_hi", [P, E, D], F32R)
            o_lo = sb("ff_o_lo", [P, E, D], F32R)
            keep = sb("ff_keep", [P, 3 * P])
            hide = sb("ff_hide", [P, 3 * P])
            now = sb("ff_now", [P, TJ, W3])
            qk_t = sb("ff_qk_t", [P, 2, T])
            score = sb("ff_score", [P, 3 * P])
            prob = sb("ff_prob", [P, 3 * P])
            prob_t = sb("ff_prob_t", [P, 3 * P])
            top = sb("ff_top", [P, TJ])
            total = sb("ff_total", [P, TJ])
            head_hi = sb("ff_head_hi", [P, 2, T], F32R)
            head_lo = sb("ff_head_lo", [P, 2, T], F32R)
            h1 = sb("ff_h1", [P, 2, TJ, D])
            side = sb("ff_side", [P, 2, TJ, D])
            scaled = sb("ff_scaled", [P, TJ, D])
            o_loaded = [sem(f"ff_o_loaded{i}") for i in range(E // EL)]
            o_hi_ready = sem("ff_o_hi_ready")
            o_lo_ready = sem("ff_o_lo_ready")
            masks = sem("ff_masks")
            copied = sem("ff_copied")
            qk_turned = sem("ff_qk_turned")
            qk_t_ready = sem("ff_qk_t_ready")
            scored = sem("ff_scored")
            score_step = sem("ff_score_step")
            prob_ready = sem("ff_prob_ready")
            inv_ready = sem("ff_inv_ready")
            prob_scaled = sem("ff_prob_scaled")
            prob_turned = sem("ff_prob_turned")
            prob_t_ready = sem("ff_prob_t_ready")
            head_summed = sem("ff_head_summed")
            head_hi_ready = sem("ff_head_hi_ready")
            head_lo_ready = sem("ff_head_lo_ready")
            multiplied = sem("ff_multiplied")
            summed = sem("ff_summed")
            weighed = sem("ff_weighed")
            side_summed = sem("ff_side_summed")
            finished = sem("ff_finished")
            h1_loaded = sem("ff_h1_loaded")
            out_stored = sem("ff_out_stored")
            SCORE_OPS = 5
            block = ctx.enter_context(nc.Block())

            @block.sync
            def _(sp):
                sp.sem_inc(out_stored, START)

                def load_h1(row, slot):
                    sp.dma_start(h1[:, slot].rearrange("p o j d -> p (o j) d"),
                                 h1_scratch[row].rearrange("o (j p) d -> (o p) j d", p=P)).then_inc(h1_loaded, 16)

                for e in range(0, E, EL):
                    sp.dma_start(o_raw[:, e:e + EL].rearrange("p e d -> p (e d)"),
                                 io["w_o"][:, e * D:(e + EL) * D]).then_inc(o_loaded[e // EL], 16)
                load_h1(bass.ds(1, 1), bass.ds(0, 1))
                with sp.Fori(0, BATCH) as b:
                    row, slot = bass.ds(sp.snap((b + 1) % BATCH + 1), 1), bass.ds(sp.snap((b + 1) % 2), 1)
                    sp.wait_ge(h1_loaded, 16 * (b + 1))
                    sp.sem_inc(sp_idle, 1)
                    sp.wait_ge(out_stored, 16 * b + START)
                    sp.sem_inc(sp_idle, 1)
                    load_h1(row, slot)
                    sp.wait_ge(finished, TJ * (b + 1) + FREE)
                    sp.sem_inc(sp_idle, 1)
                    sp.dma_start(out[bass.ds(b, 1)].rearrange("o (j p) d -> (o p) j d", p=P),
                                 h1[:, bass.ds(b % 2, 1)].rearrange("p o j d -> p (o j) d")).then_inc(out_stored, 16)
                sp.wait_ge(h1_loaded, 16 * (BATCH + 1))
                sp.wait_ge(out_stored, 16 * BATCH + START)

            @block.gpsimd
            def _(pool):
                G = nc.gpsimd
                G.memset(keep[:], 1.0).then_inc(masks, 1)
                G.memset(hide[:], 0.0).then_inc(masks, 1)
                pool.wait_ge(masks, 2)
                for c in (0, 2 * P):
                    for m, fill in ((keep, 0.0), (hide, NEG)):
                        G.affine_select(out=m[:, c:c + P], in_=m[:, c:c + P], compare_op=ALU.is_ge, fill=fill, base=0,
                                        pattern=[[-1, P]], channel_multiplier=1).then_inc(masks, 1)
                pool.sem_inc(finished, FREE)
                pool.sem_inc(side_summed, TJ)
                with pool.Fori(0, BATCH // 2) as pair:
                    for slot in range(2):
                        b = pair * 2 + slot
                        for a in range(TJ, len(ACT_P)):
                            pool.wait_ge(weighed, len(ACT_P) * b + a + 1)
                            if a >= 2 * TJ:
                                pool.wait_ge(side_summed, SIDE * b + a - TJ + 1)
                            G.tensor_tensor(side[:, slot, a % TJ], side[:, slot, a % TJ], scaled[:, a % TJ], ALU.add)\
                                .then_inc(side_summed, 1)
                        pool.wait_ge(side_summed, SIDE * (b + 1) + TJ)
                        pool.wait_ge(summed, len(DVE_P) * (b + 1) + BANKS)
                        for j in range(TJ):
                            G.tensor_tensor(h1[:, slot, j], h1[:, slot, j], side[:, slot, j], ALU.add).then_inc(finished, 1)

            @block.scalar
            def _(act):
                A = nc.scalar

                def copy_now(m, slot):
                    act.wait_ge(head_summed, m)
                    act.sem_inc(act_idle, 1)
                    A.activation(now[:], qkv[:, bass.ds((TJ * m) % NT, TJ)], ACT.Copy).then_inc(copied, 1)

                def place_qk_t(m, slot):
                    act.wait_ge(scored, m)
                    act.wait_ge(qk_turned, m + 1)
                    A.activation(qk_t[:].rearrange("p a t -> p (a t)"), ps_a[:, 0], ACT.Copy).then_inc(qk_t_ready, 1)

                def exponentials(m, slot):
                    act.wait_ge(score_step, SCORE_OPS * (m + 1))
                    act.wait_ge(prob_turned, m)
                    A.activation(prob[:, 0:P], score[:, 0:P], ACT.Exp, bias=top[:, 0:1],
                                 accum_out=total[:, 0:1]).then_inc(prob_ready, 1)
                    A.activation(prob[:, P:], score[:, P:], ACT.Exp, bias=top[:, 1:2],
                                 accum_out=total[:, 1:2]).then_inc(prob_ready, 1)

                def scale_prob(m, slot):
                    act.wait_ge(inv_ready, m + 1)
                    A.activation(prob[:, 0:P], prob[:, 0:P], ACT.Copy, scale=total[:, 0:1]).then_inc(prob_scaled, 1)
                    A.activation(prob[:, P:], prob[:, P:], ACT.Copy, scale=total[:, 1:2]).then_inc(prob_scaled, 1)

                def place_prob_t(m, slot):
                    act.wait_ge(head_summed, m)
                    act.wait_ge(prob_turned, m + 1)
                    A.activation(prob_t[:], ps_a[:, 2, 0:3 * P], ACT.Copy).then_inc(prob_t_ready, 1)

                def place_head(m, slot):
                    if not isinstance(m, int):
                        act.wait_ge(summed, len(DVE_P) * (m - 1) + BANKS)
                    act.wait_ge(head_summed, m + 1)
                    A.activation(head_hi[:, slot], ps_a[:, 3, 0:T], ACT.Copy).then_inc(head_hi_ready, 1)

                def weigh(b, slot, a):
                    e, j = ACT_P[a] // TJ, ACT_P[a] % TJ
                    act.wait_ge(multiplied, PRODUCTS * b + ACT_P[a] + 1)
                    if a < TJ:
                        act.wait_ge(finished, TJ * (b - 1) + FREE)
                    else:
                        act.wait_ge(side_summed, SIDE * b + a - TJ + 1)
                    act.sem_inc(act_idle, 1)
                    A.activation((side[:, slot] if a < TJ else scaled)[:, j], ps_o[:, ACT_P[a] % BANKS], ACT.Copy,
                                 scale=w[:, bass.ds(TJ * b + j, 1), e:e + 1].rearrange("p o e -> p (o e)"))\
                        .then_inc(weighed, 1)

                for step in (copy_now, place_qk_t, exponentials, scale_prob, place_prob_t, place_head):
                    step(0, 0)
                for e in range(E):
                    act.wait_ge(o_loaded[e // EL], 16)
                    A.activation(o_hi[:, e], o_raw[:, e], ACT.Copy).then_inc(o_hi_ready, 1)
                with act.Fori(0, BATCH // 2) as pair:
                    for slot in range(2):
                        b = pair * 2 + slot
                        for k, steps in enumerate(((copy_now,), (place_qk_t,), (exponentials, scale_prob),
                                                   (place_prob_t, place_head))):
                            for step in steps:
                                step(b + 1, 1 - slot)
                            for a in range(TJ * k, TJ * (k + 1)):
                                weigh(b, slot, a)

            @block.vector
            def _(dve):
                V = nc.vector
                dve.sem_inc(summed, BANKS)
                dve.wait_ge(masks, 6)

                def scale_scores(m, slot):
                    dve.wait_ge(scored, m + 1)
                    dve.wait_ge(prob_ready, TJ * m)
                    V.scalar_tensor_tensor(score[:], ps_a[:, 1, 0:3 * P], SCALE, keep[:], ALU.mult, ALU.mult)\
                        .then_inc(score_step, 1)

                def mask_scores(m, slot):
                    dve.wait_ge(score_step, SCORE_OPS * m + 1)
                    V.tensor_tensor(score[:], score[:], hide[:], ALU.add).then_inc(score_step, 1)

                def largest_scores(m, slot):
                    dve.wait_ge(score_step, SCORE_OPS * m + 2)
                    V.tensor_reduce(top[:, 0:1], score[:, 0:P], AX.X, ALU.max).then_inc(score_step, 1)
                    V.tensor_reduce(top[:, 1:2], score[:, P:], AX.X, ALU.max).then_inc(score_step, 1)

                def negate_largest(m, slot):
                    dve.wait_ge(score_step, SCORE_OPS * m + 4)
                    V.tensor_scalar(top[:], top[:], -1.0, None, ALU.mult).then_inc(score_step, 1)

                def invert(m, slot):
                    dve.wait_ge(prob_ready, TJ * (m + 1))
                    V.reciprocal(total[:], total[:]).then_inc(inv_ready, 1)

                def place_rest(m, slot):
                    dve.wait_ge(head_hi_ready, m + 1)
                    V.tensor_tensor(head_lo[:, slot], ps_a[:, 3, 0:T], head_hi[:, slot].bitcast(F32), ALU.subtract)\
                        .then_inc(head_lo_ready, 1)

                def add(b, slot, i):
                    if i in ACT_P:
                        return
                    e, j, d = i // TJ, i % TJ, DVE_P.index(i)
                    dve.wait_ge(multiplied, PRODUCTS * b + i + 1)
                    if d < TJ:
                        dve.wait_ge(h1_loaded, 16 * (b + 1))
                    else:
                        dve.wait_ge(summed, len(DVE_P) * b + d - TJ + 1 + BANKS)
                    weight = w[:, bass.ds(TJ * b + j, 1), e:e + 1].rearrange("p o e -> p (o e)")
                    V.scalar_tensor_tensor(h1[:, slot, j], ps_o[:, i % BANKS], weight, h1[:, slot, j],
                                           ALU.mult, ALU.add).then_inc(summed, 1)

                for step in (scale_scores, mask_scores, largest_scores, negate_largest, invert, place_rest):
                    step(0, 0)
                for e in range(E):
                    dve.wait_ge(o_hi_ready, e + 1)
                    V.tensor_tensor(o_lo[:, e], o_raw[:, e], o_hi[:, e].bitcast(F32), ALU.subtract)\
                        .then_inc(o_lo_ready, 1)
                with dve.Fori(0, BATCH // 2) as pair:
                    for slot in range(2):
                        b = pair * 2 + slot
                        for i in range(PRODUCTS):
                            for before, step in ((8, scale_scores), (9, mask_scores), (11, largest_scores),
                                                 (12, negate_largest), (15, invert), (27, place_rest)):
                                if before == i:
                                    step(b + 1, 1 - slot)
                            add(b, slot, i)

            @block.tensor
            def _(pe):
                M = nc.tensor.matmul

                def turn_qk(m, slot):
                    pe.wait_ge(qk_t_ready, m)
                    pe.wait_ge(copied, m + 1)
                    for a in range(2):
                        for j in range(TJ):
                            last = nc.tensor.transpose(ps_a[:, 0, a * T + j * P:a * T + (j + 1) * P],
                                                       now[:, j, a * HD:(a + 1) * HD], ident[:])
                    last.then_inc(qk_turned, 1)

                def score_tokens(m, slot):
                    pe.wait_ge(qk_t_ready, m + 1)
                    pe.wait_ge(score_step, SCORE_OPS * m)
                    M(ps_a[:, 1, 0:P], qk_t[:, 0, 0:P], qk_t[:, 1, 0:P], start=True, stop=True)
                    M(ps_a[:, 1, P:3 * P], qk_t[:, 0, P:], qk_t[:, 1], start=True, stop=True).then_inc(scored, 1)

                def turn_prob(m, slot):
                    pe.wait_ge(prob_scaled, TJ * (m + 1))
                    pe.wait_ge(prob_t_ready, m)
                    for k in range(3):
                        last = nc.tensor.transpose(ps_a[:, 2, k * P:(k + 1) * P], prob[:, k * P:(k + 1) * P], ident[:])
                    last.then_inc(prob_turned, 1)

                def sum_values(m, slot):
                    pe.wait_ge(head_lo_ready, m)
                    pe.wait_ge(prob_t_ready, m + 1)
                    for j, k, c in ((0, 0, 0), (1, 0, 1), (1, 1, 2)):
                        last = M(ps_a[:, 3, j * P:(j + 1) * P], now[:, k, 2 * HD:], prob_t[:, c * P:(c + 1) * P],
                                 start=(k == 0), stop=(k == j))
                    last.then_inc(head_summed, 1)

                def multiply(b, slot, i):
                    e, j = i // TJ, i % TJ
                    if i == 0:
                        pe.wait_ge(head_lo_ready, b + 1)
                    if j == 0:
                        pe.wait_ge(o_lo_ready, e + 1)
                    if i < BANKS:
                        pe.wait_ge(summed, len(DVE_P) * b + i + 1)
                    elif i - BANKS in ACT_P:
                        pe.wait_ge(weighed, len(ACT_P) * b + ACT_P.index(i - BANKS) + 1)
                    else:
                        pe.wait_ge(summed, len(DVE_P) * b + DVE_P.index(i - BANKS) + 1 + BANKS)
                    for a, s in ((head_hi, o_hi), (head_hi, o_lo), (head_lo, o_hi)):
                        last = M(ps_o[:, i % BANKS], a[:, slot, j * P:(j + 1) * P], s[:, e],
                                 start=(a is head_hi and s is o_hi), stop=(a is head_lo))
                    last.then_inc(multiplied, 1)

                for step in (turn_qk, score_tokens, turn_prob, sum_values):
                    step(0, 0)
                with pe.Fori(0, BATCH // 2) as pair:
                    for slot in range(2):
                        b = pair * 2 + slot
                        for i in range(PRODUCTS):
                            for before, step in ((2, turn_qk), (6, score_tokens), (18, turn_prob), (22, sum_values)):
                                if before == i:
                                    step(b + 1, 1 - slot)
                            multiply(b, slot, i)


def program(nc, io, out):
    batch, tokens, width = out.shape
    states = 16
    h0_scratch = nc.dram_tensor("h0_scratch", (batch, tokens, width), F32).ap()
    b_scratch = nc.dram_tensor("b_scratch", (states, tokens), F32).ap()
    h1_scratch = nc.dram_tensor("h1_scratch", (batch + 1, tokens, width), F32).ap()
    token_stage(nc, io, h0_scratch)
    mamba_stage(nc, io, h0_scratch, b_scratch, h1_scratch)
    expert_stage(nc, io, h1_scratch, out)


def _rows(w):
    return w.reshape(w.shape[0] // P, P, -1).transpose(1, 0, 2).reshape(P, -1)


def _layout(x, log_dt, log_w_real, w_imag, norm_w, w_in, conv_w, conv_b, w_x, w_dt, b_dt, a, d, w_out,
            sim, gates, q_proj, k_proj, v_proj, o_proj):
    import numpy as np

    ch, h, n, _ = x.shape
    experts, width, head = q_proj.shape
    pairs = h // 2

    def by_pair(w):
        return w.reshape(pairs, 2, n).transpose(1, 2, 0).reshape(2 * n, pairs)

    qkv = np.stack([q_proj, k_proj, v_proj], axis=2).reshape(experts, width // P, P, 3 * head)
    return {
        "xT": x.reshape(ch, pairs, 2, n, 2).transpose(2, 3, 4, 0, 1).reshape(2 * n, 2 * ch * pairs),
        "log_dt": log_dt.reshape(pairs, 2).T,
        "log_w_real": by_pair(log_w_real),
        "w_imag": by_pair(w_imag),
        "norm_w": _rows(norm_w),
        "w_in": _rows(w_in.T),
        "conv_w": _rows(conv_w),
        "conv_b": _rows(conv_b),
        "w_x": _rows(w_x.T),
        "w_dt": w_dt.T,
        "b_dt": _rows(b_dt),
        "a": _rows(a),
        "d": _rows(d),
        "w_out": _rows(w_out.T),
        "sim": _rows(sim),
        "gates": gates.reshape(1, experts),
        "w_qkv": qkv.transpose(2, 0, 1, 3).reshape(P, -1),
        "w_o": o_proj.transpose(1, 0, 2).reshape(head, -1),
    }


def kernel(x, L0_tok_log_dt, L0_tok_log_w_real, L0_tok_w_imag, L0_attn_norm_w, L0_attn_W_in, L0_attn_conv_w,
           L0_attn_conv_b, L0_attn_W_x, L0_attn_W_dt, L0_attn_b_dt, L0_attn_A, L0_attn_D, L0_attn_W_out,
           L0_ffn_sim_matrix, L0_ffn_gates, L0_ffn_q_proj, L0_ffn_k_proj, L0_ffn_v_proj, L0_ffn_o_proj):
    import numpy as np
    import concourse.bacc as bacc
    from concourse.bass_utils import run_bass_kernel_spmd

    given = (x, L0_tok_log_dt, L0_tok_log_w_real, L0_tok_w_imag, L0_attn_norm_w, L0_attn_W_in, L0_attn_conv_w,
             L0_attn_conv_b, L0_attn_W_x, L0_attn_W_dt, L0_attn_b_dt, L0_attn_A, L0_attn_D, L0_attn_W_out,
             L0_ffn_sim_matrix, L0_ffn_gates, L0_ffn_q_proj, L0_ffn_k_proj, L0_ffn_v_proj, L0_ffn_o_proj)
    laid = _layout(*(np.asarray(v) for v in given))
    nc = bacc.Bacc("TRN2", target_bir_lowering=False, num_devices=1)
    arrays, io = {}, {}
    for name, v in laid.items():
        v = np.ascontiguousarray(v)
        arrays[f"in_{name}"] = v
        io[name] = nc.dram_tensor(f"in_{name}", v.shape, mybir.dt.from_np(v.dtype), kind="ExternalInput").ap()
    ch, h = x.shape[0], x.shape[1]
    width = L0_ffn_q_proj.shape[1]
    out = nc.dram_tensor("out_0", (ch, h, width), F32, kind="ExternalOutput").ap()
    program(nc, io, out)
    result = run_bass_kernel_spmd(nc, [arrays], core_ids=[0])
    return result.results[0]["out_0"]
```
